# Optimizing a Trainium2 kernel written in Bass

```python
import numpy as np
import jax
import jax.numpy as jnp

def _softmax(x, axis=-1):
    return jax.nn.softmax(x, axis=axis)

def _gelu(x):
    return jax.nn.gelu(x, approximate=True)

def _silu(x):
    return jax.nn.silu(x)

def _sigmoid(x):
    return jax.nn.sigmoid(x)

def _layernorm(x, axis=-1, eps=1e-05):
    m = jnp.mean(x, axis=axis, keepdims=True)
    v = jnp.var(x, axis=axis, keepdims=True)
    return (x - m) / jnp.sqrt(v + eps)

def _scatter_add(tgt, idx, src, axis=0):
    return tgt.at[idx].add(src)

def _segment_sum(src, seg, n):
    return jax.ops.segment_sum(src, seg, n)
kernel_name = 'mk_conv_attn_hybrid_d2_conv_nchw256_r4_ddac19'

def setup_inputs(seed: int=0):
    np.random.seed(seed)
    _w = jnp.asarray

    def _rec_inputs():
        import jax
        import jax.numpy as jnp
        _gk = jax.random.key(seed)
        x = -0.0005153 + 1.001 * jax.random.normal(jax.random.fold_in(_gk, 1), (4, 64, 56, 56), jnp.float32)
        return x
    x = _rec_inputs()

    def _L0_conv_setup():
        import jax, jax.numpy as jnp
        import numpy as np
        K = 7
        PAD = 3
        EPS = 1e-05
        B, CIN, H, W = (4, 64, 56, 56)
        CR = 32
        COUT = 64
        SP = 8
        HN = COUT // SP
        OFFS = [(dy, dx) for dy in range(K) for dx in range(K)]

        def _conv1x1(x, w, b):
            return jnp.einsum('bchw,oc->bohw', x, w) + b[None, :, None, None]

        def _bn(y, g, b, m, v):
            inv = g / jnp.sqrt(v + EPS)
            return y * inv[None, :, None, None] + (b - m * inv)[None, :, None, None]
        key = jax.random.key(seed)
        ks = jax.random.split(key, 24)

        def n(i, shape, s=0.05):
            return jax.random.normal(ks[i], shape, dtype=jnp.float32) * s

        def pos(i, shape):
            return jax.random.uniform(ks[i], shape, dtype=jnp.float32, minval=0.5, maxval=1.5)
        return {'x': jax.random.normal(ks[0], (B, CIN, H, W), dtype=jnp.float32), 'w1c': n(1, (CR, CIN)), 'b1c': n(2, (CR,)), 'w2c': n(3, (CR, CIN)), 'b2c': n(4, (CR,)), 'w3c': n(5, (COUT, CIN)), 'b3c': n(6, (COUT,)), 'bn1_g': pos(7, (CR,)), 'bn1_b': n(8, (CR,)), 'bn1_m': n(9, (CR,)), 'bn1_v': pos(10, (CR,)), 'cw1': n(11, (CR, CR)), 'bn2_g': pos(12, (CR,)), 'bn2_b': n(13, (CR,)), 'bn2_m': n(14, (CR,)), 'bn2_v': pos(15, (CR,)), 'cw2': n(16, (HN, CR)), 'cw2_b': n(17, (HN,))}
    _L0_conv_all = _L0_conv_setup()
    _L0_conv_in = {k: v for k, v in _L0_conv_all.items() if k in ('w1c', 'b1c', 'w2c', 'b2c', 'w3c', 'b3c', 'bn1_g', 'bn1_b', 'bn1_m', 'bn1_v', 'cw1', 'bn2_g', 'bn2_b', 'bn2_m', 'bn2_v', 'cw2', 'cw2_b')}
    del _L0_conv_all

    def _L1_attn_setup():
        import jax, jax.numpy as jnp
        import numpy as np
        F_DIM = 64
        key = jax.random.key(seed)
        ks = jax.random.split(key, 8)
        B, S, F = (8, 512, F_DIM)
        scale = 1.0 / np.sqrt(F)
        return {'x': jax.random.normal(ks[0], (B, S, F), dtype=jnp.float32), 'att_w': jax.random.normal(ks[1], (3 * F,), dtype=jnp.float32) * scale, 'z_w': jax.random.normal(ks[2], (F, 2 * F), dtype=jnp.float32) * scale, 'z_b': jax.random.normal(ks[3], (F,), dtype=jnp.float32) * 0.01, 'r_w': jax.random.normal(ks[4], (F, 2 * F), dtype=jnp.float32) * scale, 'r_b': jax.random.normal(ks[5], (F,), dtype=jnp.float32) * 0.01, 'f_w': jax.random.normal(ks[6], (F, 2 * F), dtype=jnp.float32) * scale, 'f_b': jax.random.normal(ks[7], (F,), dtype=jnp.float32) * 0.01}
    _L1_attn_all = _L1_attn_setup()
    _L1_attn_in = {k: v for k, v in _L1_attn_all.items() if k in ('att_w', 'z_w', 'z_b', 'r_w', 'r_b', 'f_w', 'f_b')}
    del _L1_attn_all

    def _L1_ffn_setup():
        import jax, jax.numpy as jnp
        import numpy as np
        TOP_K = 2
        key = jax.random.key(seed)
        ks = jax.random.split(key, 4)
        B, L, D, H, E = (8, 1024, 64, 256, 8)
        s = 0.02
        return {'x': jax.random.normal(ks[0], (B, L, D), jnp.float32), 'Wg': jax.random.normal(ks[1], (D, E), jnp.float32) * s, 'bg': jnp.zeros((E,), jnp.float32), 'W1': jax.random.normal(ks[2], (E, D, H), jnp.float32) * s, 'b1': jnp.zeros((E, H), jnp.float32), 'W2': jax.random.normal(ks[3], (E, H, D), jnp.float32) * s, 'b2': jnp.zeros((E, D), jnp.float32)}
    _L1_ffn_all = _L1_ffn_setup()
    _L1_ffn_in = {k: v for k, v in _L1_ffn_all.items() if k in ('Wg', 'bg', 'W1', 'b1', 'W2', 'b2')}
    del _L1_ffn_all
    return {'x': x, 'L0_conv_w1c': _L0_conv_in['w1c'], 'L0_conv_b1c': _L0_conv_in['b1c'], 'L0_conv_w2c': _L0_conv_in['w2c'], 'L0_conv_b2c': _L0_conv_in['b2c'], 'L0_conv_w3c': _L0_conv_in['w3c'], 'L0_conv_b3c': _L0_conv_in['b3c'], 'L0_conv_bn1_g': _L0_conv_in['bn1_g'], 'L0_conv_bn1_b': _L0_conv_in['bn1_b'], 'L0_conv_bn1_m': _L0_conv_in['bn1_m'], 'L0_conv_bn1_v': _L0_conv_in['bn1_v'], 'L0_conv_cw1': _L0_conv_in['cw1'], 'L0_conv_bn2_g': _L0_conv_in['bn2_g'], 'L0_conv_bn2_b': _L0_conv_in['bn2_b'], 'L0_conv_bn2_m': _L0_conv_in['bn2_m'], 'L0_conv_bn2_v': _L0_conv_in['bn2_v'], 'L0_conv_cw2': _L0_conv_in['cw2'], 'L0_conv_cw2_b': _L0_conv_in['cw2_b'], 'L1_attn_att_w': _L1_attn_in['att_w'], 'L1_attn_z_w': _L1_attn_in['z_w'], 'L1_attn_z_b': _L1_attn_in['z_b'], 'L1_attn_r_w': _L1_attn_in['r_w'], 'L1_attn_r_b': _L1_attn_in['r_b'], 'L1_attn_f_w': _L1_attn_in['f_w'], 'L1_attn_f_b': _L1_attn_in['f_b'], 'L1_ffn_Wg': _L1_ffn_in['Wg'], 'L1_ffn_bg': _L1_ffn_in['bg'], 'L1_ffn_W1': _L1_ffn_in['W1'], 'L1_ffn_b1': _L1_ffn_in['b1'], 'L1_ffn_W2': _L1_ffn_in['W2'], 'L1_ffn_b2': _L1_ffn_in['b2']}

def reference(x, L0_conv_w1c, L0_conv_b1c, L0_conv_w2c, L0_conv_b2c, L0_conv_w3c, L0_conv_b3c, L0_conv_bn1_g, L0_conv_bn1_b, L0_conv_bn1_m, L0_conv_bn1_v, L0_conv_cw1, L0_conv_bn2_g, L0_conv_bn2_b, L0_conv_bn2_m, L0_conv_bn2_v, L0_conv_cw2, L0_conv_cw2_b, L1_attn_att_w, L1_attn_z_w, L1_attn_z_b, L1_attn_r_w, L1_attn_r_b, L1_attn_f_w, L1_attn_f_b, L1_ffn_Wg, L1_ffn_bg, L1_ffn_W1, L1_ffn_b1, L1_ffn_W2, L1_ffn_b2):
    import jax
    import jax.numpy as jnp

    def _L0_conv_ref(x, w1c, b1c, w2c, b2c, w3c, b3c, bn1_g, bn1_b, bn1_m, bn1_v, cw1, bn2_g, bn2_b, bn2_m, bn2_v, cw2, cw2_b):
        import jax, jax.numpy as jnp
        import numpy as np
        K = 7
        PAD = 3
        EPS = 1e-05
        B, CIN, H, W = (4, 64, 56, 56)
        CR = 32
        COUT = 64
        SP = 8
        HN = COUT // SP
        OFFS = [(dy, dx) for dy in range(K) for dx in range(K)]

        def _conv1x1(x, w, b):
            return jnp.einsum('bchw,oc->bohw', x, w) + b[None, :, None, None]

        def _bn(y, g, b, m, v):
            inv = g / jnp.sqrt(v + EPS)
            return y * inv[None, :, None, None] + (b - m * inv)[None, :, None, None]
        x1 = _conv1x1(x, w1c, b1c)
        x2 = _conv1x1(x, w2c, b2c)
        x3 = _conv1x1(x, w3c, b3c)
        x2p = jnp.pad(x2, ((0, 0), (0, 0), (PAD, PAD), (PAD, PAD)), mode='reflect')
        diff = jnp.stack([x1 - x2p[:, :, dy:dy + H, dx:dx + W] for dy, dx in OFFS], axis=2)
        diff = diff.reshape(B, CR, K * K, H * W)
        y = jax.nn.relu(_bn(diff, bn1_g, bn1_b, bn1_m, bn1_v))
        y = jnp.einsum('bkln,ok->boln', y, cw1)
        y = jax.nn.relu(_bn(y, bn2_g, bn2_b, bn2_m, bn2_v))
        logits = jnp.einsum('bkln,ok->boln', y, cw2) + cw2_b[None, :, None, None]
        wgt = jax.nn.softmax(logits, axis=2)
        wgt = wgt.reshape(B, HN, K * K, H, W)
        x3p = jnp.pad(x3, ((0, 0), (0, 0), (PAD, PAD), (PAD, PAD)), mode='reflect')
        out = jnp.zeros((B, HN, SP, H, W), dtype=x.dtype)
        for k, (dy, dx) in enumerate(OFFS):
            patch = x3p[:, :, dy:dy + H, dx:dx + W].reshape(B, HN, SP, H, W)
            out = out + patch * wgt[:, :, k][:, :, None]
        return out.reshape(B, COUT, H, W)

    def _L1_attn_ref(x, att_w, z_w, z_b, r_w, r_b, f_w, f_b):
        import jax, jax.numpy as jnp
        import numpy as np
        F_DIM = 64
        F = x.shape[-1]
        wa, wb, wc = (att_w[:F], att_w[F:2 * F], att_w[2 * F:])
        a = jnp.einsum('bif,f->bi', x, wa)
        b = jnp.einsum('bjf,f->bj', x, wb)
        c = jnp.einsum('bif,bjf->bij', x * wc, x)
        scores = a[:, :, None] + b[:, None, :] + c
        attn_weight = jax.nn.softmax(scores, axis=2)
        attn = jnp.einsum('bij,bjf->bif', attn_weight, x)
        cat = jnp.concatenate([x, attn], axis=-1)
        z = jnp.tanh(jnp.einsum('bsg,fg->bsf', cat, z_w) + z_b)
        r = jax.nn.sigmoid(jnp.einsum('bsg,fg->bsf', cat, r_w) + r_b)
        f = jax.nn.sigmoid(jnp.einsum('bsg,fg->bsf', cat, f_w) + f_b)
        return r * x + f * z

    def _L1_ffn_ref(x, Wg, bg, W1, b1, W2, b2):
        import jax, jax.numpy as jnp
        import numpy as np
        TOP_K = 2
        B, L, D = x.shape
        E = W1.shape[0]
        xf = x.reshape(-1, D)
        gate_logits = xf @ Wg + bg
        top_w, top_i = jax.lax.top_k(gate_logits, TOP_K)
        top_w = jax.nn.softmax(top_w, axis=-1)
        w_dense = jnp.sum(jax.nn.one_hot(top_i, E, dtype=xf.dtype) * top_w[..., None], axis=1)
        out = jnp.zeros_like(xf)
        for e in range(E):
            h = jax.nn.gelu(xf @ W1[e] + b1[e], approximate=False)
            out = out + w_dense[:, e:e + 1] * (h @ W2[e] + b2[e])
        return out.reshape(B, L, D)

    def _gn(v, G=32, eps=1e-05):
        B_, C_, H_, W_ = v.shape
        g = v.reshape(B_, G, C_ // G, H_, W_)
        m = jnp.mean(g, axis=(2, 3, 4), keepdims=True)
        s = jnp.var(g, axis=(2, 3, 4), keepdims=True)
        return ((g - m) / jnp.sqrt(s + eps)).reshape(v.shape)

    def _ln_c(v, eps=1e-06):
        m = jnp.mean(v, axis=1, keepdims=True)
        s = jnp.var(v, axis=1, keepdims=True)
        return (v - m) / jnp.sqrt(s + eps)

    def _ln_t(v, eps=1e-05):
        m = jnp.mean(v, axis=-1, keepdims=True)
        s = jnp.var(v, axis=-1, keepdims=True)
        return (v - m) / jnp.sqrt(s + eps)

    def _to_tokens(v):
        B_, C_, H_, W_ = v.shape
        return v.reshape(B_, C_, H_ * W_).transpose(0, 2, 1)

    def _from_tokens(t, like):
        B_, C_, H_, W_ = like.shape
        return t.transpose(0, 2, 1).reshape(B_, C_, H_, W_)
    x = x + _L0_conv_ref(_gn(x), L0_conv_w1c, L0_conv_b1c, L0_conv_w2c, L0_conv_b2c, L0_conv_w3c, L0_conv_b3c, L0_conv_bn1_g, L0_conv_bn1_b, L0_conv_bn1_m, L0_conv_bn1_v, L0_conv_cw1, L0_conv_bn2_g, L0_conv_bn2_b, L0_conv_bn2_m, L0_conv_bn2_v, L0_conv_cw2, L0_conv_cw2_b)
    t = _to_tokens(x)
    t = t + _L1_attn_ref(_ln_t(t), L1_attn_att_w, L1_attn_z_w, L1_attn_z_b, L1_attn_r_w, L1_attn_r_b, L1_attn_f_w, L1_attn_f_b)
    t = t + _L1_ffn_ref(_ln_t(t), L1_ffn_Wg, L1_ffn_bg, L1_ffn_W1, L1_ffn_b1, L1_ffn_W2, L1_ffn_b2)
    x = _from_tokens(t, x)
    return x

_drawn_inputs = setup_inputs


def setup_inputs(seed=0):
    import zlib

    import numpy as np

    out = dict(_drawn_inputs(seed))
    spreads = {'L1_ffn_bg': (0.0, 0.1), 'L1_ffn_b1': (0.0, 0.8), 'L1_ffn_b2': (0.0, 0.1)}
    factors = {'L0_conv_w1c': 8.0,
     'L0_conv_b1c': 8.0,
     'L0_conv_w2c': 8.0,
     'L0_conv_b2c': 8.0,
     'L0_conv_bn1_g': 8.0,
     'L0_conv_bn1_b': 8.0,
     'L0_conv_bn1_m': 8.0,
     'L0_conv_bn1_v': 8.0,
     'L0_conv_cw1': 8.0,
     'L0_conv_bn2_g': 8.0,
     'L0_conv_bn2_b': 8.0,
     'L0_conv_bn2_m': 8.0,
     'L0_conv_bn2_v': 8.0,
     'L0_conv_cw2': 8.0,
     'L0_conv_cw2_b': 8.0,
     'L1_attn_z_b': 8.0,
     'L1_attn_r_b': 8.0,
     'L1_attn_f_b': 8.0,
     'L1_ffn_W1': 4.735,
     'L1_ffn_W2': 3.974}
    for name, (base, spread) in spreads.items():
        noise = np.random.default_rng([zlib.crc32(name.encode()), seed]).standard_normal(out[name].shape)
        drawn = base * np.exp(spread * noise) if base else spread * noise
        out[name] = jnp.asarray(drawn.astype(out[name].dtype))
    for name, factor in factors.items():
        out[name] = (out[name] * factor).astype(out[name].dtype)
    return out
```

```python
from contextlib import ExitStack

import numpy as np

import concourse.bass as bass
from concourse import mybir

F32 = mybir.dt.float32
F16 = mybir.dt.float16
ALU = mybir.AluOpType
ACT = mybir.ActivationFunctionType
AX = mybir.AxisListType

B, C, H, W = 4, 64, 56, 56
PIX = H * W
PAIRS = B // 2
K, PAD = 7, 3
HP, WP = H + 2 * PAD, W + 2 * PAD
CR = 32
NH, SP = 8, 8
NQ = 4
ROWS = 8
CH = ROWS * W
NCH = H // ROWS
STEPS = 2 * K
WROWS = ROWS + K - 1
WIN = WROWS * WP
PADDED = HP * WP
STAGE = PADDED + 4
BANK = 512
EPS = 1e-5


def taps(j):
    return j // 2, NQ * (j % 2), NQ if j % 2 == 0 else K - NQ


def columns(parts):
    at, out = 0, {}
    for name, n in parts:
        out[name] = (at, at + n)
        at += n
    return out, at


CONV_COLS, CONV_N = columns([
    ("w1", PAIRS * 128), ("w2", PAIRS * 128), ("w3", 2 * PAIRS * 128), ("cw1", 128), ("cw2", 32),
    ("pair_mean", 128), ("tap_sum", 32), ("tap_sum_all", 128), ("ident", 128),
    ("vec", 16)])
VEC = {n: i for i, n in enumerate(
    ["b1", "b2", "b3a", "b3b", "g1", "t1", "m1", "v1", "g2", "t2", "m2", "v2", "cw2b", "mhalf"])}


def conv_prepare(nc, x, consts, cst, x1, x2p, x3st):
    with ExitStack() as ctx:
        def sb(name, shape, dt=F32):
            return ctx.enter_context(nc.sbuf_tensor(name, shape, dt))

        def sem(name):
            return ctx.enter_context(nc.semaphore(name))

        xin = sb("cp_xin", [128, PAIRS, PIX])
        xn = sb("cp_xn", [128, PAIRS, PIX])
        stats = sb("cp_stats", [128, PAIRS, NCH, 6])
        mv = sb("cp_mv", [128, PAIRS, 2])
        mom = sb("cp_mom", [128, PAIRS, 2])
        gm = sb("cp_gm", [128, PAIRS, 2])
        var = sb("cp_var", [128, PAIRS])
        rstd = sb("cp_rstd", [128, PAIRS])
        bnv = sb("cp_bnv", [128, 2])
        half = sb("cp_half", [128, 2])
        cwt = sb("cp_cwt", [128, 128])
        tmp = sb("cp_tmp", [128, 4])
        psx = ctx.enter_context(nc.psum_tensor("cp_psx", [128, 2, 4, BANK], F32))

        x_in = [sem(f"cp_x_in{t}") for t in range(PAIRS)]
        c_in = sem("cp_c_in")
        dve = sem("cp_dve")
        moments = sem("cp_moments")
        grouped = sem("cp_grouped")
        var_ready = sem("cp_var_ready")
        rstd_ready = sem("cp_rstd_ready")
        xn_ready = sem("cp_xn_ready")
        bn_ready = sem("cp_bn_ready")
        cw_scaled = sem("cp_cw_scaled")
        cw_turned = sem("cp_cw_turned")
        cw_copied = sem("cp_cw_copied")
        conv_done = sem("cp_conv_done")
        evac_done = sem("cp_evac_done")

        def vec(name):
            a = CONV_COLS["vec"][0] + VEC[name]
            return cst[:, a:a + 1]

        def mat(name, i=0, n=128):
            a = CONV_COLS[name][0] + i * n
            return cst[:, a:a + n]

        with nc.Block() as block:
            @block.sync
            def _(sp):
                sp.dma_start(xin[:, 0, :], x[0:2].rearrange("b c h w -> (b c) (h w)")).then_inc(x_in[0], 16)
                sp.dma_start(cst[:, :], consts).then_inc(c_in, 16)

            @block.gpsimd
            def _(pool):
                pool.wait_ge(var_ready, 1)
                pool.tensor_tensor(rstd[:, :], var[:, :], half[:, :], ALU.pow).then_inc(rstd_ready, 1)
                pool.tensor_tensor(bnv[:, :], bnv[:, :], half[:, :], ALU.pow).then_inc(rstd_ready, 1)

            @block.vector
            def _(v):
                n = [0]

                def link(ins):
                    n[0] += 1
                    ins.then_inc(dve, 1)
                    v.wait_ge(dve, n[0])

                v.wait_ge(c_in, 16)
                v.tensor_copy(half[:, 0:1], vec("mhalf"))
                v.tensor_copy(half[:, 1:2], vec("mhalf"))
                v.tensor_scalar(bnv[:, 0:1], vec("v1"), EPS, None, ALU.add)
                v.tensor_scalar(bnv[:, 1:2], vec("v2"), EPS, None, ALU.add)
                for t in range(PAIRS):
                    v.wait_ge(x_in[t], 16)
                    for k in range(NCH):
                        ins = v.bn_stats(stats[:, t, k, :], xin[:, t, k * CH:(k + 1) * CH])
                    link(ins)
                    link(v.bn_aggr(mv[:, t, :], stats[:, t, :, :].rearrange("p k s -> p (k s)")))
                link(v.tensor_tensor(mom[:, :, 0], mv[:, :, 0], mv[:, :, 0], ALU.mult))
                link(v.tensor_tensor(mom[:, :, 1], mom[:, :, 0], mv[:, :, 1], ALU.add))
                v.tensor_copy(mom[:, :, 0], mv[:, :, 0]).then_inc(moments, 1)
                v.wait_ge(grouped, 1)
                link(v.tensor_copy(gm[:, :, :], psx[:, 0, 0, 0:4].rearrange("p (t m) -> p t m", m=2)))
                link(v.tensor_tensor(var[:, :], gm[:, :, 0], gm[:, :, 0], ALU.mult))
                link(v.tensor_tensor(var[:, :], gm[:, :, 1], var[:, :], ALU.subtract))
                v.tensor_scalar(var[:, :], var[:, :], EPS, None, ALU.add).then_inc(var_ready, 1)
                v.wait_ge(rstd_ready, 1)
                for t in range(PAIRS):
                    v.tensor_scalar(xn[:, t, :], xin[:, t, :], gm[:, t, 0:1], rstd[:, t:t + 1],
                                    ALU.subtract, ALU.mult).then_inc(xn_ready, 1)
                v.wait_ge(rstd_ready, 2)
                link(v.tensor_tensor(tmp[:, 0:1], vec("g1"), bnv[:, 0:1], ALU.mult))
                link(v.tensor_tensor(tmp[:, 1:2], vec("g2"), bnv[:, 1:2], ALU.mult))
                link(v.tensor_tensor(tmp[:, 2:3], vec("b1"), vec("m1"), ALU.subtract))
                link(v.scalar_tensor_tensor(out=tmp[:, 2:3], in0=tmp[:, 2:3], scalar=tmp[:, 0:1],
                                            in1=vec("t1"), op0=ALU.mult, op1=ALU.add))
                link(v.tensor_tensor(tmp[:, 3:4], vec("b2"), tmp[:, 0:1], ALU.mult))
                link(v.tensor_tensor(vec("m2"), vec("m2"), tmp[:, 1:2], ALU.mult))
                link(v.tensor_tensor(vec("t2"), vec("t2"), vec("m2"), ALU.subtract))
                v.tensor_scalar(cwt[:, :], mat("cw1"), tmp[:, 1:2], None, ALU.mult).then_inc(bn_ready, 1)
                v.wait_ge(cw_turned, 1)
                v.tensor_copy(mat("cw1"), psx[:, 1, 0, 0:128]).then_inc(cw_copied, 1)
                v.wait_ge(evac_done, 4 * NCH)
                x3v = x3st[:, :, 0:PADDED].rearrange("p s (r c) -> p s r c", c=WP)
                x2v = x2p[:, :].rearrange("p (r c) -> p r c", c=WP)
                v.memset(x3st[:, :, PADDED:STAGE], 0.0)
                for d in range(PAD):
                    for a, b in ((d, 2 * PAD - d), (WP - 1 - d, WP - 1 - 2 * PAD + d)):
                        v.tensor_copy(x3v[:, :, PAD:PAD + H, a], x3v[:, :, PAD:PAD + H, b])
                        ins = v.tensor_copy(x2v[:, PAD:PAD + H, a], x2v[:, PAD:PAD + H, b])
                link(ins)
                for d in range(PAD):
                    for a, b in ((d, 2 * PAD - d), (HP - 1 - d, HP - 1 - 2 * PAD + d)):
                        v.tensor_copy(x3v[:, :, a, :], x3v[:, :, b, :])
                        v.tensor_copy(x2v[:, a, :], x2v[:, b, :])

            @block.scalar
            def _(act):
                act.dma_start(xin[:, 1, :], x[2:4].rearrange("b c h w -> (b c) (h w)")).then_inc(x_in[1], 16)
                act.wait_ge(bn_ready, 1)
                x2v = x2p[:, :].rearrange("p (r c) -> p r c", c=WP)
                for k in range(NCH):
                    act.wait_ge(conv_done, k + 1)
                    ps = psx[:, k % 2, :, 0:CH]
                    rows = slice(PAD + k * ROWS, PAD + (k + 1) * ROWS)
                    act.activation(x1[:, k * CH:(k + 1) * CH], ps[:, 0, :], ACT.Identity,
                                   bias=tmp[:, 2:3], scale=tmp[:, 0:1]).then_inc(evac_done, 1)
                    act.activation(x2v[:, rows, PAD:PAD + W], ps[:, 1, :].rearrange("p (r c) -> p r c", c=W),
                                   ACT.Identity, bias=tmp[:, 3:4], scale=tmp[:, 0:1]).then_inc(evac_done, 1)
                    for s in range(2):
                        x3v = x3st[:, s, 0:PADDED].rearrange("p (r c) -> p r c", c=WP)
                        act.activation(x3v[:, rows, PAD:PAD + W],
                                       ps[:, 2 + s, :].rearrange("p (r c) -> p r c", c=W), ACT.Identity,
                                       bias=vec("b3b" if s else "b3a")).then_inc(evac_done, 1)

            @block.tensor
            def _(pe):
                pe.wait_ge(c_in, 16)
                pe.wait_ge(moments, 1)
                pe.matmul(psx[:, 0, 0, 0:4], mat("pair_mean"), mom[:, :, :].rearrange("p t m -> p (t m)"),
                          start=True, stop=True).then_inc(grouped, 1)
                pe.wait_ge(bn_ready, 1)
                pe.transpose(psx[:, 1, 0, 0:128], cwt[:, :], mat("ident")).then_inc(cw_turned, 1)
                for k in range(NCH):
                    pe.wait_ge(xn_ready, 2)
                    if k == 1:
                        pe.wait_ge(cw_copied, 1)
                    if k >= 2:
                        pe.wait_ge(evac_done, 4 * (k - 1))
                    for o, name, i in ((0, "w1", 0), (1, "w2", 0), (2, "w3", 0), (3, "w3", PAIRS)):
                        for t in range(PAIRS):
                            ins = pe.matmul(psx[:, k % 2, o, 0:CH], mat(name, i + t),
                                            xn[:, t, k * CH:(k + 1) * CH], start=(t == 0), stop=(t == PAIRS - 1))
                    ins.then_inc(conv_done, 1)


def conv_main(nc, cst, x1, x2p, x3st, conv_out):
    with ExitStack() as ctx:
        def sb(name, shape, dt=F32):
            return ctx.enter_context(nc.sbuf_tensor(name, shape, dt))

        def psum(name, shape):
            return ctx.enter_context(nc.psum_tensor(name, shape, F32))

        def sem(name):
            return ctx.enter_context(nc.semaphore(name))

        diff = sb("cm_diff", [128, 2, NQ, CH])
        hid = sb("cm_hid", [128, 2, 2, 2, CH])
        lg = sb("cm_lg", [128, 2, STEPS, CH])
        win = sb("cm_win", [128, SP, WIN])
        prod = sb("cm_prod", [128, 2, NQ, CH])
        top = sb("cm_top", [128, CH])
        topb = sb("cm_topb", [128, CH])
        tq = sb("cm_tq", [32, 3, CH])
        dsum = sb("cm_dsum", [128, CH])
        rden = sb("cm_rden", [128, CH])
        cout = sb("cm_cout", [128, 2, CH])
        ps_hid = psum("cm_ps_hid", [128, 2, 2, BANK])
        ps_lg = psum("cm_ps_lg", [128, BANK])
        ps_acc = psum("cm_ps_acc", [128, 2, BANK])
        ps_den = psum("cm_ps_den", [128, BANK])

        sub_done = sem("cm_sub_done")
        relu_done = sem("cm_relu_done")
        hid_done = sem("cm_hid_done")
        hrelu_done = sem("cm_hrelu_done")
        logit_done = sem("cm_logit_done")
        logit_out = sem("cm_logit_out")
        top_done = sem("cm_top_done")
        shift_done = sem("cm_shift_done")
        exp_done = sem("cm_exp_done")
        win_in = sem("cm_win_in")
        prod_done = sem("cm_prod_done")
        acc_done = sem("cm_acc_done")
        den_out = sem("cm_den_out")
        den_done = sem("cm_den_done")
        rden_done = sem("cm_rden_done")
        out_done = sem("cm_out_done")
        out_sent = sem("cm_out_sent")
        TOPS = 13
        LAG = 3
        SLOTS = STEPS + LAG

        def mat(name, n=128):
            a = CONV_COLS[name][0]
            return cst[:, a:a + n]

        def vec(name):
            a = CONV_COLS["vec"][0] + VEC[name]
            return cst[:, a:a + 1]

        def schedule(eng, body):
            body(0, 0, True, False, False)
            body(1, 1, True, True, False)
            body(2, 0, True, True, True)
            with eng.Fori(0, (NCH - 3) // 2) as it:
                body(it * 2 + 3, 1, True, True, True)
                body(it * 2 + 4, 0, True, True, True)
            body(NCH, NCH % 2, False, True, True)
            body(NCH + 1, (NCH + 1) % 2, False, False, True)

        with nc.Block() as block:
            @block.sync
            def _(sp):
                def body(i, par, first, second, last):
                    if second:
                        if not isinstance(i, int) or i >= 2:
                            sp.wait_ge(prod_done, (i - 1) * (2 * STEPS))
                        for q in range(NQ):
                            for r in range(4):
                                src = bass.AP(tensor=x3st, offset=r * 32 * 2 * STAGE + q + (i - 1) * (ROWS * WP),
                                              ap=[[2 * STAGE, 32], [STAGE, 2], [1, WIN]])
                                dst = bass.AP(tensor=win, offset=q * 32 * SP * WIN + r * WIN,
                                              ap=[[SP * WIN, 32], [4 * WIN, 2], [1, WIN]])
                                sp.dma_start(dst, src).then_inc(win_in, 16)
                    if last:
                        sp.wait_ge(out_done, i - 1)
                        for r in range(4):
                            dst = bass.AP(tensor=conv_out.tensor, offset=r * PIX + (i - 2) * CH,
                                          ap=[[C * PIX, B], [SP * PIX, NH], [4 * PIX, 2], [1, CH]])
                            sp.dma_start(dst, cout[32 * r:32 * r + 32, :, :]).then_inc(out_sent, 16)
                schedule(sp, body)
                sp.wait_ge(out_sent, 64 * NCH)

            @block.vector
            def _(v):
                def body(i, par, first, second, last):
                    def sub(j):
                        dy, x0, n = taps(j)
                        if not (isinstance(i, int) and i == 0 and j < 2):
                            v.wait_ge(hid_done, i * (2 * STEPS) + 2 * (j - 1))
                        a = bass.AP(tensor=x1, offset=i * CH, ap=[[PIX, 128], [0, n], [1, CH]])
                        b = bass.AP(tensor=x2p, offset=i * (ROWS * WP) + dy * WP + x0,
                                    ap=[[PADDED, 128], [1, n], [WP, ROWS], [1, W]])
                        v.tensor_tensor(diff[:, j % 2, 0:n, :].rearrange("p n (r c) -> p n r c", c=W),
                                        a.rearrange("p n (r c) -> p n r c", c=W), b,
                                        ALU.subtract).then_inc(sub_done, 1)

                    p = i - 1
                    lgp = lg[:, 1 - par, :, :]

                    def maxima(part):
                        def link(k, ins):
                            ins.then_inc(top_done, 1)
                            v.wait_ge(top_done, p * TOPS + k)
                        if part == 0:
                            v.wait_ge(logit_out, i * STEPS)
                            l4 = lgp.rearrange("p (y h) n -> p h n y", h=2)
                            v.tensor_reduce(topb[0:96, :], l4[0:96, 1], AX.X, ALU.max).then_inc(top_done, 1)
                            link(2, v.tensor_reduce(top[:, :], l4[:, 0], AX.X, ALU.max))
                            link(3, v.tensor_tensor(top[0:96, :], top[0:96, :], topb[0:96, :], ALU.max))
                            for q in range(1, NQ):
                                ins = v.tensor_copy(tq[:, q - 1, :], top[32 * q:32 * q + 32, :])
                                if q < NQ - 1:
                                    ins.then_inc(top_done, 1)
                            link(6, ins)
                            v.tensor_tensor(top[0:32, :], top[0:32, :], tq[:, 0, :], ALU.max).then_inc(top_done, 1)
                            link(8, v.tensor_tensor(tq[:, 1, :], tq[:, 1, :], tq[:, 2, :], ALU.max))
                            link(9, v.tensor_tensor(tq[:, 0, :], top[0:32, :], tq[:, 1, :], ALU.max))
                            if not (isinstance(i, int) and i == 1):
                                v.wait_ge(shift_done, p * STEPS)
                            for q in range(NQ):
                                v.tensor_copy(topb[32 * q:32 * q + 32, :], tq[:, 0, :]).then_inc(top_done, 1)

                    def product(k):
                        dy, x0, n = taps(k)
                        if k == 0:
                            v.wait_ge(win_in, i * 256)
                        v.wait_ge(exp_done, p * STEPS + k + 1)
                        for hs in range(2):
                            if not (isinstance(i, int) and i == 1 and k == 0):
                                v.wait_ge(acc_done, p * (2 * STEPS) + 2 * k + hs - 1)
                            wv = win[:, 4 * hs:4 * hs + 4, dy * WP:(dy + ROWS) * WP] \
                                .rearrange("p s (r c) -> p s r c", c=WP)[:, :, :, x0:x0 + W]
                            ev = lgp[:, k, :].unsqueeze(1).broadcast_to([128, 4, CH])
                            v.tensor_tensor(prod[:, hs, :, :].rearrange("p s (r c) -> p s r c", c=W), wv,
                                            ev.rearrange("p s (r c) -> p s r c", c=W),
                                            ALU.mult).then_inc(prod_done, 1)

                    for slot in range(SLOTS):
                        if first and slot < STEPS:
                            sub(slot)
                        if slot == 0 and second:
                            maxima(0)
                        if slot == 0 and last:
                            v.wait_ge(den_done, i - 1)
                            v.reciprocal(rden[:, :], ps_den[:, 0:CH]).then_inc(rden_done, 1)
                            v.wait_ge(rden_done, i - 1)
                            if not (isinstance(i, int) and i == 2):
                                v.wait_ge(out_sent, (i - 2) * 64)
                            v.tensor_tensor(cout[:, :, :], ps_acc[:, :, 0:CH],
                                            rden[:, :].unsqueeze(1).broadcast_to([128, 2, CH]),
                                            ALU.mult).then_inc(out_done, 1)
                        if second and slot >= LAG:
                            product(slot - LAG)

                v.memset(lg[96:128, 0, :, :], 0.0)
                v.memset(lg[96:128, 1, :, :], 0.0)
                schedule(v, body)

            @block.gpsimd
            def _(pool):
                def body(i, par, first, second, last):
                    if not second:
                        return
                    p = i - 1
                    pool.wait_ge(top_done, i * TOPS)
                    for k in range(STEPS):
                        n = 32 * taps(k)[2]
                        pool.tensor_tensor(lg[0:n, 1 - par, k, :], lg[0:n, 1 - par, k, :], topb[0:n, :],
                                           ALU.subtract).then_inc(shift_done, 1)
                schedule(pool, body)

            @block.scalar
            def _(act):
                def body(i, par, first, second, last):
                    p = i - 1

                    def front(j):
                        dy, x0, n = taps(j)
                        act.wait_ge(sub_done, i * STEPS + j + 1)
                        act.activation(diff[:, j % 2, 0:n, :], diff[:, j % 2, 0:n, :],
                                       ACT.Relu).then_inc(relu_done, 1)

                    def hidden(j):
                        dy, x0, n = taps(j)
                        for a in range(2):
                            m = min(2, n - 2 * a)
                            act.wait_ge(hid_done, i * (2 * STEPS) + 2 * j + a + 1)
                            if not (isinstance(i, int) and i == 0 and j < 2):
                                act.wait_ge(logit_done, i * STEPS + j - 1)
                            act.activation(hid[:, j % 2, a, 0:m, :], ps_hid[:, a, 0:m, 0:CH], ACT.Relu,
                                           bias=vec("t2")).then_inc(hrelu_done, 1)

                    def logits(j):
                        dy, x0, n = taps(j)
                        act.wait_ge(logit_done, i * STEPS + j + 1)
                        if j == 0 and not (isinstance(i, int) and i < 2):
                            act.wait_ge(acc_done, (i - 1) * (2 * STEPS))
                        act.activation(lg[0:32 * n, par, j, :], ps_lg[0:32 * n, 0:CH], ACT.Identity,
                                       bias=vec("cw2b")[0:32 * n]).then_inc(logit_out, 1)

                    for slot in range(SLOTS):
                        if first and slot < STEPS:
                            front(slot)
                            hidden(slot)
                        if second and slot >= LAG - 1 and slot < STEPS + LAG - 1:
                            k = slot - LAG + 1
                            n = 32 * taps(k)[2]
                            act.wait_ge(shift_done, p * STEPS + k + 1)
                            act.activation(lg[0:n, 1 - par, k, :], lg[0:n, 1 - par, k, :],
                                           ACT.Exp).then_inc(exp_done, 1)
                        if first and 1 <= slot <= STEPS:
                            logits(slot - 1)
                    if second:
                        act.wait_ge(acc_done, i * (2 * STEPS))
                        act.copy(dsum[:, :], ps_den[:, 0:CH]).then_inc(den_out, 1)
                schedule(act, body)

            @block.tensor
            def _(pe):
                def body(i, par, first, second, last):
                    p = i - 1

                    def hidden(j):
                        dy, x0, n = taps(j)
                        pe.wait_ge(relu_done, i * STEPS + j + 1)
                        for a in range(2):
                            m = min(2, n - 2 * a)
                            if not (isinstance(i, int) and i == 0 and j == 0):
                                pe.wait_ge(hrelu_done, i * (2 * STEPS) + 2 * j + a - 1)
                            for b in range(m):
                                ins = pe.matmul(ps_hid[:, a, b, 0:CH], mat("cw1"), diff[:, j % 2, 2 * a + b, :],
                                                start=True, stop=True)
                            ins.then_inc(hid_done, 1)

                    def logits(j):
                        dy, x0, n = taps(j)
                        if not (isinstance(i, int) and i == 0 and j == 0):
                            pe.wait_ge(logit_out, i * STEPS + j)
                        for q in range(n):
                            if q % 2 == 0:
                                pe.wait_ge(hrelu_done, i * (2 * STEPS) + 2 * j + q // 2 + 1)
                            ins = pe.matmul(ps_lg[32 * q:32 * q + 32, 0:CH], mat("cw2", 32), hid[:, j % 2, q // 2, q % 2, :],
                                            start=True, stop=True, tile_position=(0, 32 * q))
                        ins.then_inc(logit_done, 1)

                    def sums(k):
                        if k == 0 and not (isinstance(i, int) and i == 1):
                            pe.wait_ge(out_done, i - 1)
                        r = k % NQ
                        pe.wait_ge(exp_done, p * STEPS + k + 1)
                        pe.matmul(ps_den[32 * r:32 * r + 32, 0:CH], mat("tap_sum", 32), lg[:, 1 - par, k, :],
                                  start=(k < NQ), stop=(k >= STEPS - NQ), tile_position=(0, 32 * r))
                        for hs in range(2):
                            pe.wait_ge(prod_done, p * (2 * STEPS) + 2 * k + hs + 1)
                            for r in range(4):
                                ins = pe.matmul(ps_acc[32 * r:32 * r + 32, hs, 0:CH], mat("tap_sum", 32),
                                                prod[:, hs, r, :], start=(k == 0), stop=(k == STEPS - 1),
                                                tile_position=(0, 32 * r))
                            ins.then_inc(acc_done, 1)

                    for slot in range(SLOTS):
                        if first and slot < STEPS:
                            hidden(slot)
                        if slot == 0 and last:
                            pe.wait_ge(den_out, i - 1)
                            pe.matmul(ps_den[:, 0:CH], mat("tap_sum_all"), dsum[:, :], start=True,
                                      stop=True).then_inc(den_done, 1)
                        if first and 1 <= slot <= STEPS:
                            logits(slot - 1)
                        if second and slot >= LAG:
                            sums(slot - LAG)
                schedule(pe, body)


TT = 128
NT = -(-PIX // TT)
LAST = PIX - (NT - 1) * TT
GROUP = 4
NG = -(-NT // GROUP)
E, HID = 8, 256
HT = E * HID // 128
EP = E // 2
NORM = 112
NN = PIX // NORM

TOK_COLS, TOK_N = columns([
    ("ident", 128), ("drop", 128), ("wx", 3 * 128), ("wa", 3 * C), ("den", 1), ("fold", C), ("tvec", 12)])
FFN_COLS, FFN_N = columns([
    ("w1", E * HID), ("w2", HT * C), ("b1", HT), ("b2", EP), ("wg", 2 * E), ("bg", 2 * E), ("rank", 2 * E),
    ("spread", 2 * EP * 128)])
TVEC = {n: i for i, n in enumerate(["keep", "one", "wa", "wb", "wc", "bz", "br", "bf"])}


def columns_of(k):
    return slice(k * CH, (k + 1) * CH) if isinstance(k, int) else bass.ds(k * CH, CH)


def column_of(k):
    return slice(k, k + 1) if isinstance(k, int) else bass.ds(k, 1)


def tile_tokens(n):
    return TT if n < NT - 1 else LAST


def group_tiles(g):
    return range(GROUP * g, min(NT, GROUP * (g + 1)))


def token_norm(nc, tok, tres, xhat, xT, loads, t1_dram):
    with ExitStack() as ctx:
        def sb(name, shape, dt=F32):
            return ctx.enter_context(nc.sbuf_tensor(name, shape, dt))

        def sem(name):
            return ctx.enter_context(nc.semaphore(name))

        tag = "n1_" if loads else "n2_"
        if loads:
            xa = sb(tag + "xa", [128, PAIRS, PIX])
        sq = sb(tag + "sq", [128, NT, 128])
        mean = sb(tag + "mean", [128, PAIRS, 2 * NT])
        var = sb(tag + "var", [128, PAIRS, 2 * NT])
        rstd = sb(tag + "rstd", [128, PAIRS, 2 * NT])
        mhalf = sb(tag + "mhalf", [128, 2 * NT])
        ps_f = ctx.enter_context(nc.psum_tensor(tag + "ps_f", [128, 2, BANK], F32))
        ps_b = ctx.enter_context(nc.psum_tensor(tag + "ps_b", [128, 2, BANK], F32))

        loaded = [sem(tag + f"loaded{t}") for t in range(PAIRS)]
        added = sem(tag + "added")
        turned = sem(tag + "turned")
        turned_out = sem(tag + "turned_out")
        dve = sem(tag + "dve")
        centred = sem(tag + "centred")
        squared = sem(tag + "squared")
        var_done = sem(tag + "var_done")
        rstd_done = sem(tag + "rstd_done")
        normed = sem(tag + "normed")
        back = sem(tag + "back")
        back_out = sem(tag + "back_out")
        sent = sem(tag + "sent")
        ident = tok[:, TOK_COLS["ident"][0]:TOK_COLS["ident"][1]]

        def g_par(t, g):
            return (t * NG + g) % 2

        with nc.Block() as block:
            @block.sync
            def _(sp):
                if loads:
                    x, conv = loads
                    for t in range(PAIRS):
                        sp.dma_start(xa[:, t, :], x[2 * t:2 * t + 2].rearrange("b c h w -> (b c) (h w)")).then_inc(loaded[t], 16)
                        sp.dma_start(tres[:, t, :], conv[2 * t:2 * t + 2].rearrange("b c n -> (b c) n")).then_inc(loaded[t], 16)
                    for t in range(PAIRS):
                        sp.wait_ge(added, t + 1)
                        sp.dma_start(t1_dram[t], tres[:, t, :]).then_inc(sent, 16)
                    sp.wait_ge(sent, 16 * PAIRS)

            @block.gpsimd
            def _(pool):
                for t in range(PAIRS):
                    pool.wait_ge(var_done, t + 1)
                    pool.tensor_tensor(rstd[:, t, :], var[:, t, :], mhalf[:, :], ALU.pow).then_inc(rstd_done, 1)

            @block.tensor
            def _(pe):
                for t in range(PAIRS):
                    if loads:
                        pe.wait_ge(added, t + 1)
                    for g in range(NG):
                        if t * NG + g >= 2:
                            pe.wait_ge(turned_out, t * NG + g - 1)
                        for n in group_tiles(g):
                            m = tile_tokens(n)
                            ins = pe.transpose(ps_f[0:m, g_par(t, g), (n % GROUP) * 128:(n % GROUP) * 128 + 128],
                                               tres[:, t, n * TT:n * TT + m], ident)
                        ins.then_inc(turned, 1)
                for t in range(PAIRS):
                    pe.wait_ge(normed, t + 1)
                    for g in range(NG):
                        if t * NG + g >= 2:
                            pe.wait_ge(back_out, t * NG + g - 1)
                        for n in group_tiles(g):
                            m = tile_tokens(n)
                            ins = pe.transpose(ps_b[:, g_par(t, g), (n % GROUP) * TT:(n % GROUP) * TT + m],
                                               xT[0:m, t, n, :], ident[0:m, 0:m])
                        ins.then_inc(back, 1)

            @block.scalar
            def _(act):
                def forth(t):
                    for g in range(NG):
                        tiles = group_tiles(g)
                        m = tile_tokens(tiles[-1])
                        act.wait_ge(turned, t * NG + g + 1)
                        act.copy(xT[0:m, t, tiles[0]:tiles[-1] + 1, :].rearrange("p n c -> p (n c)"),
                                 ps_f[0:m, g_par(t, g), 0:128 * len(tiles)]).then_inc(turned_out, 1)

                def square(t):
                    act.wait_ge(centred, t + 1)
                    if t > 0:
                        act.wait_ge(var_done, t)
                    act.activation(sq[:, :, :], xT[:, t, :, :], ACT.Square).then_inc(squared, 1)

                def back_again(t):
                    for g in range(NG):
                        tiles = group_tiles(g)
                        n = sum(tile_tokens(a) for a in tiles)
                        act.wait_ge(back, t * NG + g + 1)
                        act.copy(xhat[:, t, tiles[0] * TT:tiles[0] * TT + n],
                                 ps_b[:, g_par(t, g), 0:n]).then_inc(back_out, 1)
                forth(0)
                square(0)
                forth(1)
                square(1)
                back_again(0)
                back_again(1)

            @block.vector
            def _(v):
                n = [0]

                def link(ins):
                    n[0] += 1
                    ins.then_inc(dve, 1)
                    v.wait_ge(dve, n[0])

                v.memset(mhalf[:, :], -0.5)
                for t in range(PAIRS):
                    link(v.memset(xT[LAST:128, t, NT - 1, :], 0.0))
                if loads:
                    for t in range(PAIRS):
                        v.wait_ge(loaded[t], 32)
                        v.tensor_tensor(tres[:, t, :], tres[:, t, :], xa[:, t, :], ALU.add).then_inc(added, 1)
                def rows(t):
                    return xT[:, t, :, :].rearrange("p n (i c) -> p (n i) c", i=2)

                def centre(t):
                    v.wait_ge(turned_out, NG * (t + 1))
                    link(v.tensor_reduce(mean[:, t, :], rows(t), AX.X, ALU.add))
                    link(v.tensor_scalar(mean[:, t, :], mean[:, t, :], 1.0 / C, None, ALU.mult))
                    v.tensor_tensor(rows(t), rows(t), mean[:, t, :].unsqueeze(2).broadcast_to([128, 2 * NT, C]),
                                    ALU.subtract).then_inc(centred, 1)

                def variance(t):
                    v.wait_ge(squared, t + 1)
                    link(v.tensor_reduce(var[:, t, :], sq[:, :, :].rearrange("p n (i c) -> p (n i) c", i=2),
                                         AX.X, ALU.add))
                    v.tensor_scalar(var[:, t, :], var[:, t, :], 1.0 / C, EPS, ALU.mult, ALU.add).then_inc(var_done, 1)

                def normalize(t):
                    v.wait_ge(rstd_done, t + 1)
                    v.wait_ge(squared, t + 1)
                    v.tensor_tensor(rows(t), rows(t), rstd[:, t, :].unsqueeze(2).broadcast_to([128, 2 * NT, C]),
                                    ALU.mult).then_inc(normed, 1)
                centre(0)
                variance(0)
                centre(1)
                normalize(0)
                variance(1)
                normalize(1)


def attention_prepare(nc, tok, xhat, xT, xs, vh, vl, wa):
    with ExitStack() as ctx:
        def sb(name, shape, dt=F32):
            return ctx.enter_context(nc.sbuf_tensor(name, shape, dt))

        def sem(name):
            return ctx.enter_context(nc.semaphore(name))

        proj = sb("ap_proj", [128, 2, 128])
        vbias = sb("ap_vbias", [128, 1])
        hi = sb("ap_hi", [128, PIX], F16)
        lo = sb("ap_lo", [128, PIX], F16)
        ps_w = ctx.enter_context(nc.psum_tensor("ap_ps_w", [128, 2, BANK], F32))
        ps_v = ctx.enter_context(nc.psum_tensor("ap_ps_v", [128, 2, BANK], F32))
        dve = sem("ap_dve")
        folded = sem("ap_folded")
        ready = sem("ap_ready")
        v_done = sem("ap_v_done")
        vh_done = sem("ap_vh_done")
        vl_done = sem("ap_vl_done")
        split = sem("ap_split")
        spread = sem("ap_spread")

        def mat(name, i=0, n=128):
            a = TOK_COLS[name][0] + i * n
            return tok[:, a:a + n]

        def vec(name):
            a = TOK_COLS["tvec"][0] + TVEC[name]
            return tok[:, a:a + 1]

        with nc.Block() as block:
            @block.sync
            def _(sp):
                for t in range(PAIRS):
                    sp.wait_ge(split, t + 1)
                    for i in range(2):
                        part = slice(64 * i, 64 * i + 64)
                        sp.dma_start(xs[0:64, 2 * t + i, :], hi[part, :]).then_inc(spread, 16)
                        sp.dma_start(xs[64:128, 2 * t + i, :], lo[part, :]).then_inc(spread, 16)
                sp.wait_ge(spread, 128)

            @block.tensor
            def _(pe):
                pe.matmul(ps_w[:, 0, 0:3 * C], mat("drop"), mat("wa", 0, 3 * C), start=True, stop=True)
                pe.matmul(ps_w[:, 1, 0:1], mat("drop"), vec("wb"), start=True, stop=True).then_inc(folded, 1)
                pe.wait_ge(ready, 1)
                for b in range(B):
                    for k in range(NCH):
                        g = b * NCH + k
                        if g >= 2:
                            pe.wait_ge(vl_done, g - 1)
                        pe.matmul(ps_v[:, g % 2, 0:CH], proj[:, b % 2, :], xhat[:, b // 2, k * CH:(k + 1) * CH],
                                  start=True, stop=True).then_inc(v_done, 1)

            @block.scalar
            def _(act):
                act.wait_ge(ready, 1)
                for g in range(B * NCH):
                    act.wait_ge(v_done, g + 1)
                    act.activation(vh[:, g // NCH, g % NCH * CH:(g % NCH + 1) * CH], ps_v[:, g % 2, 0:CH],
                                   ACT.Identity, bias=vbias[:, :]).then_inc(vh_done, 1)

            @block.vector
            def _(v):
                n = [0]

                def link(ins):
                    n[0] += 1
                    ins.then_inc(dve, 1)
                    v.wait_ge(dve, n[0])

                link(v.memset(proj[:, :, :], 0.0))
                for i in range(2):
                    part = slice(64 * i, 64 * i + 64)
                    for d in range(2):
                        ins = v.tensor_scalar(proj[part, i, 64 * d:64 * d + 64], mat("drop")[part, 0:64], vec("wc")[part], None, ALU.mult)
                link(ins)
                for i in range(2):
                    part = slice(64 * i, 64 * i + 64)
                    v.tensor_copy(proj[part, i, 63:64], vec("wa")[part])
                v.wait_ge(folded, 1)
                v.tensor_copy(wa[:, :], ps_w[:, 0, 0:3 * C])
                v.tensor_copy(vbias[:, :], ps_w[:, 1, 0:1]).then_inc(ready, 1)
                for t in range(PAIRS):
                    if t > 0:
                        v.wait_ge(spread, 64 * t)
                    link(v.tensor_scalar(hi[:, :], xhat[:, t, :], vec("keep"), vec("one"), ALU.mult, ALU.add))
                    v.scalar_tensor_tensor(out=lo[:, :], in0=xhat[:, t, :], scalar=vec("keep"), in1=hi[:, :],
                                           op0=ALU.mult, op1=ALU.subtract).then_inc(split, 1)
                    for c in (C - 1, 2 * C - 1):
                        v.memset(xT[:, t, 0:NT - 1, c], 1.0)
                        v.memset(xT[0:LAST, t, NT - 1:NT, c], 1.0)
                for g in range(B * NCH):
                    at = slice(g % NCH * CH, (g % NCH + 1) * CH)
                    v.wait_ge(vh_done, g + 1)
                    v.scalar_tensor_tensor(out=vl[:, g // NCH, at], in0=ps_v[:, g % 2, 0:CH], scalar=vbias[:, :],
                                           in1=vh[:, g // NCH, at], op0=ALU.add,
                                           op1=ALU.subtract).then_inc(vl_done, 1)


def attention(nc, tok, xT, xs, vh, vl, attn, m_dram):
    with ExitStack() as ctx:
        def sb(name, shape, dt=F32):
            return ctx.enter_context(nc.sbuf_tensor(name, shape, dt))

        def psum(name, shape):
            return ctx.enter_context(nc.psum_tensor(name, shape, F32))

        def sem(name):
            return ctx.enter_context(nc.semaphore(name))

        NP = 3
        prob = sb("at_prob", [128, NP, 2, CH])
        mpart = sb("at_mpart", [128, NT, NCH])
        mtop = sb("at_mtop", [128, NT])
        mrow = sb("at_mrow", [NT, TT], F16)
        ps_s = psum("at_ps_s", [128, 2, 2, BANK])
        ps_m = psum("at_ps_m", [128, 2, BANK])
        ps_a = psum("at_ps_a", [128, BANK])
        ps_t = psum("at_ps_t", [128, BANK])
        SL = (NT + 1) // 2
        LAG = 2

        rough_done = sem("at_rough_done")
        rough_max = sem("at_rough_max")
        top_done = sem("at_top_done")
        top_turned = sem("at_top_turned")
        top_half = sem("at_top_half")
        top_out = sem("at_top_out")
        top_in = sem("at_top_in")
        score_done = sem("at_score_done")
        exp_done = sem("at_exp_done")
        sum_done = sem("at_sum_done")
        attn_out = sem("at_attn_out")
        filled = sem("at_filled")
        ident = tok[:, TOK_COLS["ident"][0]:TOK_COLS["ident"][1]]

        def tiles(s):
            return range(2 * s, min(NT, 2 * s + 2))

        def stages(eng, body, tail, first=0):
            for b in range(first, B + 1):
                body(b, 0)
                with eng.Fori(1, NCH) as k:
                    body(b, k)
                if tail and b < B:
                    tail(b)

        def after(b, k, per):
            return k * per + b * NCH * per

        with nc.Block() as block:
            @block.sync
            def _(sp):
                for b in range(B):
                    sp.wait_ge(top_half, b + 1)
                    sp.dma_start(m_dram[b].rearrange("(n t) -> n t", t=TT), mrow[:, :]).then_inc(top_out, 16)
                    sp.wait_ge(top_out, 16 * (b + 1))
                    sp.dma_start(vh[127:128, b, :], m_dram[b:b + 1, 0:PIX]).then_inc(top_in, 16)
                sp.wait_ge(top_in, 16 * B)

            @block.tensor
            def _(pe):
                def body(b, k):
                    rough = b < B
                    main = b > 0
                    m = b - 1
                    if main:
                        pe.wait_ge(top_in, 16 * b)

                    def rough_scores(n):
                        if n < NT - 1:
                            pe.wait_ge(rough_max, after(b, k, NT) + max(0, n - 1) + (n == NT - 2))
                        w = tile_tokens(n)
                        pe.matmul(ps_m[0:w, n % 2, 0:CH], vh[:, b, n * TT:n * TT + w],
                                  xs[:, b, columns_of(k)], start=True, stop=True).then_inc(rough_done, 1)

                    def scores(s):
                        if s < SL - 1:
                            pe.wait_ge(exp_done, after(m, k, SL) + max(0, s - 1))
                        for a, n in enumerate(tiles(s)):
                            w = tile_tokens(n)
                            for h, half in enumerate((vh, vl)):
                                ins = pe.matmul(ps_s[0:w, s % 2, a, 0:CH], xs[:, m, n * TT:n * TT + w],
                                                half[:, m, columns_of(k)], start=(h == 0), stop=(h == 1))
                        ins.then_inc(score_done, 1)

                    def sums(s):
                        if s == 0:
                            pe.wait_ge(attn_out, after(m, k, 1))
                        pe.wait_ge(exp_done, after(m, k, SL) + s + 1)
                        for a, n in enumerate(tiles(s)):
                            i = m % 2
                            ins = pe.matmul(ps_a[64 * a:64 * a + 64, 0:CH], xT[:, m // 2, n, 64 * i:64 * i + 64],
                                            prob[:, s % NP, a, :], start=(n < 2), stop=(n >= NT - 2),
                                            tile_position=(0, 64 * a))
                        ins.then_inc(sum_done, 1)

                    for s in range(SL):
                        if main and s == SL - 1:
                            sums(s - LAG)
                        if main:
                            scores(s)
                        if rough:
                            for n in tiles(s):
                                rough_scores(n)
                        if main and LAG <= s < SL - 1:
                            sums(s - LAG)
                    if main:
                        for s in range(SL - LAG, SL):
                            sums(s)

                def tail(b):
                    pe.wait_ge(top_done, b + 1)
                    pe.transpose(ps_t[0:NT, 0:128], mtop[:, :], ident).then_inc(top_turned, 1)
                stages(pe, body, tail)

            @block.scalar
            def _(act):
                def body(b, k):
                    m = b - 1
                    for s in range(SL):
                        act.wait_ge(score_done, after(m, k, SL) + s + 1)
                        if s >= NP:
                            act.wait_ge(sum_done, after(m, k, SL) + s - NP + 1)
                        else:
                            act.wait_ge(sum_done, after(m, k, SL))
                        a = len(tiles(s))
                        w = tile_tokens(tiles(s)[-1])
                        act.activation(prob[0:w, s % NP, 0:a, :], ps_s[0:w, s % 2, 0:a, 0:CH],
                                       ACT.Exp).then_inc(exp_done, 1)
                stages(act, body, None, first=1)

            @block.vector
            def _(v):
                v.memset(mpart[:, NT - 1, :], 0.0).then_inc(filled, 1)
                v.wait_ge(filled, 1)

                def body(b, k):
                    if b < B:
                        for n in range(NT):
                            w = tile_tokens(n)
                            v.wait_ge(rough_done, after(b, k, NT) + n + 1)
                            v.tensor_reduce(mpart[0:w, n, column_of(k)], ps_m[0:w, n % 2, 0:CH], AX.X,
                                            ALU.max).then_inc(rough_max, 1)
                    if b > 0:
                        v.wait_ge(sum_done, after(b - 1, k, SL) + SL)
                        v.tensor_copy(attn[:, b - 1, columns_of(k)], ps_a[:, 0:CH]).then_inc(attn_out, 1)

                def tail(b):
                    v.wait_ge(rough_max, NT * NCH * (b + 1))
                    v.tensor_reduce(mtop[:, :], mpart[:, :, :], AX.X, ALU.max).then_inc(top_done, 1)
                    v.wait_ge(top_turned, b + 1)
                    if b > 0:
                        v.wait_ge(top_out, 16 * b)
                    v.tensor_copy(mrow[:, :], ps_t[0:NT, 0:128]).then_inc(top_half, 1)
                stages(v, body, tail)


def gates(nc, tok, wa, xhat, attn, tres, t1_dram):
    with ExitStack() as ctx:
        def sb(name, shape, dt=F32):
            return ctx.enter_context(nc.sbuf_tensor(name, shape, dt))

        def sem(name):
            return ctx.enter_context(nc.semaphore(name))

        rden = sb("ga_rden", [NORM, B, NN])
        hb = sb("ga_hb", [128, 2])
        g3 = sb("ga_g3", [128, 2, 3, CH])
        ps = ctx.enter_context(nc.psum_tensor("ga_ps", [128, 8, BANK], F32))
        dve = sem("ga_dve")
        in_t = [sem(f"ga_in_t{t}") for t in range(PAIRS)]
        den_done = sem("ga_den_done")
        rden_done = sem("ga_rden_done")
        spread_done = sem("ga_spread_done")
        attn_done = sem("ga_attn_done")
        gate_done = sem("ga_gate_done")
        tanh_done = sem("ga_tanh_done")
        used = sem("ga_used")
        NB = PAIRS * NCH

        def mat(name, i=0, n=128):
            a = TOK_COLS[name][0] + i * n
            return tok[:, a:a + n]

        def vec(name):
            a = TOK_COLS["tvec"][0] + TVEC[name]
            return tok[:, a:a + 1]

        ident = mat("ident")
        with nc.Block() as block:
            @block.sync
            def _(sp):
                for t in range(PAIRS):
                    sp.dma_start(tres[:, t, :], t1_dram[t]).then_inc(in_t[t], 16)

            @block.tensor
            def _(pe):
                for b in range(B):
                    for n in range(NN):
                        ins = pe.matmul(ps[0:NORM, 0, b * NN + n:b * NN + n + 1], attn[:, b, n * NORM:(n + 1) * NORM],
                                        mat("den", 0, 1), start=True, stop=True)
                    ins.then_inc(den_done, 1)
                for b in range(B):
                    pe.wait_ge(rden_done, b + 1)
                    for k in range(NCH):
                        g = b * NCH + k
                        if g >= 2:
                            pe.wait_ge(attn_done, g - 1)
                        for a in range(CH // NORM):
                            n = k * (CH // NORM) + a
                            ins = pe.transpose(ps[:, 6 + g % 2, a * NORM:(a + 1) * NORM],
                                               rden[:, b, n:n + 1].broadcast_to([NORM, 128]), ident[0:NORM, 0:NORM])
                        ins.then_inc(spread_done, 1)
                for g in range(NB):
                    t, k = divmod(g, NCH)
                    at = slice(k * CH, (k + 1) * CH)
                    pe.wait_ge(attn_done, (2 * t + 1) * NCH + k + 1)
                    for j in range(3):
                        if g >= 2:
                            pe.wait_ge(tanh_done, 3 * (g - 2) + j + 1)
                        bank = 3 * (g % 2) + j
                        for i in range(2):
                            pe.matmul(ps[64 * i:64 * i + 64, bank, 0:CH], mat("wx", 2 * j + i, C), xhat[:, t, at],
                                      start=True, stop=False, tile_position=(0, 64 * i))
                        for i in range(2):
                            ins = pe.matmul(ps[64 * i:64 * i + 64, bank, 0:CH], wa[:, j * C:(j + 1) * C],
                                            attn[:, 2 * t + i, at], start=False, stop=True,
                                            tile_position=(0, 64 * i))
                        ins.then_inc(gate_done, 1)

            @block.scalar
            def _(act):
                for g in range(NB):
                    if g >= 2:
                        act.wait_ge(used, g - 1)
                    for j in range(3):
                        act.wait_ge(gate_done, 3 * g + j + 1)
                        if g == 0 and j == 0:
                            act.wait_ge(dve, 1)
                        act.activation(g3[:, g % 2, j, :], ps[:, 3 * (g % 2) + j, 0:CH], ACT.Tanh,
                                       bias=vec("bz") if j == 0 else hb[:, j - 1:j],
                                       scale=1.0 if j == 0 else 0.5).then_inc(tanh_done, 1)

            @block.vector
            def _(v):
                a = TOK_COLS["tvec"][0] + TVEC["br"]
                v.tensor_scalar(hb[:, :], tok[:, a:a + 2], 0.5, None, ALU.mult).then_inc(dve, 1)
                for b in range(B):
                    v.wait_ge(den_done, B)
                    v.reciprocal(rden[:, b, :], ps[0:NORM, 0, b * NN:(b + 1) * NN]).then_inc(rden_done, 1)
                for b in range(B):
                    for k in range(NCH):
                        g = b * NCH + k
                        v.wait_ge(spread_done, g + 1)
                        at = slice(k * CH, (k + 1) * CH)
                        v.tensor_tensor(attn[:, b, at], attn[:, b, at], ps[:, 6 + g % 2, 0:CH],
                                        ALU.mult).then_inc(attn_done, 1)
                n = [1]

                def link(ins):
                    n[0] += 1
                    ins.then_inc(dve, 1)
                    v.wait_ge(dve, n[0])

                for g in range(NB):
                    t, k = divmod(g, NCH)
                    at = slice(k * CH, (k + 1) * CH)
                    z, r, f = (g3[:, g % 2, j, :] for j in range(3))
                    v.wait_ge(in_t[t], 16)
                    v.wait_ge(tanh_done, 3 * (g + 1))
                    v.scalar_tensor_tensor(out=r, in0=r, scalar=1.0, in1=xhat[:, t, at], op0=ALU.add, op1=ALU.mult)
                    link(v.scalar_tensor_tensor(out=f, in0=f, scalar=1.0, in1=z, op0=ALU.add, op1=ALU.mult))
                    link(v.tensor_tensor(r, r, f, ALU.add))
                    v.scalar_tensor_tensor(out=tres[:, t, at], in0=r, scalar=0.5, in1=tres[:, t, at],
                                           op0=ALU.mult, op1=ALU.add).then_inc(used, 1)


def route(nc, tok, ffn, xhat, w1h, w1l, xs, wt):
    with ExitStack() as ctx:
        def sb(name, shape, dt=F32):
            return ctx.enter_context(nc.sbuf_tensor(name, shape, dt))

        def sem(name):
            return ctx.enter_context(nc.semaphore(name))

        hi = sb("ro_hi", [128, PIX], F16)
        lo = sb("ro_lo", [128, PIX], F16)
        R = PAIRS * NT * 2
        lg = sb("ro_lg", [128, R, E])
        eq = sb("ro_eq", [128, R, E])
        one1 = sb("ro_one1", [128, R, E])
        best = sb("ro_best", [128, 4, R])
        ps_g = ctx.enter_context(nc.psum_tensor("ro_ps_g", [128, PAIRS, BANK], F32))
        ps_w = ctx.enter_context(nc.psum_tensor("ro_ps_w", [128, 2, BANK], F32))
        dve = sem("ro_dve")
        split = sem("ro_split")
        spread = sem("ro_spread")
        gate_done = sem("ro_gate_done")
        diff_done = sem("ro_diff_done")
        exp_done = sem("ro_exp_done")
        w_done = sem("ro_w_done")
        w_turned = sem("ro_w_turned")
        w_out = sem("ro_w_out")

        def mat(name, i=0, n=128):
            cols, tile = (FFN_COLS, ffn) if name in FFN_COLS else (TOK_COLS, tok)
            a = cols[name][0] + i * n
            return tile[:, a:a + n]

        with nc.Block() as block:
            @block.sync
            def _(sp):
                for t in range(PAIRS):
                    sp.wait_ge(split, t + 1)
                    for i in range(2):
                        part = slice(64 * i, 64 * i + 64)
                        sp.dma_start(xs[0:64, 2 * t + i, :], hi[part, :]).then_inc(spread, 16)
                        sp.dma_start(xs[64:128, 2 * t + i, :], lo[part, :]).then_inc(spread, 16)
                sp.wait_ge(spread, 128)

            @block.tensor
            def _(pe):
                for t in range(PAIRS):
                    for n in range(NT):
                        w = tile_tokens(n)
                        ins = pe.matmul(ps_g[0:w, t, 16 * n:16 * n + 16], xhat[:, t, n * TT:n * TT + w],
                                        mat("wg", 0, 2 * E), start=True, stop=True)
                ins.then_inc(gate_done, 1)
                pe.wait_ge(w_done, 1)
                for t in range(PAIRS):
                    for g in range(NG):
                        if t * NG + g >= 2:
                            pe.wait_ge(w_out, t * NG + g - 1)
                        for n in group_tiles(g):
                            w = tile_tokens(n)
                            r = (t * NT + n) * 2
                            ins = pe.transpose(ps_w[0:16, (t * NG + g) % 2, n % GROUP * TT:n % GROUP * TT + w],
                                               lg[0:w, r:r + 2, :].rearrange("p r e -> p (r e)"),
                                               mat("ident")[0:w, 0:w])
                        ins.then_inc(w_turned, 1)

            @block.scalar
            def _(act):
                act.wait_ge(diff_done, 1)
                act.activation(best[:, 2, :], best[:, 1, :], ACT.Exp).then_inc(exp_done, 1)

            @block.vector
            def _(v):
                n = [0]

                def link(ins):
                    n[0] += 1
                    ins.then_inc(dve, 1)
                    v.wait_ge(dve, n[0])

                v.memset(wt[:, :, :], 0.0)
                for t in range(PAIRS):
                    if t > 0:
                        v.wait_ge(spread, 64 * t)
                    link(v.tensor_copy(hi[:, :], xhat[:, t, :]))
                    v.tensor_tensor(lo[:, :], xhat[:, t, :], hi[:, :], ALU.subtract).then_inc(split, 1)
                link(v.tensor_copy(w1h[:, :], mat("w1", 0, E * HID)))
                v.tensor_tensor(w1l[:, :], mat("w1", 0, E * HID), w1h[:, :], ALU.subtract)
                v.wait_ge(gate_done, 1)
                link(v.memset(lg[:, :, :], 0.0))
                for t in range(PAIRS):
                    for a, w in ((0, NT - 1), (NT - 1, NT)):
                        p = TT if a == 0 else LAST
                        bg = mat("bg", 0, 2 * E)[0:p].unsqueeze(1).broadcast_to([p, w - a, 2 * E])
                        ins = v.tensor_tensor(lg[0:p, (t * NT + a) * 2:(t * NT + w) * 2, :]
                                              .rearrange("p (n i) e -> p n (i e)", i=2),
                                              ps_g[0:p, t, 16 * a:16 * w].rearrange("p (n c) -> p n c", c=16),
                                              bg, ALU.add)
                link(ins)
                rank = mat("rank", 0, E).unsqueeze(1).broadcast_to([128, R, E])

                def wide(i):
                    return best[:, i, :].unsqueeze(2).broadcast_to([128, R, E])

                def largest(i, out):
                    link(v.tensor_reduce(best[:, i, :], lg[:, :, :], AX.X, ALU.max))
                    link(v.tensor_tensor(eq[:, :, :], lg[:, :, :], wide(i), ALU.is_equal))
                    link(v.tensor_tensor(eq[:, :, :], eq[:, :, :], rank, ALU.mult))
                    link(v.tensor_reduce(best[:, 3, :], eq[:, :, :], AX.X, ALU.max))
                    link(v.tensor_tensor(out, eq[:, :, :], wide(3), ALU.is_equal))

                largest(0, one1[:, :, :])
                link(v.scalar_tensor_tensor(out=lg[:, :, :], in0=one1[:, :, :], scalar=-3.0e38, in1=lg[:, :, :],
                                            op0=ALU.mult, op1=ALU.add))
                largest(1, eq[:, :, :])
                v.tensor_tensor(best[:, 1, :], best[:, 1, :], best[:, 0, :], ALU.subtract).then_inc(diff_done, 1)
                v.wait_ge(exp_done, 1)
                link(v.tensor_scalar(best[:, 3, :], best[:, 2, :], 1.0, None, ALU.add))
                link(v.reciprocal(best[:, 0, :], best[:, 3, :]))
                link(v.tensor_tensor(best[:, 1, :], best[:, 2, :], best[:, 0, :], ALU.mult))
                v.tensor_tensor(one1[:, :, :], one1[:, :, :], wide(0), ALU.mult)
                link(v.tensor_tensor(eq[:, :, :], eq[:, :, :], wide(1), ALU.mult))
                v.tensor_tensor(lg[:, :, :], one1[:, :, :], eq[:, :, :], ALU.add).then_inc(w_done, 1)
                for t in range(PAIRS):
                    for g in range(NG):
                        tiles = group_tiles(g)
                        c = sum(tile_tokens(a) for a in tiles)
                        at = slice(tiles[0] * TT, tiles[0] * TT + c)
                        v.wait_ge(w_turned, t * NG + g + 1)
                        src = ps_w[0:16, (t * NG + g) % 2, 0:c]
                        link(v.tensor_copy(wt[0:16, t, at], src))
                        v.tensor_tensor(wt[32:48, t, at], src, wt[0:16, t, at], ALU.subtract).then_inc(w_out, 1)


def experts(nc, tok, ffn, w1h, w1l, xs, wt, tres, out):
    with ExitStack() as ctx:
        def sb(name, shape, dt=F32):
            return ctx.enter_context(nc.sbuf_tensor(name, shape, dt))

        def psum(name, shape):
            return ctx.enter_context(nc.psum_tensor(name, shape, F32))

        def sem(name):
            return ctx.enter_context(nc.semaphore(name))

        NHB = 8
        hid = sb("ex_hid", [128, NHB, CH])
        wide = sb("ex_wide", [128, 2, CH])
        part = sb("ex_part", [128, EP, CH])
        total = sb("ex_total", [128, 2, CH])
        spread16 = sb("ex_spread16", [128, 2 * EP * 128], F16)
        ps_h = psum("ex_ps_h", [128, 4, BANK])
        ps_o = psum("ex_ps_o", [128, 2, BANK])
        ps_w = psum("ex_ps_w", [128, BANK])
        ps_t = psum("ex_ps_t", [128, BANK])
        cast = sem("ex_cast")
        h_done = sem("ex_h_done")
        gelu_done = sem("ex_gelu_done")
        o_done = sem("ex_o_done")
        wide_done = sem("ex_wide_done")
        wide_out = sem("ex_wide_out")
        part_done = sem("ex_part_done")
        sum_done = sem("ex_sum_done")
        total_done = sem("ex_total_done")
        res_done = sem("ex_res_done")
        sent = sem("ex_sent")

        def mat(name, i=0, n=128):
            cols, tile = (FFN_COLS, ffn) if name in FFN_COLS else (TOK_COLS, tok)
            a = cols[name][0] + i * n
            return tile[:, a:a + n]

        UNITS = B * NCH
        HP2 = HT // EP

        def order(ep):
            return [((2 * ep + a) * 2 + h, a, h) for h in range(2) for a in range(2)]

        def units(eng, body):
            for b in range(B):
                body(b, 0, b * NCH, (b - 1, NCH - 1) if b else None)
                with eng.Fori(1, NCH) as k:
                    body(b, k, b * NCH + k, (b, k - 1))

        with nc.Block() as block:
            @block.tensor
            def _(pe):
                pe.wait_ge(cast, 1)

                def body(b, k, u, before):
                    def hidden(j):
                        n = order(j // HP2)[j % HP2][0]
                        pe.wait_ge(gelu_done, u * HT + max(0, j - 3))
                        for h, w in enumerate((w1h, w1l)):
                            ins = pe.matmul(ps_h[:, j % 4, 0:CH], w[:, n * 128:(n + 1) * 128],
                                            xs[:, b, columns_of(k)], start=(h == 0), stop=(h == 1))
                        ins.then_inc(h_done, 1)

                    def outer(j):
                        ep = j // HP2
                        n, a, h = order(ep)[j % HP2]
                        if j % HP2 == 0:
                            pe.wait_ge(part_done, u * EP + max(0, ep - 1))
                        pe.wait_ge(gelu_done, u * HT + j + 1)
                        ins = pe.matmul(ps_o[64 * a:64 * a + 64, ep % 2, 0:CH], mat("w2", n, C), hid[:, j % NHB, :],
                                        start=(h == 0), stop=(h == 1), tile_position=(0, 64 * a))
                        if j % HP2 == HP2 - 1:
                            ins.then_inc(o_done, 1)

                    def weights(ep):
                        pe.wait_ge(wide_out, u * EP + ep)
                        s = (b % 2) * EP + ep
                        pe.matmul(ps_w[:, 0:CH], spread16[:, s * 128:(s + 1) * 128], wt[:, b // 2, columns_of(k)],
                                  start=True, stop=True).then_inc(wide_done, 1)

                    for j in range(HT + 2):
                        if j < HT:
                            hidden(j)
                            if j % HP2 == 0:
                                weights(j // HP2)
                        if j >= 2:
                            outer(j - 2)
                        if j == HP2 and before:
                            fold(before[0], u - 1)

                def fold(b, u):
                    i = b % 2
                    pe.wait_ge(sum_done, u * 3 + 3)
                    pe.matmul(ps_t[64 * i:64 * i + 64, 0:CH], mat("fold", 0, C), total[:, 1, :], start=True,
                              stop=True, tile_position=(0, 64 * i)).then_inc(total_done, 1)
                units(pe, body)
                fold(B - 1, UNITS - 1)

            @block.scalar
            def _(act):
                def body(b, k, u, before):
                    for j in range(HT):
                        n = order(j // HP2)[j % HP2][0]
                        act.wait_ge(h_done, u * HT + j + 1)
                        if j % HP2 == 1:
                            ep = j // HP2
                            act.wait_ge(wide_done, u * EP + ep + 1)
                            act.wait_ge(part_done, u * EP + max(0, ep - 1))
                            act.copy(wide[:, ep % 2, :], ps_w[:, 0:CH]).then_inc(wide_out, 1)
                        act.wait_ge(o_done, u * EP + max(0, j // HP2 - 1))
                        act.activation(hid[:, j % NHB, :], ps_h[:, j % 4, 0:CH], ACT.Gelu,
                                       bias=mat("b1", n, 1)).then_inc(gelu_done, 1)
                units(act, body)

            @block.vector
            def _(v):
                v.tensor_copy(spread16[:, :], mat("spread", 0, 2 * EP * 128)).then_inc(cast, 1)

                def body(b, k, u, before):
                    for ep in range(EP):
                        v.wait_ge(o_done, u * EP + ep + 1)
                        v.wait_ge(wide_out, u * EP + ep + 1)
                        if ep == 1 and before:
                            residual(*before, u - 1)
                        v.wait_ge(sum_done, u * 3)
                        v.scalar_tensor_tensor(out=part[:, ep, :], in0=ps_o[:, ep % 2, 0:CH], scalar=mat("b2", ep, 1),
                                               in1=wide[:, ep % 2, :], op0=ALU.add,
                                               op1=ALU.mult).then_inc(part_done, 1)

                def residual(b, k, u):
                    i = b % 2
                    at = tres[64 * i:64 * i + 64, b // 2, columns_of(k)]
                    v.wait_ge(total_done, u + 1)
                    v.tensor_tensor(at, at, ps_t[64 * i:64 * i + 64, 0:CH], ALU.add).then_inc(res_done, 1)
                units(v, body)
                residual(B - 1, NCH - 1, UNITS - 1)

            @block.gpsimd
            def _(pool):
                def body(b, k, u, before):
                    pool.wait_ge(part_done, u * EP + 2)
                    pool.tensor_tensor(total[:, 0, :], part[:, 0, :], part[:, 1, :], ALU.add).then_inc(sum_done, 1)
                    pool.wait_ge(part_done, u * EP + 3)
                    pool.wait_ge(sum_done, u * 3 + 1)
                    pool.tensor_tensor(total[:, 0, :], total[:, 0, :], part[:, 2, :], ALU.add).then_inc(sum_done, 1)
                    pool.wait_ge(part_done, u * EP + 4)
                    pool.wait_ge(sum_done, u * 3 + 2)
                    pool.wait_ge(total_done, u)
                    pool.tensor_tensor(total[:, 1, :], total[:, 0, :], part[:, 3, :], ALU.add).then_inc(sum_done, 1)
                units(pool, body)

            @block.sync
            def _(sp):
                def body(b, k, u, before):
                    sp.wait_ge(res_done, u + 1)
                    i = b % 2
                    sp.dma_start(bass.AP(tensor=out.tensor, offset=b * C * PIX + k * CH, ap=[[PIX, C], [1, CH]]),
                                 tres[64 * i:64 * i + 64, b // 2, columns_of(k)]).then_inc(sent, 16)
                units(sp, body)
                sp.wait_ge(sent, 16 * UNITS)


def token_constants(w):
    f = np.float32
    tok = np.zeros((128, TOK_N), f)
    ffn = np.zeros((128, FFN_N), f)

    def put(name, a, i=0):
        cols, out = (FFN_COLS, ffn) if name in FFN_COLS else (TOK_COLS, tok)
        at = cols[name][0] + i * a.shape[1]
        out[:a.shape[0], at:at + a.shape[1]] = a

    put("ident", np.eye(128, dtype=f))
    drop = np.eye(C, dtype=f)
    drop[C - 1, :] = -1.0
    drop[C - 1, C - 1] = 0.0
    put("drop", np.tile(drop, (2, 2)))
    for j, n in enumerate(("z", "r", "f")):
        g = w[f"L1_attn_{n}_w"]
        m = np.zeros((2, C, 2, C), f)
        for i in range(2):
            m[i, :, i, :] = g[:, :C].T
        put("wx", m.reshape(128, 128), j)
        put("wa", np.ascontiguousarray(g[:, C:].T), j)
    den = np.zeros((128, 1), f)
    den[C - 1] = den[2 * C - 1] = 1.0
    put("den", den)
    put("fold", np.tile(np.eye(C, dtype=f), (2, 1)))
    put("w1", np.tile(w["L1_ffn_W1"].transpose(1, 0, 2).reshape(C, E * HID), (2, 1)))
    put("w2", w["L1_ffn_W2"].reshape(HT, 128, C).transpose(1, 0, 2).reshape(128, HT * C))
    put("b1", w["L1_ffn_b1"].reshape(HT, 128).T)
    put("b2", w["L1_ffn_b2"].reshape(EP, 2 * C).T)
    m = np.zeros((2, C, 2, E), f)
    for i in range(2):
        m[i, :, i, :] = w["L1_ffn_Wg"]
    put("wg", m.reshape(128, 2 * E))
    put("bg", np.tile(w["L1_ffn_bg"], (128, 2)))
    put("rank", np.tile(np.arange(E, 0, -1, dtype=f), (128, 2)))
    m = np.zeros((128, 2, EP, 2, C), f)
    for i in range(2):
        for e in range(E):
            for half in (0, 32):
                m[half + i * E + e, i, e // 2, e % 2, :] = 1.0
    put("spread", m.reshape(128, 2 * EP * 128))
    v = np.zeros((128, 12), f)
    v[:, TVEC["keep"]] = np.tile(np.arange(C) < C - 1, 2)
    v[:, TVEC["one"]] = np.tile(np.arange(C) == C - 1, 2)
    a = w["L1_attn_att_w"]
    v[:, TVEC["wa"]] = np.tile(a[:C], 2)
    v[:C, TVEC["wb"]] = a[C:2 * C]
    v[:, TVEC["wc"]] = np.tile(a[2 * C:], 2)
    for n in "zrf":
        v[:, TVEC["b" + n]] = np.tile(w[f"L1_attn_{n}_b"], 2)
    put("tvec", v)
    return tok, ffn


def build(nc, x, conv_c, tok_c, ffn_c, out):
    conv_out = nc.dram_tensor("conv_out", (B, C, PIX), F32).ap()
    t1_dram = nc.dram_tensor("t1_dram", (PAIRS, 128, PIX), F32).ap()
    m_dram = nc.dram_tensor("m_dram", (B, NT * TT), F16).ap()
    with ExitStack() as ctx:
        def sb(name, shape, dt=F32):
            return ctx.enter_context(nc.sbuf_tensor(name, shape, dt))

        cst = sb("cst", [128, CONV_N])
        x1 = sb("x1", [128, PIX])
        x2p = sb("x2p", [128, PADDED])
        x3st = sb("x3st", [128, 2, STAGE])
        conv_prepare(nc, x, conv_c, cst, x1, x2p, x3st)
        conv_main(nc, cst, x1, x2p, x3st, conv_out)
    with ExitStack() as whole:
        tok = whole.enter_context(nc.sbuf_tensor("tok", [128, TOK_N], F32))
        xhat = whole.enter_context(nc.sbuf_tensor("xhat", [128, PAIRS, PIX], F32))
        xT = whole.enter_context(nc.sbuf_tensor("xT", [128, PAIRS, NT, 128], F32))
        wa = whole.enter_context(nc.sbuf_tensor("wa", [128, 3 * C], F32))
        load(nc, [(tok, tok_c)])
        tres = whole.enter_context(nc.sbuf_tensor("tres", [128, PAIRS, PIX], F32))
        token_norm(nc, tok, tres, xhat, xT, (x, conv_out), t1_dram)
        with nc.sbuf_tensor("attn", [128, B, PIX], F32) as attn:
            with nc.sbuf_tensor("vh", [128, B, PIX], F16) as vh, nc.sbuf_tensor("vl", [128, B, PIX], F16) as vl:
                xs = tres[:, :, :].rearrange("p t n -> p (t n)").bitcast(F16).rearrange("p (b n) -> p b n", b=B)
                attention_prepare(nc, tok, xhat, xT, xs, vh, vl, wa)
                attention(nc, tok, xT, xs, vh, vl, attn, m_dram)
            gates(nc, tok, wa, xhat, attn, tres, t1_dram)
        with ExitStack() as ctx:
            ffn = ctx.enter_context(nc.sbuf_tensor("ffn", [128, FFN_N], F32))
            w1h = ctx.enter_context(nc.sbuf_tensor("w1h", [128, E * HID], F16))
            w1l = ctx.enter_context(nc.sbuf_tensor("w1l", [128, E * HID], F16))
            xs = ctx.enter_context(nc.sbuf_tensor("xs2", [128, B, PIX], F16))
            wt = ctx.enter_context(nc.sbuf_tensor("wt", [128, PAIRS, PIX], F16))
            load(nc, [(ffn, ffn_c)])
            token_norm(nc, tok, tres, xhat, xT, None, None)
            route(nc, tok, ffn, xhat, w1h, w1l, xs, wt)
            experts(nc, tok, ffn, w1h, w1l, xs, wt, tres, out)


def load(nc, pairs):
    with nc.semaphore() as arrived, nc.Block() as block:
        @block.sync
        def _(sp):
            for tile, dram in pairs:
                sp.dma_start(tile[:, :], dram).then_inc(arrived, 16)
            sp.wait_ge(arrived, 16 * len(pairs))


def conv_constants(w):
    f = np.float32
    out = np.zeros((128, CONV_N), f)

    def put(name, a, i=0):
        at = CONV_COLS[name][0] + i * a.shape[1]
        out[:, at:at + a.shape[1]] = a

    for name, src in (("w1", w["L0_conv_w1c"]), ("w2", w["L0_conv_w2c"])):
        for t in range(PAIRS):
            m = np.zeros((2, C, B, CR), f)
            for i in range(2):
                m[i, :, 2 * t + i, :] = src.T
            put(name, m.reshape(128, 128), t)
    w3 = w["L0_conv_w3c"].reshape(NH, 2, 4, C)
    for s in range(2):
        for t in range(PAIRS):
            m = np.zeros((2, C, 4, B, NH), f)
            for i in range(2):
                m[i, :, :, 2 * t + i, :] = w3[:, s].transpose(2, 1, 0)
            put("w3", m.reshape(128, 128), s * PAIRS + t)
    m = np.zeros((B, CR, B, CR), f)
    for b in range(B):
        m[b, :, b, :] = w["L0_conv_cw1"]
    put("cw1", m.reshape(128, 128))
    m = np.zeros((B, CR, B, NH), f)
    for b in range(B):
        m[b, :, b, :] = w["L0_conv_cw2"].T
    put("cw2", m.reshape(128, 32))
    eye = np.eye(128, dtype=f)
    put("ident", eye)
    put("pair_mean", np.kron(np.eye(64, dtype=f), np.full((2, 2), 0.5, f)))
    put("tap_sum", np.tile(np.eye(32, dtype=f), (4, 1)))
    put("tap_sum_all", np.tile(np.eye(32, dtype=f), (4, 4)))
    b3 = w["L0_conv_b3c"].reshape(NH, 2, 4)
    rows = {n: np.tile(w["L0_conv_" + s], B) for n, s in
            (("b1", "b1c"), ("b2", "b2c"), ("g1", "bn1_g"), ("t1", "bn1_b"), ("m1", "bn1_m"), ("v1", "bn1_v"),
             ("g2", "bn2_g"), ("t2", "bn2_b"), ("m2", "bn2_m"), ("v2", "bn2_v"))}
    for s, n in enumerate(("b3a", "b3b")):
        rows[n] = np.broadcast_to(b3[:, s].T[:, None, :], (4, B, NH)).reshape(128)
    rows["cw2b"] = np.tile(w["L0_conv_cw2_b"], 16)
    rows["mhalf"] = np.full(128, -0.5, f)
    v = np.zeros((128, 16), f)
    for n, a in rows.items():
        v[:, VEC[n]] = a
    put("vec", v)
    return out


def kernel(**inputs):
    import concourse.bacc as bacc
    from concourse.bass_utils import run_bass_kernel_spmd

    w = {n: np.asarray(a) for n, a in inputs.items()}
    tok_c, ffn_c = token_constants(w)
    arrays = {"x": np.ascontiguousarray(w["x"]), "conv_c": conv_constants(w), "tok_c": tok_c, "ffn_c": ffn_c}
    nc = bacc.Bacc("TRN2", target_bir_lowering=False, num_devices=1)
    args = [nc.dram_tensor(n, a.shape, F32, kind="ExternalInput").ap() for n, a in arrays.items()]
    out = nc.dram_tensor("out", (B, C, H, W), F32, kind="ExternalOutput").ap()
    build(nc, *args, out)
    r = run_bass_kernel_spmd(nc, [arrays], core_ids=[0])
    return r.results[0]["out"]
```

```python
from contextlib import ExitStack

import numpy as np

import concourse.bass as bass
from concourse import mybir

F32 = mybir.dt.float32
F16 = mybir.dt.float16
ALU = mybir.AluOpType
ACT = mybir.ActivationFunctionType
AX = mybir.AxisListType

B, C, H, W = 4, 64, 56, 56
PIX = H * W
PAIRS = B // 2
K, PAD = 7, 3
HP, WP = H + 2 * PAD, W + 2 * PAD
CR = 32
NH, SP = 8, 8
NQ = 4
ROWS = 8
CH = ROWS * W
NCH = H // ROWS
STEPS = 2 * K
WROWS = ROWS + K - 1
WIN = WROWS * WP
PADDED = HP * WP
STAGE = PADDED + 4
BANK = 512
EPS = 1e-5


def taps(j):
    return j // 2, NQ * (j % 2), NQ if j % 2 == 0 else K - NQ


def columns(parts):
    at, out = 0, {}
    for name, n in parts:
        out[name] = (at, at + n)
        at += n
    return out, at


CONV_COLS, CONV_N = columns([
    ("w1", PAIRS * 128), ("w2", PAIRS * 128), ("w3", 2 * PAIRS * 128), ("cw1", 128), ("cw2", 32),
    ("pair_mean", 128), ("tap_sum", 32), ("tap_sum_all", 128), ("ident", 128),
    ("vec", 16)])
VEC = {n: i for i, n in enumerate(
    ["b1", "b2", "b3a", "b3b", "g1", "t1", "m1", "v1", "g2", "t2", "m2", "v2", "cw2b", "mhalf"])}


def conv_prepare(nc, x, consts, cst, x1, x2p, x3_dram):
    with ExitStack() as ctx:
        def sb(name, shape, dt=F32):
            return ctx.enter_context(nc.sbuf_tensor(name, shape, dt))

        def sem(name):
            return ctx.enter_context(nc.semaphore(name))

        xin = sb("cp_xin", [128, PAIRS, PIX])
        xn = sb("cp_xn", [128, PAIRS, PIX])
        stats = sb("cp_stats", [128, PAIRS, NCH, 6])
        mv = sb("cp_mv", [128, PAIRS, 2])
        mom = sb("cp_mom", [128, PAIRS, 2])
        gm = sb("cp_gm", [128, PAIRS, 2])
        var = sb("cp_var", [128, PAIRS])
        rstd = sb("cp_rstd", [128, PAIRS])
        bnv = sb("cp_bnv", [128, 2])
        half = sb("cp_half", [128, 2])
        cwt = sb("cp_cwt", [128, 128])
        tmp = sb("cp_tmp", [128, 4])
        x3st = sb("cp_x3st", [128, 2, STAGE])
        psx = ctx.enter_context(nc.psum_tensor("cp_psx", [128, 2, 4, BANK], F32))

        x_in = [sem(f"cp_x_in{t}") for t in range(PAIRS)]
        c_in = sem("cp_c_in")
        dve = sem("cp_dve")
        moments = sem("cp_moments")
        grouped = sem("cp_grouped")
        var_ready = sem("cp_var_ready")
        rstd_ready = sem("cp_rstd_ready")
        xn_ready = sem("cp_xn_ready")
        bn_ready = sem("cp_bn_ready")
        cw_scaled = sem("cp_cw_scaled")
        cw_turned = sem("cp_cw_turned")
        cw_copied = sem("cp_cw_copied")
        conv_done = sem("cp_conv_done")
        evac_done = sem("cp_evac_done")
        padded = sem("cp_padded")
        x3_sent = sem("cp_x3_sent")

        def vec(name):
            a = CONV_COLS["vec"][0] + VEC[name]
            return cst[:, a:a + 1]

        def mat(name, i=0, n=128):
            a = CONV_COLS[name][0] + i * n
            return cst[:, a:a + n]

        with nc.Block() as block:
            @block.sync
            def _(sp):
                sp.dma_start(xin[:, 0, :], x[0:2].rearrange("b c h w -> (b c) (h w)")).then_inc(x_in[0], 16)
                sp.dma_start(cst[:, :], consts).then_inc(c_in, 16)
                sp.wait_ge(padded, 1)
                for r in range(4):
                    sp.dma_start(x3_dram[:, r::4, :], x3st[32 * r:32 * r + 32, :, :]).then_inc(x3_sent, 16)
                sp.wait_ge(x3_sent, 64)

            @block.gpsimd
            def _(pool):
                pool.wait_ge(var_ready, 1)
                pool.tensor_tensor(rstd[:, :], var[:, :], half[:, :], ALU.pow).then_inc(rstd_ready, 1)
                pool.tensor_tensor(bnv[:, :], bnv[:, :], half[:, :], ALU.pow).then_inc(rstd_ready, 1)

            @block.vector
            def _(v):
                n = [0]

                def link(ins):
                    n[0] += 1
                    ins.then_inc(dve, 1)
                    v.wait_ge(dve, n[0])

                v.wait_ge(c_in, 16)
                v.tensor_copy(half[:, 0:1], vec("mhalf"))
                v.tensor_copy(half[:, 1:2], vec("mhalf"))
                v.tensor_scalar(bnv[:, 0:1], vec("v1"), EPS, None, ALU.add)
                v.tensor_scalar(bnv[:, 1:2], vec("v2"), EPS, None, ALU.add)
                for t in range(PAIRS):
                    v.wait_ge(x_in[t], 16)
                    for k in range(NCH):
                        ins = v.bn_stats(stats[:, t, k, :], xin[:, t, k * CH:(k + 1) * CH])
                    link(ins)
                    link(v.bn_aggr(mv[:, t, :], stats[:, t, :, :].rearrange("p k s -> p (k s)")))
                link(v.tensor_tensor(mom[:, :, 0], mv[:, :, 0], mv[:, :, 0], ALU.mult))
                link(v.tensor_tensor(mom[:, :, 1], mom[:, :, 0], mv[:, :, 1], ALU.add))
                v.tensor_copy(mom[:, :, 0], mv[:, :, 0]).then_inc(moments, 1)
                v.wait_ge(grouped, 1)
                link(v.tensor_copy(gm[:, :, :], psx[:, 0, 0, 0:4].rearrange("p (t m) -> p t m", m=2)))
                link(v.tensor_tensor(var[:, :], gm[:, :, 0], gm[:, :, 0], ALU.mult))
                link(v.tensor_tensor(var[:, :], gm[:, :, 1], var[:, :], ALU.subtract))
                v.tensor_scalar(var[:, :], var[:, :], EPS, None, ALU.add).then_inc(var_ready, 1)
                v.wait_ge(rstd_ready, 1)
                for t in range(PAIRS):
                    v.tensor_scalar(xn[:, t, :], xin[:, t, :], gm[:, t, 0:1], rstd[:, t:t + 1],
                                    ALU.subtract, ALU.mult).then_inc(xn_ready, 1)
                v.wait_ge(rstd_ready, 2)
                link(v.tensor_tensor(tmp[:, 0:1], vec("g1"), bnv[:, 0:1], ALU.mult))
                link(v.tensor_tensor(tmp[:, 1:2], vec("g2"), bnv[:, 1:2], ALU.mult))
                link(v.tensor_tensor(tmp[:, 2:3], vec("b1"), vec("m1"), ALU.subtract))
                link(v.scalar_tensor_tensor(out=tmp[:, 2:3], in0=tmp[:, 2:3], scalar=tmp[:, 0:1],
                                            in1=vec("t1"), op0=ALU.mult, op1=ALU.add))
                link(v.tensor_tensor(tmp[:, 3:4], vec("b2"), tmp[:, 0:1], ALU.mult))
                link(v.tensor_tensor(vec("m2"), vec("m2"), tmp[:, 1:2], ALU.mult))
                link(v.tensor_tensor(vec("t2"), vec("t2"), vec("m2"), ALU.subtract))
                v.tensor_scalar(cwt[:, :], mat("cw1"), tmp[:, 1:2], None, ALU.mult).then_inc(bn_ready, 1)
                v.wait_ge(cw_turned, 1)
                v.tensor_copy(mat("cw1"), psx[:, 1, 0, 0:128]).then_inc(cw_copied, 1)
                v.wait_ge(evac_done, 4 * NCH)
                x3v = x3st[:, :, 0:PADDED].rearrange("p s (r c) -> p s r c", c=WP)
                x2v = x2p[:, :].rearrange("p (r c) -> p r c", c=WP)
                v.memset(x3st[:, :, PADDED:STAGE], 0.0)
                for d in range(PAD):
                    for a, b in ((d, 2 * PAD - d), (WP - 1 - d, WP - 1 - 2 * PAD + d)):
                        v.tensor_copy(x3v[:, :, PAD:PAD + H, a], x3v[:, :, PAD:PAD + H, b])
                        ins = v.tensor_copy(x2v[:, PAD:PAD + H, a], x2v[:, PAD:PAD + H, b])
                link(ins)
                for d in range(PAD):
                    for a, b in ((d, 2 * PAD - d), (HP - 1 - d, HP - 1 - 2 * PAD + d)):
                        ins = v.tensor_copy(x3v[:, :, a, :], x3v[:, :, b, :])
                        v.tensor_copy(x2v[:, a, :], x2v[:, b, :])
                ins.then_inc(padded, 1)

            @block.scalar
            def _(act):
                act.dma_start(xin[:, 1, :], x[2:4].rearrange("b c h w -> (b c) (h w)")).then_inc(x_in[1], 16)
                act.wait_ge(bn_ready, 1)
                x2v = x2p[:, :].rearrange("p (r c) -> p r c", c=WP)
                for k in range(NCH):
                    act.wait_ge(conv_done, k + 1)
                    ps = psx[:, k % 2, :, 0:CH]
                    rows = slice(PAD + k * ROWS, PAD + (k + 1) * ROWS)
                    act.activation(x1[:, k * CH:(k + 1) * CH], ps[:, 0, :], ACT.Identity,
                                   bias=tmp[:, 2:3], scale=tmp[:, 0:1]).then_inc(evac_done, 1)
                    act.activation(x2v[:, rows, PAD:PAD + W], ps[:, 1, :].rearrange("p (r c) -> p r c", c=W),
                                   ACT.Identity, bias=tmp[:, 3:4], scale=tmp[:, 0:1]).then_inc(evac_done, 1)
                    for s in range(2):
                        x3v = x3st[:, s, 0:PADDED].rearrange("p (r c) -> p r c", c=WP)
                        act.activation(x3v[:, rows, PAD:PAD + W],
                                       ps[:, 2 + s, :].rearrange("p (r c) -> p r c", c=W), ACT.Identity,
                                       bias=vec("b3b" if s else "b3a")).then_inc(evac_done, 1)

            @block.tensor
            def _(pe):
                pe.wait_ge(c_in, 16)
                pe.wait_ge(moments, 1)
                pe.matmul(psx[:, 0, 0, 0:4], mat("pair_mean"), mom[:, :, :].rearrange("p t m -> p (t m)"),
                          start=True, stop=True).then_inc(grouped, 1)
                pe.wait_ge(bn_ready, 1)
                pe.transpose(psx[:, 1, 0, 0:128], cwt[:, :], mat("ident")).then_inc(cw_turned, 1)
                for k in range(NCH):
                    pe.wait_ge(xn_ready, 2)
                    if k == 1:
                        pe.wait_ge(cw_copied, 1)
                    if k >= 2:
                        pe.wait_ge(evac_done, 4 * (k - 1))
                    for o, name, i in ((0, "w1", 0), (1, "w2", 0), (2, "w3", 0), (3, "w3", PAIRS)):
                        for t in range(PAIRS):
                            ins = pe.matmul(psx[:, k % 2, o, 0:CH], mat(name, i + t),
                                            xn[:, t, k * CH:(k + 1) * CH], start=(t == 0), stop=(t == PAIRS - 1))
                    ins.then_inc(conv_done, 1)


def conv_main(nc, cst, x1, x2p, x3_dram, conv_out):
    with ExitStack() as ctx:
        def sb(name, shape, dt=F32):
            return ctx.enter_context(nc.sbuf_tensor(name, shape, dt))

        def psum(name, shape):
            return ctx.enter_context(nc.psum_tensor(name, shape, F32))

        def sem(name):
            return ctx.enter_context(nc.semaphore(name))

        diff = sb("cm_diff", [128, 2, NQ, CH])
        hid = sb("cm_hid", [128, 2, 2, 2, CH])
        lg = sb("cm_lg", [128, 2, STEPS, CH])
        win = sb("cm_win", [128, 2, SP, WIN])
        prod = sb("cm_prod", [128, 2, NQ, CH])
        top = sb("cm_top", [128, CH])
        topb = sb("cm_topb", [128, CH])
        tq = sb("cm_tq", [32, 3, CH])
        dsum = sb("cm_dsum", [128, CH])
        rden = sb("cm_rden", [128, CH])
        cout = sb("cm_cout", [128, 2, CH])
        ps_hid = psum("cm_ps_hid", [128, 2, 2, BANK])
        ps_lg = psum("cm_ps_lg", [128, BANK])
        ps_acc = psum("cm_ps_acc", [128, 2, BANK])
        ps_den = psum("cm_ps_den", [128, BANK])

        sub_done = sem("cm_sub_done")
        relu_done = sem("cm_relu_done")
        hid_done = sem("cm_hid_done")
        hrelu_done = sem("cm_hrelu_done")
        logit_done = sem("cm_logit_done")
        logit_out = sem("cm_logit_out")
        run_done = sem("cm_run_done")
        top_done = sem("cm_top_done")
        shift_done = sem("cm_shift_done")
        exp_done = sem("cm_exp_done")
        win_in = [sem(f"cm_win_in{a}") for a in range(2)]
        prod_done = sem("cm_prod_done")
        acc_done = sem("cm_acc_done")
        acc_out = sem("cm_acc_out")
        den_done = sem("cm_den_done")
        den_out = sem("cm_den_out")
        rden_done = sem("cm_rden_done")
        out_done = sem("cm_out_done")
        out_sent = sem("cm_out_sent")
        out_free = sem("cm_out_free")
        lanes_done = sem("cm_lanes_done")
        TOPS = 10
        SHIFT_D, EXP_D, SUM_D = 2, 3, 4
        HALVES = 2 * STEPS

        def mat(name, n=128):
            a = CONV_COLS[name][0]
            return cst[:, a:a + n]

        def vec(name):
            a = CONV_COLS["vec"][0] + VEC[name]
            return cst[:, a:a + 1]

        def schedule(eng, body):
            body(0, 0, 0)
            body(1, 1, 1)
            with eng.Fori(0, (NCH - 3) // 2) as it:
                body(it * 2 + 2, 0, None)
                body(it * 2 + 3, 1, None)
            body(NCH - 1, (NCH - 1) % 2, NCH - 1)
            body(NCH, NCH % 2, NCH)
            body(NCH + 1, (NCH + 1) % 2, NCH + 1)

        def stage(i, par, known, j, d):
            back, k = divmod(j - d, STEPS)
            if known is not None and not 0 <= known + back < NCH:
                return None
            return i + back, (par + back) % 2, k

        with nc.Block() as block:
            @block.sync
            def _(sp):
                sp.sem_inc(out_free, 1)

                def body(i, par, known):
                    if known is None or known < NCH:
                        if known is None or known >= 2:
                            sp.wait_ge(prod_done, (i - 1) * HALVES)
                        for q in range(NQ):
                            src = bass.AP(tensor=x3_dram.tensor, offset=q + i * (ROWS * WP),
                                          ap=[[SP * STAGE, B * NH], [STAGE, SP], [1, WIN]])
                            sp.dma_start(win[32 * q:32 * q + 32, par, :, :], src).then_inc(win_in[par], 16)
                    if known is None or known >= 2:
                        c = i - 2
                        sp.wait_ge(out_done, c + 1)
                        for r in range(4):
                            dst = bass.AP(tensor=conv_out.tensor, offset=r * PIX + c * CH,
                                          ap=[[C * PIX, B], [SP * PIX, NH], [4 * PIX, 2], [1, CH]])
                            sp.dma_start(dst, cout[32 * r:32 * r + 32, :, :]).then_inc(out_sent, 16)
                        sp.wait_ge(out_sent, (c + 1) * 64)
                        sp.sem_inc(out_free, 1)
                schedule(sp, body)

            @block.gpsimd
            def _(pool):
                for a in range(2):
                    pool.memset(lg[96:128, a, 1::2, :], 0.0).then_inc(lanes_done, 1)

            @block.vector
            def _(v):
                def sub(i, par, j, early):
                    dy, x0, n = taps(j)
                    if not early:
                        v.wait_ge(hid_done, i * HALVES + 2 * (j - 1))
                    a = bass.AP(tensor=x1, offset=i * CH, ap=[[PIX, 128], [0, n], [1, CH]])
                    b = bass.AP(tensor=x2p, offset=i * (ROWS * WP) + dy * WP + x0,
                                ap=[[PADDED, 128], [1, n], [WP, ROWS], [1, W]])
                    v.tensor_tensor(diff[:, j % 2, 0:n, :].rearrange("p n (r c) -> p n r c", c=W),
                                    a.rearrange("p n (r c) -> p n r c", c=W), b, ALU.subtract).then_inc(sub_done, 1)

                def running(c, par, k):
                    n = 32 * taps(k)[2]
                    v.wait_ge(logit_out, c * STEPS + k + 1)
                    if k == 0:
                        v.tensor_copy(top[:, :], lg[:, par, k, :]).then_inc(run_done, 1)
                    else:
                        v.wait_ge(run_done, c * STEPS + k)
                        v.tensor_tensor(top[0:n, :], top[0:n, :], lg[0:n, par, k, :], ALU.max).then_inc(run_done, 1)

                def across(c):
                    def link(k, ins):
                        ins.then_inc(top_done, 1)
                        v.wait_ge(top_done, c * TOPS + k)
                    v.wait_ge(run_done, (c + 1) * STEPS)
                    for q in range(1, NQ):
                        ins = v.tensor_copy(tq[:, q - 1, :], top[32 * q:32 * q + 32, :])
                        if q < NQ - 1:
                            ins.then_inc(top_done, 1)
                    link(3, ins)
                    v.tensor_tensor(tq[:, 0, :], top[0:32, :], tq[:, 0, :], ALU.max).then_inc(top_done, 1)
                    link(5, v.tensor_tensor(tq[:, 1, :], tq[:, 1, :], tq[:, 2, :], ALU.max))
                    link(6, v.tensor_tensor(tq[:, 0, :], tq[:, 0, :], tq[:, 1, :], ALU.max))
                    for q in range(NQ):
                        v.tensor_copy(topb[32 * q:32 * q + 32, :], tq[:, 0, :]).then_inc(top_done, 1)

                def shift(c, par, k):
                    n = 32 * taps(k)[2]
                    if k == 0:
                        v.wait_ge(top_done, (c + 1) * TOPS)
                    v.tensor_tensor(lg[0:n, par, k, :], lg[0:n, par, k, :], topb[0:n, :],
                                    ALU.subtract).then_inc(shift_done, 1)

                def product(c, par, k, known_c):
                    dy, x0, n = taps(k)
                    if known_c == 0 and k == 0:
                        v.wait_ge(lanes_done, 2)
                    if k == 0:
                        v.wait_ge(win_in[par], window_count(c, par, known_c))
                    v.wait_ge(exp_done, c * STEPS + k + 1)
                    for hs in range(2):
                        if not (known_c == 0 and k == 0):
                            v.wait_ge(acc_done, c * HALVES + 2 * k + hs - 1)
                        wv = win[:, par, 4 * hs:4 * hs + 4, dy * WP:(dy + ROWS) * WP] \
                            .rearrange("p s (r c) -> p s r c", c=WP)[:, :, :, x0:x0 + W]
                        ev = lg[:, par, k, :].unsqueeze(1).broadcast_to([128, 4, CH])
                        v.tensor_tensor(prod[:, hs, :, :].rearrange("p s (r c) -> p s r c", c=W), wv,
                                        ev.rearrange("p s (r c) -> p s r c", c=W), ALU.mult).then_inc(prod_done, 1)

                def window_count(c, par, known_c):
                    return 64 * (c // 2 + 1) if known_c is not None else (c - par) * 32 + 64

                def output(c):
                    v.wait_ge(den_out, c + 1)
                    v.reciprocal(rden[:, :], rden[:, :]).then_inc(rden_done, 1)
                    v.wait_ge(rden_done, c + 1)
                    v.tensor_tensor(cout[:, :, :], cout[:, :, :], rden[:, :].unsqueeze(1).broadcast_to([128, 2, CH]),
                                    ALU.mult).then_inc(out_done, 1)

                def body(i, par, known):
                    for j in range(STEPS):
                        at = stage(i, par, known, j, -1)
                        if at:
                            sub(*at, early=(known == 0 and at[2] < 2 and j < 2))
                        at = stage(i, par, known, j, STEPS + SHIFT_D)
                        if at:
                            shift(*at)
                        at = stage(i, par, known, j, 2)
                        if at:
                            running(*at)
                            if j == 1:
                                across(at[0])
                        at = stage(i, par, known, j, STEPS + SUM_D)
                        if at:
                            product(*at, known_c=at[0] if known is not None else None)
                        if j == 6 and (known is None or known >= 2):
                            output(i - 2)

                sub(0, 0, 0, True)
                schedule(v, body)

            @block.scalar
            def _(act):
                def front(i, par, j):
                    n = taps(j)[2]
                    act.wait_ge(sub_done, i * STEPS + j + 1)
                    act.activation(diff[:, j % 2, 0:n, :], diff[:, j % 2, 0:n, :], ACT.Relu).then_inc(relu_done, 1)

                def hidden(i, par, j, known):
                    n = taps(j)[2]
                    for a in range(2):
                        m = min(2, n - 2 * a)
                        act.wait_ge(hid_done, i * HALVES + 2 * j + a + 1)
                        if not (known == 0 and j < 2):
                            act.wait_ge(logit_done, i * STEPS + j - 1)
                        act.activation(hid[:, j % 2, a, 0:m, :], ps_hid[:, a, 0:m, 0:CH], ACT.Relu,
                                       bias=vec("t2")).then_inc(hrelu_done, 1)

                def exponent(c, par, k):
                    n = 32 * taps(k)[2]
                    act.wait_ge(shift_done, c * STEPS + k + 1)
                    act.activation(lg[0:n, par, k, :], lg[0:n, par, k, :], ACT.Exp).then_inc(exp_done, 1)

                def logits(c, par, k, known_c):
                    n = 32 * taps(k)[2]
                    act.wait_ge(logit_done, c * STEPS + k + 1)
                    if known_c is None or known_c >= 2:
                        act.wait_ge(acc_done, (c - 2) * HALVES + 2 * k + 2)
                    act.activation(lg[0:n, par, k, :], ps_lg[0:n, 0:CH], ACT.Identity,
                                   bias=vec("cw2b")[0:n]).then_inc(logit_out, 1)

                def body(i, par, known):
                    for j in range(STEPS):
                        at = stage(i, par, known, j, -1)
                        if at:
                            front(*at)
                        at = stage(i, par, known, j, 0)
                        if at:
                            hidden(*at, known)
                        if j == SUM_D + 1 and (known is None or known >= 2):
                            act.wait_ge(den_done, i - 1)
                            act.copy(rden[:, :], ps_lg[:, 0:CH]).then_inc(den_out, 1)
                        at = stage(i, par, known, j, STEPS + EXP_D)
                        if at:
                            exponent(*at)
                        at = stage(i, par, known, j, 1)
                        if at:
                            logits(*at, known_c=at[0] if known is not None else None)
                        if j == SUM_D - 1 and (known is None or known >= 2):
                            act.wait_ge(acc_done, (i - 1) * HALVES)
                            act.wait_ge(out_free, i - 1)
                            act.copy(dsum[:, :], ps_den[:, 0:CH])
                            act.copy(cout[:, :, :], ps_acc[:, :, 0:CH]).then_inc(acc_out, 1)

                front(0, 0, 0)
                schedule(act, body)

            @block.tensor
            def _(pe):
                def hidden(i, par, j, known):
                    n = taps(j)[2]
                    pe.wait_ge(relu_done, i * STEPS + j + 1)
                    for a in range(2):
                        m = min(2, n - 2 * a)
                        if not (known == 0 and j == 0):
                            pe.wait_ge(hrelu_done, i * HALVES + 2 * j + a - 1)
                        for b in range(m):
                            ins = pe.matmul(ps_hid[:, a, b, 0:CH], mat("cw1"), diff[:, j % 2, 2 * a + b, :],
                                            start=True, stop=True)
                        ins.then_inc(hid_done, 1)

                def logits(c, par, k, known_c, den_chunk):
                    if not (known_c == 0 and k == 0):
                        pe.wait_ge(logit_out, c * STEPS + k)
                    if den_chunk is not None:
                        pe.wait_ge(acc_out, den_chunk + 1)
                        pe.matmul(ps_lg[:, 0:CH], mat("tap_sum_all"), dsum[:, :], start=True,
                                  stop=True).then_inc(den_done, 1)
                        pe.wait_ge(den_out, den_chunk + 1)
                    n = taps(k)[2]
                    for q in range(n):
                        if q % 2 == 0:
                            pe.wait_ge(hrelu_done, c * HALVES + 2 * k + q // 2 + 1)
                        ins = pe.matmul(ps_lg[32 * q:32 * q + 32, 0:CH], mat("cw2", 32), hid[:, k % 2, q // 2, q % 2, :],
                                        start=True, stop=True, tile_position=(0, 32 * q))
                    ins.then_inc(logit_done, 1)

                def sums(c, par, k, known_c):
                    if k == 0 and known_c == 0:
                        pe.wait_ge(lanes_done, 2)
                    if k == 0 and known_c != 0:
                        pe.wait_ge(acc_out, c)
                    r = k % NQ
                    pe.wait_ge(exp_done, c * STEPS + k + 1)
                    pe.matmul(ps_den[32 * r:32 * r + 32, 0:CH], mat("tap_sum", 32), lg[:, par, k, :],
                              start=(k < NQ), stop=(k >= STEPS - NQ), tile_position=(0, 32 * r))
                    for hs in range(2):
                        pe.wait_ge(prod_done, c * HALVES + 2 * k + hs + 1)
                        for r in range(4):
                            ins = pe.matmul(ps_acc[32 * r:32 * r + 32, hs, 0:CH], mat("tap_sum", 32),
                                            prod[:, hs, r, :], start=(k == 0), stop=(k == STEPS - 1),
                                            tile_position=(0, 32 * r))
                        ins.then_inc(acc_done, 1)

                def body(i, par, known):
                    for j in range(STEPS):
                        at = stage(i, par, known, j, 0)
                        if at:
                            hidden(*at, known)
                        den = i - 2 if j == SUM_D + 1 and (known is None or known >= 2) else None
                        at = stage(i, par, known, j, 1)
                        if at:
                            logits(*at, known_c=at[0] if known is not None else None, den_chunk=den)
                        elif den is not None:
                            pe.wait_ge(acc_out, den + 1)
                            pe.matmul(ps_lg[:, 0:CH], mat("tap_sum_all"), dsum[:, :], start=True,
                                      stop=True).then_inc(den_done, 1)
                        at = stage(i, par, known, j, STEPS + SUM_D)
                        if at:
                            sums(*at, known_c=at[0] if known is not None else None)
                schedule(pe, body)


TT = 128
NT = -(-PIX // TT)
LAST = PIX - (NT - 1) * TT
GROUP = 4
NG = -(-NT // GROUP)
E, HID = 8, 256
HT = E * HID // 128
EP = E // 2
NORM = 112
NN = PIX // NORM

TOK_COLS, TOK_N = columns([
    ("ident", 128), ("drop", 128), ("wx", 3 * 128), ("wa", 3 * C), ("den", 1), ("fold", C), ("tvec", 12)])
FFN_COLS, FFN_N = columns([
    ("w1", E * HID), ("w2", HT * C), ("b1", HT), ("b2", EP), ("wg", 2 * E), ("bg", 2 * E), ("rank", 2 * E),
    ("spread", 2 * EP * 128)])
TVEC = {n: i for i, n in enumerate(["keep", "one", "wa", "wb", "wc", "bz", "br", "bf"])}


def columns_of(k):
    return slice(k * CH, (k + 1) * CH) if isinstance(k, int) else bass.ds(k * CH, CH)


def column_of(k):
    return slice(k, k + 1) if isinstance(k, int) else bass.ds(k, 1)


def tile_tokens(n):
    return TT if n < NT - 1 else LAST


def group_tiles(g):
    return range(GROUP * g, min(NT, GROUP * (g + 1)))


def token_norm(nc, tok, tres, xhat, xT, loads, t1_dram):
    with ExitStack() as ctx:
        def sb(name, shape, dt=F32):
            return ctx.enter_context(nc.sbuf_tensor(name, shape, dt))

        def sem(name):
            return ctx.enter_context(nc.semaphore(name))

        tag = "n1_" if loads else "n2_"
        if loads:
            xa = sb(tag + "xa", [128, PAIRS, PIX])
        sq = sb(tag + "sq", [128, NT, 128])
        mean = sb(tag + "mean", [128, PAIRS, 2 * NT])
        var = sb(tag + "var", [128, PAIRS, 2 * NT])
        rstd = sb(tag + "rstd", [128, PAIRS, 2 * NT])
        mhalf = sb(tag + "mhalf", [128, 2 * NT])
        ps_f = ctx.enter_context(nc.psum_tensor(tag + "ps_f", [128, 2, BANK], F32))
        ps_b = ctx.enter_context(nc.psum_tensor(tag + "ps_b", [128, 2, BANK], F32))

        loaded = [sem(tag + f"loaded{t}") for t in range(PAIRS)]
        added = sem(tag + "added")
        turned = sem(tag + "turned")
        turned_out = sem(tag + "turned_out")
        dve = sem(tag + "dve")
        centred = sem(tag + "centred")
        squared = sem(tag + "squared")
        var_done = sem(tag + "var_done")
        rstd_done = sem(tag + "rstd_done")
        normed = sem(tag + "normed")
        back = sem(tag + "back")
        back_out = sem(tag + "back_out")
        sent = sem(tag + "sent")
        ident = tok[:, TOK_COLS["ident"][0]:TOK_COLS["ident"][1]]

        def g_par(t, g):
            return (t * NG + g) % 2

        with nc.Block() as block:
            @block.sync
            def _(sp):
                if loads:
                    x, conv = loads
                    for t in range(PAIRS):
                        sp.dma_start(xa[:, t, :], x[2 * t:2 * t + 2].rearrange("b c h w -> (b c) (h w)")).then_inc(loaded[t], 16)
                        sp.dma_start(tres[:, t, :], conv[2 * t:2 * t + 2].rearrange("b c n -> (b c) n")).then_inc(loaded[t], 16)
                    for t in range(PAIRS):
                        sp.wait_ge(added, t + 1)
                        sp.dma_start(t1_dram[t], tres[:, t, :]).then_inc(sent, 16)
                    sp.wait_ge(sent, 16 * PAIRS)

            @block.gpsimd
            def _(pool):
                for t in range(PAIRS):
                    pool.wait_ge(var_done, t + 1)
                    pool.tensor_tensor(rstd[:, t, :], var[:, t, :], mhalf[:, :], ALU.pow).then_inc(rstd_done, 1)

            @block.tensor
            def _(pe):
                for t in range(PAIRS):
                    if loads:
                        pe.wait_ge(added, t + 1)
                    for g in range(NG):
                        if t * NG + g >= 2:
                            pe.wait_ge(turned_out, t * NG + g - 1)
                        for n in group_tiles(g):
                            m = tile_tokens(n)
                            ins = pe.transpose(ps_f[0:m, g_par(t, g), (n % GROUP) * 128:(n % GROUP) * 128 + 128],
                                               tres[:, t, n * TT:n * TT + m], ident)
                        ins.then_inc(turned, 1)
                for t in range(PAIRS):
                    pe.wait_ge(normed, t + 1)
                    for g in range(NG):
                        if t * NG + g >= 2:
                            pe.wait_ge(back_out, t * NG + g - 1)
                        for n in group_tiles(g):
                            m = tile_tokens(n)
                            ins = pe.transpose(ps_b[:, g_par(t, g), (n % GROUP) * TT:(n % GROUP) * TT + m],
                                               xT[0:m, t, n, :], ident[0:m, 0:m])
                        ins.then_inc(back, 1)

            @block.scalar
            def _(act):
                def forth(t):
                    for g in range(NG):
                        tiles = group_tiles(g)
                        m = tile_tokens(tiles[-1])
                        act.wait_ge(turned, t * NG + g + 1)
                        act.copy(xT[0:m, t, tiles[0]:tiles[-1] + 1, :].rearrange("p n c -> p (n c)"),
                                 ps_f[0:m, g_par(t, g), 0:128 * len(tiles)]).then_inc(turned_out, 1)

                def square(t):
                    act.wait_ge(centred, t + 1)
                    if t > 0:
                        act.wait_ge(var_done, t)
                    act.activation(sq[:, :, :], xT[:, t, :, :], ACT.Square).then_inc(squared, 1)

                def back_again(t):
                    for g in range(NG):
                        tiles = group_tiles(g)
                        n = sum(tile_tokens(a) for a in tiles)
                        act.wait_ge(back, t * NG + g + 1)
                        act.copy(xhat[:, t, tiles[0] * TT:tiles[0] * TT + n],
                                 ps_b[:, g_par(t, g), 0:n]).then_inc(back_out, 1)
                forth(0)
                square(0)
                forth(1)
                square(1)
                back_again(0)
                back_again(1)

            @block.vector
            def _(v):
                n = [0]

                def link(ins):
                    n[0] += 1
                    ins.then_inc(dve, 1)
                    v.wait_ge(dve, n[0])

                v.memset(mhalf[:, :], -0.5)
                for t in range(PAIRS):
                    link(v.memset(xT[LAST:128, t, NT - 1, :], 0.0))
                if loads:
                    for t in range(PAIRS):
                        v.wait_ge(loaded[t], 32)
                        v.tensor_tensor(tres[:, t, :], tres[:, t, :], xa[:, t, :], ALU.add).then_inc(added, 1)
                def rows(t):
                    return xT[:, t, :, :].rearrange("p n (i c) -> p (n i) c", i=2)

                def centre(t):
                    v.wait_ge(turned_out, NG * (t + 1))
                    link(v.tensor_reduce(mean[:, t, :], rows(t), AX.X, ALU.add))
                    link(v.tensor_scalar(mean[:, t, :], mean[:, t, :], 1.0 / C, None, ALU.mult))
                    v.tensor_tensor(rows(t), rows(t), mean[:, t, :].unsqueeze(2).broadcast_to([128, 2 * NT, C]),
                                    ALU.subtract).then_inc(centred, 1)

                def variance(t):
                    v.wait_ge(squared, t + 1)
                    link(v.tensor_reduce(var[:, t, :], sq[:, :, :].rearrange("p n (i c) -> p (n i) c", i=2),
                                         AX.X, ALU.add))
                    v.tensor_scalar(var[:, t, :], var[:, t, :], 1.0 / C, EPS, ALU.mult, ALU.add).then_inc(var_done, 1)

                def normalize(t):
                    v.wait_ge(rstd_done, t + 1)
                    v.wait_ge(squared, t + 1)
                    v.tensor_tensor(rows(t), rows(t), rstd[:, t, :].unsqueeze(2).broadcast_to([128, 2 * NT, C]),
                                    ALU.mult).then_inc(normed, 1)
                centre(0)
                variance(0)
                centre(1)
                normalize(0)
                variance(1)
                normalize(1)


def attention(nc, tok, xhat, xT, xs, vh, vl, wa, attn):
    with ExitStack() as ctx:
        def sb(name, shape, dt=F32):
            return ctx.enter_context(nc.sbuf_tensor(name, shape, dt))

        def psum(name, shape):
            return ctx.enter_context(nc.psum_tensor(name, shape, F32))

        def sem(name):
            return ctx.enter_context(nc.semaphore(name))

        NP = 3
        prob = sb("at_prob", [128, NP, 2, CH])
        prob_last = sb("at_prob_last", [128, CH])
        mpart = sb("at_mpart", [128, NT, NCH])
        mtop = sb("at_mtop", [128, NT])
        mrow = sb("at_mrow", [NT, TT], F16)
        proj = sb("at_proj", [128, 2, 128])
        vbias = sb("at_vbias", [128, 1])
        hi = sb("at_hi", [128, PIX], F16)
        lo = sb("at_lo", [128, PIX], F16)
        ps_s = psum("at_ps_s", [128, 2, 2, BANK])
        ps_m = psum("at_ps_m", [128, 2, BANK])
        ps_a = psum("at_ps_a", [128, 2, BANK])
        SL = (NT + 1) // 2
        LAG = 2

        folded = sem("at_folded")
        ready = sem("at_ready")
        chain = sem("at_chain")
        split = sem("at_split")
        spread = [sem(f"at_spread{t}") for t in range(PAIRS)]
        ones_done = sem("at_ones_done")
        v_done = sem("at_v_done")
        vh_done = sem("at_vh_done")
        vl_done = sem("at_vl_done")
        rough_done = sem("at_rough_done")
        rough_max = sem("at_rough_max")
        pair_done = sem("at_pair_done")
        rough_pairs = sem("at_rough_pairs")
        top_done = sem("at_top_done")
        top_turned = sem("at_top_turned")
        top_half = sem("at_top_half")
        top_in = sem("at_top_in")
        score_done = sem("at_score_done")
        exp_done = sem("at_exp_done")
        sum_done = sem("at_sum_done")
        attn_out = sem("at_attn_out")

        def mat(name, i=0, n=128):
            a = TOK_COLS[name][0] + i * n
            return tok[:, a:a + n]

        def vec(name):
            a = TOK_COLS["tvec"][0] + TVEC[name]
            return tok[:, a:a + 1]

        def tiles(s):
            return range(2 * s, min(NT, 2 * s + 2))

        def rough_banks(s):
            return (ps_m, ps_a, ps_s[:, 1])[s % 3 if s < SL - 1 else (s + 1) % 3]

        def prob_of(s):
            return prob_last[:, :].unsqueeze(1) if s == SL - 1 else prob[:, s % NP, :, :]

        def stages(eng, body, tail):
            assert NCH % 2 == 1
            for b in range(B + 1):
                body(b, 0, b % 2)
                with eng.Fori(0, NCH // 2) as pair:
                    body(b, pair * 2 + 1, (b + 1) % 2)
                    body(b, pair * 2 + 2, b % 2)
                tail(b)

        def after(b, k, per):
            return k * per + b * NCH * per

        PROJECT = {1: 1, 5: 2, 9: 3}

        def unit(b, k):
            return k if b == 0 else k * (B - 1) + NCH + b - 1

        def unit_bank(b, par):
            return ps_s[:, 0, (b + par) % 2, 0:CH]

        with nc.Block() as block:
            @block.sync
            def _(sp):
                for t in range(PAIRS):
                    sp.wait_ge(split, t + 1)
                    for i in range(2):
                        part = slice(64 * i, 64 * i + 64)
                        sp.dma_start(xs[0:64, 2 * t + i, :], hi[part, :]).then_inc(spread[t], 16)
                        sp.dma_start(xs[64:128, 2 * t + i, :], lo[part, :]).then_inc(spread[t], 16)
                for b in range(B):
                    sp.wait_ge(top_half, b + 1)
                    full = (NT - 1) * TT
                    sp.dma_start(vh[127:128, b, 0:full].rearrange("p (n t) -> p n t", t=TT),
                                 mrow[0:NT - 1, :]).then_inc(top_in, 16)
                    sp.dma_start(vh[127:128, b, full:PIX], mrow[NT - 1:NT, 0:LAST]).then_inc(top_in, 16)
                sp.wait_ge(top_in, 32 * B)

            @block.tensor
            def _(pe):
                def project(b, k, par):
                    u = unit(b, k)
                    if b > 0 or k >= 2:
                        pe.wait_ge(vl_done, u - 1)
                    pe.matmul(unit_bank(b, par), proj[:, b % 2, :], xhat[:, b // 2, columns_of(k)],
                              start=True, stop=True).then_inc(v_done, 1)

                def rough_scores(b, k, par, n):
                    if n < NT - 1 and not (b == 1 and isinstance(k, int) and n < 2):
                        pe.wait_ge(rough_max, after(b - 1, k, NT) + n - 1)
                    w = tile_tokens(n)
                    pe.matmul(ps_m[0:w, (n + par) % 2, 0:CH], vh[:, b, n * TT:n * TT + w], xs[:, b, columns_of(k)],
                              start=True, stop=True).then_inc(rough_done, 1)

                def rough_pair(b, k, s):
                    if 3 <= s < SL - 1 or s < 3 and not isinstance(k, int):
                        pe.wait_ge(rough_pairs, after(b, k, SL) + s - (1 if s == 1 else 2))
                    for a, n in enumerate(tiles(s)):
                        if s == SL - 2 and a == 1:
                            pe.wait_ge(rough_pairs, after(b, k, SL) + SL - 2)
                        w = tile_tokens(n)
                        ins = pe.matmul(rough_banks(s)[0:w, a, 0:CH], vh[:, b, n * TT:n * TT + w],
                                        xs[:, b, columns_of(k)], start=True, stop=True)
                    ins.then_inc(pair_done, 1)

                def scores(m, k, par, s):
                    if s < SL - 1 and not (m == 0 and isinstance(k, int) and s < 2):
                        pe.wait_ge(exp_done, after(m, k, SL) + s - 1)
                    for a, n in enumerate(tiles(s)):
                        w = tile_tokens(n)
                        for h, half in enumerate((vh, vl)):
                            ins = pe.matmul(ps_s[0:w, (s + par) % 2, a, 0:CH], xs[:, m, n * TT:n * TT + w],
                                            half[:, m, columns_of(k)], start=(h == 0), stop=(h == 1))
                    ins.then_inc(score_done, 1)

                def sums(m, k, par, s):
                    if s == 0:
                        pe.wait_ge(attn_out, after(m, k, 1))
                    pe.wait_ge(exp_done, after(m, k, SL) + s + 1)
                    for a, n in enumerate(tiles(s)):
                        if s == SL - 1 - LAG and a == 1 and m + 1 < B:
                            pe.wait_ge(rough_max, after(m, k, NT) + NT - 2)
                        i = m % 2
                        ins = pe.matmul(ps_a[64 * a:64 * a + 64, par, 0:CH], xT[:, m // 2, n, 64 * i:64 * i + 64],
                                        prob_of(s)[:, a, :], start=(n < 2), stop=(n >= NT - 2),
                                        tile_position=(0, 64 * a))
                    ins.then_inc(sum_done, 1)

                pe.matmul(ps_s[:, 0, 0, 0:3 * C], mat("drop"), mat("wa", 0, 3 * C), start=True, stop=True)
                pe.matmul(ps_s[:, 0, 1, 0:1], mat("drop"), vec("wb"), start=True, stop=True).then_inc(folded, 1)
                pe.wait_ge(ready, 1)
                for k in range(NCH):
                    project(0, k, k % 2)
                pe.wait_ge(spread[0], 64)
                pe.wait_ge(vh_done, NCH)

                def body(b, k, par):
                    first = isinstance(k, int)
                    if b > 0 and first:
                        pe.wait_ge(top_in, 32 * b)
                    if b == 2 and first:
                        pe.wait_ge(spread[1], 64)
                    for s in range(SL):
                        if b > 0:
                            if s >= LAG:
                                sums(b - 1, k, par, s - LAG)
                            elif not first:
                                sums(b - 1, k - 1, 1 - par, SL - LAG + s)
                            scores(b - 1, k, par, s)
                        elif s in PROJECT:
                            project(PROJECT[s], k, par)
                        if b == 0:
                            rough_pair(b, k, s)
                        elif b < B:
                            for n in tiles(s):
                                rough_scores(b, k, par, n)

                def tail(b):
                    if b > 0:
                        for s in range(SL - LAG, SL):
                            sums(b - 1, NCH - 1, b % 2, s)
                    if b < B:
                        pe.wait_ge(top_done, b + 1)
                        for h in range(2):
                            ins = pe.matmul(ps_m[0:NT, h, CH:BANK], mtop[:, :], mat("ident", h, 64), start=True,
                                            stop=True)
                        ins.then_inc(top_turned, 1)
                stages(pe, body, tail)

            @block.scalar
            def _(act):
                def query_half(b, k, par):
                    u = unit(b, k)
                    act.wait_ge(v_done, u + 1)
                    act.activation(vh[:, b, columns_of(k)], unit_bank(b, par), ACT.Identity,
                                   bias=vbias[:, :]).then_inc(vh_done, 1)

                def body(b, k, par):
                    if b == 0:
                        for a in range(1, B):
                            query_half(a, k, par)
                        return
                    m = b - 1
                    for s in range(SL):
                        act.wait_ge(score_done, after(m, k, SL) + s + 1)
                        if s == SL - 1:
                            act.wait_ge(sum_done, after(m, k, SL))
                        elif s >= NP:
                            act.wait_ge(sum_done, after(m, k, SL) + s - NP + 1)
                        elif not (isinstance(k, int) and m == 0):
                            act.wait_ge(sum_done, after(m, k, SL) + s - NP)
                        a = len(tiles(s))
                        w = tile_tokens(tiles(s)[-1])
                        act.activation(prob_of(s)[0:w, 0:a, :], ps_s[0:w, (s + par) % 2, 0:a, 0:CH],
                                       ACT.Exp).then_inc(exp_done, 1)
                act.wait_ge(ready, 1)
                for k in range(NCH):
                    query_half(0, k, k % 2)
                act.wait_ge(ready, 2)
                stages(act, body, lambda b: None)

            @block.vector
            def _(v):
                n = [0]

                def link(ins):
                    n[0] += 1
                    ins.then_inc(chain, 1)
                    v.wait_ge(chain, n[0])

                def query_rest(b, k, par):
                    v.wait_ge(vh_done, unit(b, k) + 1)
                    v.scalar_tensor_tensor(out=vl[:, b, columns_of(k)], in0=unit_bank(b, par), scalar=vbias[:, :],
                                           in1=vh[:, b, columns_of(k)], op0=ALU.add,
                                           op1=ALU.subtract).then_inc(vl_done, 1)

                def halves(t):
                    if t > 0:
                        v.wait_ge(spread[t - 1], 64)
                    link(v.tensor_scalar(hi[:, :], xhat[:, t, :], vec("keep"), vec("one"), ALU.mult, ALU.add))
                    v.scalar_tensor_tensor(out=lo[:, :], in0=xhat[:, t, :], scalar=vec("keep"), in1=hi[:, :],
                                           op0=ALU.mult, op1=ALU.subtract).then_inc(split, 1)
                    for c in (C - 1, 2 * C - 1):
                        v.memset(xT[:, t, 0:NT - 1, c], 1.0)
                        ins = v.memset(xT[0:LAST, t, NT - 1:NT, c], 1.0)
                    return ins

                link(v.memset(proj[:, :, :], 0.0))
                for i in range(2):
                    part = slice(64 * i, 64 * i + 64)
                    for d in range(2):
                        ins = v.tensor_scalar(proj[part, i, 64 * d:64 * d + 64], mat("drop")[part, 0:64],
                                              vec("wc")[part], None, ALU.mult)
                link(ins)
                for i in range(2):
                    part = slice(64 * i, 64 * i + 64)
                    v.tensor_copy(proj[part, i, 63:64], vec("wa")[part])
                v.wait_ge(folded, 1)
                v.tensor_copy(wa[:, :], ps_s[:, 0, 0, 0:3 * C])
                v.tensor_copy(vbias[:, :], ps_s[:, 0, 1, 0:1]).then_inc(ready, 1)
                halves(0)
                v.memset(prob_last[:, :], 0.0).then_inc(attn_out, 1)
                link(v.memset(mpart[:, NT - 1, :], 0.0))
                halves(1).then_inc(ready, 1)
                for k in range(NCH):
                    query_rest(0, k, k % 2)

                def body(b, k, par):
                    for a in range(NT):
                        if b == 0 and a < SL:
                            c = len(tiles(a))
                            w = tile_tokens(tiles(a)[-1])
                            v.wait_ge(pair_done, after(b, k, SL) + a + 1)
                            v.tensor_reduce(mpart[0:w, 2 * a:2 * a + c, column_of(k)],
                                            rough_banks(a)[0:w, 0:c, 0:CH], AX.X, ALU.max).then_inc(rough_pairs, 1)
                        elif 0 < b < B:
                            w = tile_tokens(a)
                            v.wait_ge(rough_done, after(b - 1, k, NT) + a + 1)
                            v.tensor_reduce(mpart[0:w, a, column_of(k)], ps_m[0:w, (a + par) % 2, 0:CH], AX.X,
                                            ALU.max).then_inc(rough_max, 1)
                        if b == 0 and a - 1 in PROJECT:
                            query_rest(PROJECT[a - 1], k, par)
                        if b > 0 and a == 3 and not isinstance(k, int):
                            block_out(b - 1, k - 1, 1 - par)

                def block_out(m, k, par):
                    v.wait_ge(sum_done, after(m, k, SL) + SL)
                    v.tensor_copy(attn[:, m, columns_of(k)], ps_a[:, par, 0:CH]).then_inc(attn_out, 1)

                def tail(b):
                    if b < B:
                        if b == 0:
                            v.wait_ge(rough_pairs, SL * NCH)
                        else:
                            v.wait_ge(rough_max, NT * NCH * b)
                        v.tensor_reduce(mtop[:, :], mpart[:, :, :], AX.X, ALU.max).then_inc(top_done, 1)
                    if b > 0:
                        block_out(b - 1, NCH - 1, b % 2)
                    if b < B:
                        v.wait_ge(top_turned, b + 1)
                        if b > 0:
                            v.wait_ge(top_in, 32 * b)
                        v.tensor_copy(mrow[:, :].rearrange("n (h c) -> n h c", h=2), ps_m[0:NT, 0:2, CH:BANK]).then_inc(top_half, 1)
                stages(v, body, tail)


def gates(nc, tok, wa, xhat, attn, tres, t1_dram):
    with ExitStack() as ctx:
        def sb(name, shape, dt=F32):
            return ctx.enter_context(nc.sbuf_tensor(name, shape, dt))

        def sem(name):
            return ctx.enter_context(nc.semaphore(name))

        rden = sb("ga_rden", [NORM, B, NN])
        hb = sb("ga_hb", [128, 2])
        g3 = sb("ga_g3", [128, 2, 3, CH])
        ps = ctx.enter_context(nc.psum_tensor("ga_ps", [128, 8, BANK], F32))
        dve = sem("ga_dve")
        in_t = [sem(f"ga_in_t{t}") for t in range(PAIRS)]
        den_done = sem("ga_den_done")
        rden_done = sem("ga_rden_done")
        spread_done = sem("ga_spread_done")
        attn_done = sem("ga_attn_done")
        gate_done = sem("ga_gate_done")
        tanh_done = sem("ga_tanh_done")
        used = sem("ga_used")
        NB = PAIRS * NCH

        def mat(name, i=0, n=128):
            a = TOK_COLS[name][0] + i * n
            return tok[:, a:a + n]

        def vec(name):
            a = TOK_COLS["tvec"][0] + TVEC[name]
            return tok[:, a:a + 1]

        ident = mat("ident")
        with nc.Block() as block:
            @block.sync
            def _(sp):
                for t in range(PAIRS):
                    sp.dma_start(tres[:, t, :], t1_dram[t]).then_inc(in_t[t], 16)

            @block.tensor
            def _(pe):
                for b in range(B):
                    for n in range(NN):
                        ins = pe.matmul(ps[0:NORM, 0, b * NN + n:b * NN + n + 1], attn[:, b, n * NORM:(n + 1) * NORM],
                                        mat("den", 0, 1), start=True, stop=True)
                    ins.then_inc(den_done, 1)
                for b in range(B):
                    pe.wait_ge(rden_done, b + 1)
                    for k in range(NCH):
                        g = b * NCH + k
                        if g >= 2:
                            pe.wait_ge(attn_done, g - 1)
                        for a in range(CH // NORM):
                            n = k * (CH // NORM) + a
                            ins = pe.transpose(ps[:, 6 + g % 2, a * NORM:(a + 1) * NORM],
                                               rden[:, b, n:n + 1].broadcast_to([NORM, 128]), ident[0:NORM, 0:NORM])
                        ins.then_inc(spread_done, 1)
                for g in range(NB):
                    t, k = divmod(g, NCH)
                    at = slice(k * CH, (k + 1) * CH)
                    pe.wait_ge(attn_done, (2 * t + 1) * NCH + k + 1)
                    for j in range(3):
                        if g >= 2:
                            pe.wait_ge(tanh_done, 3 * (g - 2) + j + 1)
                        bank = 3 * (g % 2) + j
                        for i in range(2):
                            pe.matmul(ps[64 * i:64 * i + 64, bank, 0:CH], mat("wx", 2 * j + i, C), xhat[:, t, at],
                                      start=True, stop=False, tile_position=(0, 64 * i))
                        for i in range(2):
                            ins = pe.matmul(ps[64 * i:64 * i + 64, bank, 0:CH], wa[:, j * C:(j + 1) * C],
                                            attn[:, 2 * t + i, at], start=False, stop=True,
                                            tile_position=(0, 64 * i))
                        ins.then_inc(gate_done, 1)

            @block.scalar
            def _(act):
                for g in range(NB):
                    if g >= 2:
                        act.wait_ge(used, g - 1)
                    for j in range(3):
                        act.wait_ge(gate_done, 3 * g + j + 1)
                        if g == 0 and j == 0:
                            act.wait_ge(dve, 1)
                        act.activation(g3[:, g % 2, j, :], ps[:, 3 * (g % 2) + j, 0:CH], ACT.Tanh,
                                       bias=vec("bz") if j == 0 else hb[:, j - 1:j],
                                       scale=1.0 if j == 0 else 0.5).then_inc(tanh_done, 1)

            @block.vector
            def _(v):
                a = TOK_COLS["tvec"][0] + TVEC["br"]
                v.tensor_scalar(hb[:, :], tok[:, a:a + 2], 0.5, None, ALU.mult).then_inc(dve, 1)
                for b in range(B):
                    v.wait_ge(den_done, B)
                    v.reciprocal(rden[:, b, :], ps[0:NORM, 0, b * NN:(b + 1) * NN]).then_inc(rden_done, 1)
                for b in range(B):
                    for k in range(NCH):
                        g = b * NCH + k
                        v.wait_ge(spread_done, g + 1)
                        at = slice(k * CH, (k + 1) * CH)
                        v.tensor_tensor(attn[:, b, at], attn[:, b, at], ps[:, 6 + g % 2, 0:CH],
                                        ALU.mult).then_inc(attn_done, 1)
                n = [1]

                def link(ins):
                    n[0] += 1
                    ins.then_inc(dve, 1)
                    v.wait_ge(dve, n[0])

                for g in range(NB):
                    t, k = divmod(g, NCH)
                    at = slice(k * CH, (k + 1) * CH)
                    z, r, f = (g3[:, g % 2, j, :] for j in range(3))
                    v.wait_ge(in_t[t], 16)
                    v.wait_ge(tanh_done, 3 * (g + 1))
                    v.scalar_tensor_tensor(out=r, in0=r, scalar=1.0, in1=xhat[:, t, at], op0=ALU.add, op1=ALU.mult)
                    link(v.scalar_tensor_tensor(out=f, in0=f, scalar=1.0, in1=z, op0=ALU.add, op1=ALU.mult))
                    link(v.tensor_tensor(r, r, f, ALU.add))
                    v.scalar_tensor_tensor(out=tres[:, t, at], in0=r, scalar=0.5, in1=tres[:, t, at],
                                           op0=ALU.mult, op1=ALU.add).then_inc(used, 1)


def route(nc, tok, ffn, xhat, w1h, w1l, xs, wt):
    with ExitStack() as ctx:
        def sb(name, shape, dt=F32):
            return ctx.enter_context(nc.sbuf_tensor(name, shape, dt))

        def sem(name):
            return ctx.enter_context(nc.semaphore(name))

        hi = sb("ro_hi", [128, PIX], F16)
        lo = sb("ro_lo", [128, PIX], F16)
        R = PAIRS * NT * 2
        lg = sb("ro_lg", [128, R, E])
        eq = sb("ro_eq", [128, R, E])
        one1 = sb("ro_one1", [128, R, E])
        best = sb("ro_best", [128, 4, R])
        ps_g = ctx.enter_context(nc.psum_tensor("ro_ps_g", [128, PAIRS, BANK], F32))
        ps_w = ctx.enter_context(nc.psum_tensor("ro_ps_w", [128, 2, BANK], F32))
        dve = sem("ro_dve")
        split = sem("ro_split")
        spread = sem("ro_spread")
        gate_done = sem("ro_gate_done")
        diff_done = sem("ro_diff_done")
        exp_done = sem("ro_exp_done")
        w_done = sem("ro_w_done")
        w_turned = sem("ro_w_turned")
        w_out = sem("ro_w_out")

        def mat(name, i=0, n=128):
            cols, tile = (FFN_COLS, ffn) if name in FFN_COLS else (TOK_COLS, tok)
            a = cols[name][0] + i * n
            return tile[:, a:a + n]

        with nc.Block() as block:
            @block.sync
            def _(sp):
                for t in range(PAIRS):
                    sp.wait_ge(split, t + 1)
                    for i in range(2):
                        part = slice(64 * i, 64 * i + 64)
                        sp.dma_start(xs[0:64, 2 * t + i, :], hi[part, :]).then_inc(spread, 16)
                        sp.dma_start(xs[64:128, 2 * t + i, :], lo[part, :]).then_inc(spread, 16)
                sp.wait_ge(spread, 128)

            @block.tensor
            def _(pe):
                for t in range(PAIRS):
                    for n in range(NT):
                        w = tile_tokens(n)
                        ins = pe.matmul(ps_g[0:w, t, 16 * n:16 * n + 16], xhat[:, t, n * TT:n * TT + w],
                                        mat("wg", 0, 2 * E), start=True, stop=True)
                ins.then_inc(gate_done, 1)
                pe.wait_ge(w_done, 1)
                for t in range(PAIRS):
                    for g in range(NG):
                        if t * NG + g >= 2:
                            pe.wait_ge(w_out, t * NG + g - 1)
                        for n in group_tiles(g):
                            w = tile_tokens(n)
                            r = (t * NT + n) * 2
                            ins = pe.transpose(ps_w[0:16, (t * NG + g) % 2, n % GROUP * TT:n % GROUP * TT + w],
                                               lg[0:w, r:r + 2, :].rearrange("p r e -> p (r e)"),
                                               mat("ident")[0:w, 0:w])
                        ins.then_inc(w_turned, 1)

            @block.scalar
            def _(act):
                act.wait_ge(diff_done, 1)
                act.activation(best[:, 2, :], best[:, 1, :], ACT.Exp).then_inc(exp_done, 1)

            @block.vector
            def _(v):
                n = [0]

                def link(ins):
                    n[0] += 1
                    ins.then_inc(dve, 1)
                    v.wait_ge(dve, n[0])

                v.memset(wt[:, :, :], 0.0)
                for t in range(PAIRS):
                    if t > 0:
                        v.wait_ge(spread, 64 * t)
                    link(v.tensor_copy(hi[:, :], xhat[:, t, :]))
                    v.tensor_tensor(lo[:, :], xhat[:, t, :], hi[:, :], ALU.subtract).then_inc(split, 1)
                link(v.tensor_copy(w1h[:, :], mat("w1", 0, E * HID)))
                v.tensor_tensor(w1l[:, :], mat("w1", 0, E * HID), w1h[:, :], ALU.subtract)
                v.wait_ge(gate_done, 1)
                link(v.memset(lg[:, :, :], 0.0))
                for t in range(PAIRS):
                    for a, w in ((0, NT - 1), (NT - 1, NT)):
                        p = TT if a == 0 else LAST
                        bg = mat("bg", 0, 2 * E)[0:p].unsqueeze(1).broadcast_to([p, w - a, 2 * E])
                        ins = v.tensor_tensor(lg[0:p, (t * NT + a) * 2:(t * NT + w) * 2, :]
                                              .rearrange("p (n i) e -> p n (i e)", i=2),
                                              ps_g[0:p, t, 16 * a:16 * w].rearrange("p (n c) -> p n c", c=16),
                                              bg, ALU.add)
                link(ins)
                rank = mat("rank", 0, E).unsqueeze(1).broadcast_to([128, R, E])

                def wide(i):
                    return best[:, i, :].unsqueeze(2).broadcast_to([128, R, E])

                def largest(i, out):
                    link(v.tensor_reduce(best[:, i, :], lg[:, :, :], AX.X, ALU.max))
                    link(v.tensor_tensor(eq[:, :, :], lg[:, :, :], wide(i), ALU.is_equal))
                    link(v.tensor_tensor(eq[:, :, :], eq[:, :, :], rank, ALU.mult))
                    link(v.tensor_reduce(best[:, 3, :], eq[:, :, :], AX.X, ALU.max))
                    link(v.tensor_tensor(out, eq[:, :, :], wide(3), ALU.is_equal))

                largest(0, one1[:, :, :])
                link(v.scalar_tensor_tensor(out=lg[:, :, :], in0=one1[:, :, :], scalar=-3.0e38, in1=lg[:, :, :],
                                            op0=ALU.mult, op1=ALU.add))
                largest(1, eq[:, :, :])
                v.tensor_tensor(best[:, 1, :], best[:, 1, :], best[:, 0, :], ALU.subtract).then_inc(diff_done, 1)
                v.wait_ge(exp_done, 1)
                link(v.tensor_scalar(best[:, 3, :], best[:, 2, :], 1.0, None, ALU.add))
                link(v.reciprocal(best[:, 0, :], best[:, 3, :]))
                link(v.tensor_tensor(best[:, 1, :], best[:, 2, :], best[:, 0, :], ALU.mult))
                v.tensor_tensor(one1[:, :, :], one1[:, :, :], wide(0), ALU.mult)
                link(v.tensor_tensor(eq[:, :, :], eq[:, :, :], wide(1), ALU.mult))
                v.tensor_tensor(lg[:, :, :], one1[:, :, :], eq[:, :, :], ALU.add).then_inc(w_done, 1)
                for t in range(PAIRS):
                    for g in range(NG):
                        tiles = group_tiles(g)
                        c = sum(tile_tokens(a) for a in tiles)
                        at = slice(tiles[0] * TT, tiles[0] * TT + c)
                        v.wait_ge(w_turned, t * NG + g + 1)
                        src = ps_w[0:16, (t * NG + g) % 2, 0:c]
                        link(v.tensor_copy(wt[0:16, t, at], src))
                        v.tensor_tensor(wt[32:48, t, at], src, wt[0:16, t, at], ALU.subtract).then_inc(w_out, 1)


def experts(nc, tok, ffn, w1h, w1l, xs, wt, tres, out):
    with ExitStack() as ctx:
        def sb(name, shape, dt=F32):
            return ctx.enter_context(nc.sbuf_tensor(name, shape, dt))

        def psum(name, shape):
            return ctx.enter_context(nc.psum_tensor(name, shape, F32))

        def sem(name):
            return ctx.enter_context(nc.semaphore(name))

        NHB = 8
        hid = sb("ex_hid", [128, NHB, CH])
        wide = sb("ex_wide", [128, 2, CH])
        part = sb("ex_part", [128, EP, CH])
        total = sb("ex_total", [128, 2, CH])
        spread16 = sb("ex_spread16", [128, 2 * EP * 128], F16)
        ps_h = psum("ex_ps_h", [128, 4, BANK])
        ps_o = psum("ex_ps_o", [128, 2, BANK])
        ps_w = psum("ex_ps_w", [128, BANK])
        ps_t = psum("ex_ps_t", [128, BANK])
        cast = sem("ex_cast")
        h_done = sem("ex_h_done")
        gelu_done = sem("ex_gelu_done")
        o_done = sem("ex_o_done")
        wide_done = sem("ex_wide_done")
        wide_out = sem("ex_wide_out")
        part_done = sem("ex_part_done")
        sum_done = sem("ex_sum_done")
        total_done = sem("ex_total_done")
        res_done = sem("ex_res_done")
        sent = sem("ex_sent")

        def mat(name, i=0, n=128):
            cols, tile = (FFN_COLS, ffn) if name in FFN_COLS else (TOK_COLS, tok)
            a = cols[name][0] + i * n
            return tile[:, a:a + n]

        UNITS = B * NCH
        HP2 = HT // EP

        def order(ep):
            return [((2 * ep + a) * 2 + h, a, h) for h in range(2) for a in range(2)]

        def units(eng, body):
            for b in range(B):
                body(b, 0, b * NCH, (b - 1, NCH - 1) if b else None)
                with eng.Fori(0, NCH // 2) as pair:
                    for i in (1, 2):
                        k = pair * 2 + i
                        body(b, k, b * NCH + k, (b, pair * 2 + i - 1))

        with nc.Block() as block:
            @block.tensor
            def _(pe):
                pe.wait_ge(cast, 1)

                def outer(j, u, before):
                    ep = j // HP2
                    n, a, h = order(ep)[j % HP2]
                    if j % HP2 == 0 and (before or ep >= 2):
                        pe.wait_ge(part_done, u * EP + ep - 1)
                    pe.wait_ge(gelu_done, u * HT + j + 1)
                    ins = pe.matmul(ps_o[64 * a:64 * a + 64, ep % 2, 0:CH], mat("w2", n, C), hid[:, j % NHB, :],
                                    start=(h == 0), stop=(h == 1), tile_position=(0, 64 * a))
                    if j % HP2 == HP2 - 1:
                        ins.then_inc(o_done, 1)

                def body(b, k, u, before):
                    def hidden(j):
                        n = order(j // HP2)[j % HP2][0]
                        if before or j >= 4:
                            pe.wait_ge(gelu_done, u * HT + j - 3)
                        for h, w in enumerate((w1h, w1l)):
                            ins = pe.matmul(ps_h[:, j % 4, 0:CH], w[:, n * 128:(n + 1) * 128],
                                            xs[:, b, columns_of(k)], start=(h == 0), stop=(h == 1))
                        ins.then_inc(h_done, 1)

                    def weights(ep):
                        if before or ep >= 1:
                            pe.wait_ge(wide_out, u * EP + ep)
                        s = (b % 2) * EP + ep
                        pe.matmul(ps_w[:, 0:CH], spread16[:, s * 128:(s + 1) * 128], wt[:, b // 2, columns_of(k)],
                                  start=True, stop=True).then_inc(wide_done, 1)

                    for j in range(HT):
                        hidden(j)
                        if j % HP2 == 0:
                            weights(j // HP2)
                        if j >= 2:
                            outer(j - 2, u, before)
                        elif before:
                            outer(HT - 2 + j, u - 1, True)
                        if j == HP2 + 2 and before:
                            fold(before[0], u - 1)

                def fold(b, u):
                    i = b % 2
                    pe.wait_ge(sum_done, u * 3 + 3)
                    pe.matmul(ps_t[64 * i:64 * i + 64, 0:CH], mat("fold", 0, C), total[:, 1, :], start=True,
                              stop=True, tile_position=(0, 64 * i)).then_inc(total_done, 1)
                units(pe, body)
                for j in (HT - 2, HT - 1):
                    outer(j, UNITS - 1, True)
                fold(B - 1, UNITS - 1)

            @block.scalar
            def _(act):
                def body(b, k, u, before):
                    for j in range(HT):
                        n = order(j // HP2)[j % HP2][0]
                        act.wait_ge(h_done, u * HT + j + 1)
                        if j % HP2 == 1:
                            ep = j // HP2
                            act.wait_ge(wide_done, u * EP + ep + 1)
                            if before or ep >= 2:
                                act.wait_ge(part_done, u * EP + ep - 1)
                            act.copy(wide[:, ep % 2, :], ps_w[:, 0:CH]).then_inc(wide_out, 1)
                        if before or j >= NHB:
                            act.wait_ge(o_done, u * EP + j // HP2 - 1)
                        act.activation(hid[:, j % NHB, :], ps_h[:, j % 4, 0:CH], ACT.Gelu,
                                       bias=mat("b1", n, 1)).then_inc(gelu_done, 1)
                units(act, body)

            @block.vector
            def _(v):
                v.tensor_copy(spread16[:, :], mat("spread", 0, 2 * EP * 128)).then_inc(cast, 1)

                def body(b, k, u, before):
                    for ep in range(EP):
                        v.wait_ge(o_done, u * EP + ep + 1)
                        v.wait_ge(wide_out, u * EP + ep + 1)
                        if ep == 1 and before:
                            residual(*before, u - 1)
                        if before:
                            v.wait_ge(sum_done, u * 3)
                        v.scalar_tensor_tensor(out=part[:, ep, :], in0=ps_o[:, ep % 2, 0:CH], scalar=mat("b2", ep, 1),
                                               in1=wide[:, ep % 2, :], op0=ALU.add,
                                               op1=ALU.mult).then_inc(part_done, 1)

                def residual(b, k, u):
                    i = b % 2
                    at = tres[64 * i:64 * i + 64, b // 2, columns_of(k)]
                    v.wait_ge(total_done, u + 1)
                    v.tensor_tensor(at, at, ps_t[64 * i:64 * i + 64, 0:CH], ALU.add).then_inc(res_done, 1)
                units(v, body)
                residual(B - 1, NCH - 1, UNITS - 1)

            @block.gpsimd
            def _(pool):
                def body(b, k, u, before):
                    pool.wait_ge(part_done, u * EP + 2)
                    pool.tensor_tensor(total[:, 0, :], part[:, 0, :], part[:, 1, :], ALU.add).then_inc(sum_done, 1)
                    pool.wait_ge(part_done, u * EP + 3)
                    pool.wait_ge(sum_done, u * 3 + 1)
                    pool.tensor_tensor(total[:, 0, :], total[:, 0, :], part[:, 2, :], ALU.add).then_inc(sum_done, 1)
                    pool.wait_ge(part_done, u * EP + 4)
                    pool.wait_ge(sum_done, u * 3 + 2)
                    if before:
                        pool.wait_ge(total_done, u)
                    pool.tensor_tensor(total[:, 1, :], total[:, 0, :], part[:, 3, :], ALU.add).then_inc(sum_done, 1)
                units(pool, body)

            @block.sync
            def _(sp):
                def body(b, k, u, before):
                    sp.wait_ge(res_done, u + 1)
                    i = b % 2
                    sp.dma_start(bass.AP(tensor=out.tensor, offset=b * C * PIX + k * CH, ap=[[PIX, C], [1, CH]]),
                                 tres[64 * i:64 * i + 64, b // 2, columns_of(k)]).then_inc(sent, 16)
                units(sp, body)
                sp.wait_ge(sent, 16 * UNITS)


def token_constants(w):
    f = np.float32
    tok = np.zeros((128, TOK_N), f)
    ffn = np.zeros((128, FFN_N), f)

    def put(name, a, i=0):
        cols, out = (FFN_COLS, ffn) if name in FFN_COLS else (TOK_COLS, tok)
        at = cols[name][0] + i * a.shape[1]
        out[:a.shape[0], at:at + a.shape[1]] = a

    put("ident", np.eye(128, dtype=f))
    drop = np.eye(C, dtype=f)
    drop[C - 1, :] = -1.0
    drop[C - 1, C - 1] = 0.0
    put("drop", np.tile(drop, (2, 2)))
    for j, n in enumerate(("z", "r", "f")):
        g = w[f"L1_attn_{n}_w"]
        m = np.zeros((2, C, 2, C), f)
        for i in range(2):
            m[i, :, i, :] = g[:, :C].T
        put("wx", m.reshape(128, 128), j)
        put("wa", np.ascontiguousarray(g[:, C:].T), j)
    den = np.zeros((128, 1), f)
    den[C - 1] = den[2 * C - 1] = 1.0
    put("den", den)
    put("fold", np.tile(np.eye(C, dtype=f), (2, 1)))
    put("w1", np.tile(w["L1_ffn_W1"].transpose(1, 0, 2).reshape(C, E * HID), (2, 1)))
    put("w2", w["L1_ffn_W2"].reshape(HT, 128, C).transpose(1, 0, 2).reshape(128, HT * C))
    put("b1", w["L1_ffn_b1"].reshape(HT, 128).T)
    put("b2", w["L1_ffn_b2"].reshape(EP, 2 * C).T)
    m = np.zeros((2, C, 2, E), f)
    for i in range(2):
        m[i, :, i, :] = w["L1_ffn_Wg"]
    put("wg", m.reshape(128, 2 * E))
    put("bg", np.tile(w["L1_ffn_bg"], (128, 2)))
    put("rank", np.tile(np.arange(E, 0, -1, dtype=f), (128, 2)))
    m = np.zeros((128, 2, EP, 2, C), f)
    for i in range(2):
        for e in range(E):
            for half in (0, 32):
                m[half + i * E + e, i, e // 2, e % 2, :] = 1.0
    put("spread", m.reshape(128, 2 * EP * 128))
    v = np.zeros((128, 12), f)
    v[:, TVEC["keep"]] = np.tile(np.arange(C) < C - 1, 2)
    v[:, TVEC["one"]] = np.tile(np.arange(C) == C - 1, 2)
    a = w["L1_attn_att_w"]
    v[:, TVEC["wa"]] = np.tile(a[:C], 2)
    v[:C, TVEC["wb"]] = a[C:2 * C]
    v[:, TVEC["wc"]] = np.tile(a[2 * C:], 2)
    for n in "zrf":
        v[:, TVEC["b" + n]] = np.tile(w[f"L1_attn_{n}_b"], 2)
    put("tvec", v)
    return tok, ffn


def build(nc, x, conv_c, tok_c, ffn_c, out):
    x3_dram = nc.dram_tensor("x3_dram", (B * NH, SP, STAGE), F32).ap()
    conv_out = nc.dram_tensor("conv_out", (B, C, PIX), F32).ap()
    t1_dram = nc.dram_tensor("t1_dram", (PAIRS, 128, PIX), F32).ap()
    m_dram = nc.dram_tensor("m_dram", (B, NT * TT), F16).ap()
    with ExitStack() as ctx:
        def sb(name, shape, dt=F32):
            return ctx.enter_context(nc.sbuf_tensor(name, shape, dt))

        cst = sb("cst", [128, CONV_N])
        x1 = sb("x1", [128, PIX])
        x2p = sb("x2p", [128, PADDED])
        conv_prepare(nc, x, conv_c, cst, x1, x2p, x3_dram)
        conv_main(nc, cst, x1, x2p, x3_dram, conv_out)
    with ExitStack() as whole:
        tok = whole.enter_context(nc.sbuf_tensor("tok", [128, TOK_N], F32))
        xhat = whole.enter_context(nc.sbuf_tensor("xhat", [128, PAIRS, PIX], F32))
        xT = whole.enter_context(nc.sbuf_tensor("xT", [128, PAIRS, NT, 128], F32))
        wa = whole.enter_context(nc.sbuf_tensor("wa", [128, 3 * C], F32))
        load(nc, [(tok, tok_c)])
        tres = whole.enter_context(nc.sbuf_tensor("tres", [128, PAIRS, PIX], F32))
        token_norm(nc, tok, tres, xhat, xT, (x, conv_out), t1_dram)
        with nc.sbuf_tensor("attn", [128, B, PIX], F32) as attn:
            with nc.sbuf_tensor("vh", [128, B, PIX], F16) as vh, nc.sbuf_tensor("vl", [128, B, PIX], F16) as vl:
                xs = tres[:, :, :].rearrange("p t n -> p (t n)").bitcast(F16).rearrange("p (b n) -> p b n", b=B)
                attention(nc, tok, xhat, xT, xs, vh, vl, wa, attn)
            gates(nc, tok, wa, xhat, attn, tres, t1_dram)
        with ExitStack() as ctx:
            ffn = ctx.enter_context(nc.sbuf_tensor("ffn", [128, FFN_N], F32))
            w1h = ctx.enter_context(nc.sbuf_tensor("w1h", [128, E * HID], F16))
            w1l = ctx.enter_context(nc.sbuf_tensor("w1l", [128, E * HID], F16))
            xs = ctx.enter_context(nc.sbuf_tensor("xs2", [128, B, PIX], F16))
            wt = ctx.enter_context(nc.sbuf_tensor("wt", [128, PAIRS, PIX], F16))
            load(nc, [(ffn, ffn_c)])
            token_norm(nc, tok, tres, xhat, xT, None, None)
            route(nc, tok, ffn, xhat, w1h, w1l, xs, wt)
            experts(nc, tok, ffn, w1h, w1l, xs, wt, tres, out)


def load(nc, pairs):
    with nc.semaphore() as arrived, nc.Block() as block:
        @block.sync
        def _(sp):
            for tile, dram in pairs:
                sp.dma_start(tile[:, :], dram).then_inc(arrived, 16)
            sp.wait_ge(arrived, 16 * len(pairs))


def conv_constants(w):
    f = np.float32
    out = np.zeros((128, CONV_N), f)

    def put(name, a, i=0):
        at = CONV_COLS[name][0] + i * a.shape[1]
        out[:, at:at + a.shape[1]] = a

    for name, src in (("w1", w["L0_conv_w1c"]), ("w2", w["L0_conv_w2c"])):
        for t in range(PAIRS):
            m = np.zeros((2, C, B, CR), f)
            for i in range(2):
                m[i, :, 2 * t + i, :] = src.T
            put(name, m.reshape(128, 128), t)
    w3 = w["L0_conv_w3c"].reshape(NH, 2, 4, C)
    for s in range(2):
        for t in range(PAIRS):
            m = np.zeros((2, C, 4, B, NH), f)
            for i in range(2):
                m[i, :, :, 2 * t + i, :] = w3[:, s].transpose(2, 1, 0)
            put("w3", m.reshape(128, 128), s * PAIRS + t)
    m = np.zeros((B, CR, B, CR), f)
    for b in range(B):
        m[b, :, b, :] = w["L0_conv_cw1"]
    put("cw1", m.reshape(128, 128))
    m = np.zeros((B, CR, B, NH), f)
    for b in range(B):
        m[b, :, b, :] = w["L0_conv_cw2"].T
    put("cw2", m.reshape(128, 32))
    eye = np.eye(128, dtype=f)
    put("ident", eye)
    put("pair_mean", np.kron(np.eye(64, dtype=f), np.full((2, 2), 0.5, f)))
    put("tap_sum", np.tile(np.eye(32, dtype=f), (4, 1)))
    put("tap_sum_all", np.tile(np.eye(32, dtype=f), (4, 4)))
    b3 = w["L0_conv_b3c"].reshape(NH, 2, 4)
    rows = {n: np.tile(w["L0_conv_" + s], B) for n, s in
            (("b1", "b1c"), ("b2", "b2c"), ("g1", "bn1_g"), ("t1", "bn1_b"), ("m1", "bn1_m"), ("v1", "bn1_v"),
             ("g2", "bn2_g"), ("t2", "bn2_b"), ("m2", "bn2_m"), ("v2", "bn2_v"))}
    for s, n in enumerate(("b3a", "b3b")):
        rows[n] = np.broadcast_to(b3[:, s].T[:, None, :], (4, B, NH)).reshape(128)
    rows["cw2b"] = np.tile(w["L0_conv_cw2_b"], 16)
    rows["mhalf"] = np.full(128, -0.5, f)
    v = np.zeros((128, 16), f)
    for n, a in rows.items():
        v[:, VEC[n]] = a
    put("vec", v)
    return out


def kernel(**inputs):
    import concourse.bacc as bacc
    from concourse.bass_utils import run_bass_kernel_spmd

    w = {n: np.asarray(a) for n, a in inputs.items()}
    tok_c, ffn_c = token_constants(w)
    arrays = {"x": np.ascontiguousarray(w["x"]), "conv_c": conv_constants(w), "tok_c": tok_c, "ffn_c": ffn_c}
    nc = bacc.Bacc("TRN2", target_bir_lowering=False, num_devices=1)
    args = [nc.dram_tensor(n, a.shape, F32, kind="ExternalInput").ap() for n, a in arrays.items()]
    out = nc.dram_tensor("out", (B, C, H, W), F32, kind="ExternalOutput").ap()
    build(nc, *args, out)
    r = run_bass_kernel_spmd(nc, [arrays], core_ids=[0])
    return r.results[0]["out"]
```

```python
from contextlib import ExitStack

import numpy as np

import concourse.bass as bass
from concourse import mybir

F32 = mybir.dt.float32
F16 = mybir.dt.float16
ALU = mybir.AluOpType
ACT = mybir.ActivationFunctionType
AX = mybir.AxisListType

B, C, H, W = 4, 64, 56, 56
PIX = H * W
PAIRS = B // 2
K, PAD = 7, 3
HP, WP = H + 2 * PAD, W + 2 * PAD
CR = 32
NH, SP = 8, 8
NQ = 4
ROWS = 8
CH = ROWS * W
NCH = H // ROWS
STEPS = 2 * K
WROWS = ROWS + K - 1
WIN = WROWS * WP
PADDED = HP * WP
STAGE = PADDED + 4
BANK = 512
EPS = 1e-5


def taps(j):
    return j // 2, NQ * (j % 2), NQ if j % 2 == 0 else K - NQ


def columns(parts):
    at, out = 0, {}
    for name, n in parts:
        out[name] = (at, at + n)
        at += n
    return out, at


CONV_COLS, CONV_N = columns([
    ("w1", PAIRS * 128), ("w2", PAIRS * 128), ("w3", 2 * PAIRS * 128), ("cw1", 128), ("cw2", 32),
    ("pair_mean", 128), ("tap_sum", 32), ("tap_sum_all", 128), ("ident", 128),
    ("vec", 16)])
VEC = {n: i for i, n in enumerate(
    ["b1", "b2", "b3a", "b3b", "g1", "t1", "m1", "v1", "g2", "t2", "m2", "v2", "cw2b", "mhalf"])}


def conv_prepare(nc, x, consts, tok_c, cst, tok, x1, x2p, x3st, x3_dram, x3_sent):
    with ExitStack() as ctx:
        def sb(name, shape, dt=F32):
            return ctx.enter_context(nc.sbuf_tensor(name, shape, dt))

        def sem(name):
            return ctx.enter_context(nc.semaphore(name))

        xin = sb("cp_xin", [128, PAIRS, PIX])
        xn = sb("cp_xn", [128, PAIRS, PIX])
        stats = sb("cp_stats", [128, PAIRS, NCH, 6])
        mv = sb("cp_mv", [128, PAIRS, 2])
        mom = sb("cp_mom", [128, PAIRS, 2])
        gm = sb("cp_gm", [128, PAIRS, 2])
        var = sb("cp_var", [128, PAIRS])
        rstd = sb("cp_rstd", [128, PAIRS])
        bnv = sb("cp_bnv", [128, 2])
        half = sb("cp_half", [128, 2])
        cwt = sb("cp_cwt", [128, 128])
        tmp = sb("cp_tmp", [128, 4])
        psx = ctx.enter_context(nc.psum_tensor("cp_psx", [128, 2, 4, BANK], F32))

        x_in = [[sem(f"cp_x_in{t}{a}") for a in range(2)] for t in range(PAIRS)]
        c_in = sem("cp_c_in")
        tok_in = sem("cp_tok_in")
        dve = sem("cp_dve")
        moments = sem("cp_moments")
        grouped = sem("cp_grouped")
        var_ready = sem("cp_var_ready")
        rstd_ready = sem("cp_rstd_ready")
        xn_ready = sem("cp_xn_ready")
        bn_ready = sem("cp_bn_ready")
        cw_turned = sem("cp_cw_turned")
        cw_copied = sem("cp_cw_copied")
        conv_done = sem("cp_conv_done")
        evac_done = sem("cp_evac_done")
        padded = sem("cp_padded")

        CUTS = (slice(0, 4 * CH), slice(4 * CH, PIX))

        def vec(name):
            a = CONV_COLS["vec"][0] + VEC[name]
            return cst[:, a:a + 1]

        def mat(name, i=0, n=128):
            a = CONV_COLS[name][0] + i * n
            return cst[:, a:a + n]

        with nc.Block() as block:
            @block.sync
            def _(sp):
                for t in range(PAIRS):
                    src = x[2 * t:2 * t + 2].rearrange("b c h w -> (b c) (h w)")
                    for a, cut in enumerate(CUTS):
                        sp.dma_start(xin[:, t, cut], src[:, cut]).then_inc(x_in[t][a], 16)
                sp.dma_start(tok[:, :], tok_c).then_inc(tok_in, 16)
                sp.wait_ge(padded, 1)
                for b in range(B):
                    dst = bass.AP(tensor=x3_dram.tensor, offset=b * NH * SP * STAGE,
                                  ap=[[STAGE, 4], [SP * STAGE, NH], [4 * STAGE, 2], [1, STAGE]])
                    sp.dma_start(dst, x3st[32 * b:32 * b + 32, :, :]).then_inc(x3_sent, 16)
                sp.wait_ge(tok_in, 16)

            @block.gpsimd
            def _(pool):
                pool.wait_ge(var_ready, 1)
                pool.tensor_tensor(bnv[:, :], bnv[:, :], half[:, :], ALU.pow).then_inc(rstd_ready, 1)
                pool.wait_ge(var_ready, 2)
                pool.tensor_tensor(rstd[:, :], var[:, :], half[:, :], ALU.pow).then_inc(rstd_ready, 1)

            @block.vector
            def _(v):
                n = [0]

                def link(ins):
                    n[0] += 1
                    ins.then_inc(dve, 1)
                    v.wait_ge(dve, n[0])

                v.wait_ge(c_in, 16)
                v.tensor_copy(half[:, 0:1], vec("mhalf"))
                v.tensor_copy(half[:, 1:2], vec("mhalf"))
                v.tensor_scalar(bnv[:, 0:1], vec("v1"), EPS, None, ALU.add)
                v.tensor_scalar(bnv[:, 1:2], vec("v2"), EPS, None, ALU.add).then_inc(var_ready, 1)
                v.wait_ge(rstd_ready, 1)
                link(v.tensor_tensor(tmp[:, 0:1], vec("g1"), bnv[:, 0:1], ALU.mult))
                link(v.tensor_tensor(tmp[:, 1:2], vec("g2"), bnv[:, 1:2], ALU.mult))
                link(v.tensor_tensor(tmp[:, 2:3], vec("b1"), vec("m1"), ALU.subtract))
                link(v.scalar_tensor_tensor(out=tmp[:, 2:3], in0=tmp[:, 2:3], scalar=tmp[:, 0:1],
                                            in1=vec("t1"), op0=ALU.mult, op1=ALU.add))
                link(v.tensor_tensor(tmp[:, 3:4], vec("b2"), tmp[:, 0:1], ALU.mult))
                link(v.tensor_tensor(vec("m2"), vec("m2"), tmp[:, 1:2], ALU.mult))
                link(v.tensor_tensor(vec("t2"), vec("t2"), vec("m2"), ALU.subtract))
                v.tensor_scalar(cwt[:, :], mat("cw1"), tmp[:, 1:2], None, ALU.mult).then_inc(bn_ready, 1)
                v.wait_ge(cw_turned, 1)
                v.tensor_copy(mat("cw1"), psx[:, 1, 0, 0:128]).then_inc(cw_copied, 1)
                for t in range(PAIRS):
                    for k in range(NCH):
                        if k % 4 == 0:
                            v.wait_ge(x_in[t][k // 4], 16)
                        ins = v.bn_stats(stats[:, t, k, :], xin[:, t, k * CH:(k + 1) * CH])
                    link(ins)
                    link(v.bn_aggr(mv[:, t, :], stats[:, t, :, :].rearrange("p k s -> p (k s)")))
                link(v.tensor_tensor(mom[:, :, 0], mv[:, :, 0], mv[:, :, 0], ALU.mult))
                link(v.tensor_tensor(mom[:, :, 1], mom[:, :, 0], mv[:, :, 1], ALU.add))
                v.tensor_copy(mom[:, :, 0], mv[:, :, 0]).then_inc(moments, 1)
                v.wait_ge(grouped, 1)
                link(v.tensor_copy(gm[:, :, :], psx[:, 0, 0, 0:4].rearrange("p (t m) -> p t m", m=2)))
                link(v.tensor_tensor(var[:, :], gm[:, :, 0], gm[:, :, 0], ALU.mult))
                link(v.tensor_tensor(var[:, :], gm[:, :, 1], var[:, :], ALU.subtract))
                v.tensor_scalar(var[:, :], var[:, :], EPS, None, ALU.add).then_inc(var_ready, 1)
                v.wait_ge(rstd_ready, 2)
                for t in range(PAIRS):
                    v.tensor_scalar(xn[:, t, :], xin[:, t, :], gm[:, t, 0:1], rstd[:, t:t + 1],
                                    ALU.subtract, ALU.mult).then_inc(xn_ready, 1)
                v.wait_ge(evac_done, 4 * NCH)
                x3v = x3st[:, :, 0:PADDED].rearrange("p s (r c) -> p s r c", c=WP)
                x2v = x2p[:, :].rearrange("p (r c) -> p r c", c=WP)
                v.memset(x3st[:, :, PADDED:STAGE], 0.0)
                for d in range(PAD):
                    for a, b in ((d, 2 * PAD - d), (WP - 1 - d, WP - 1 - 2 * PAD + d)):
                        v.tensor_copy(x3v[:, :, PAD:PAD + H, a], x3v[:, :, PAD:PAD + H, b])
                        ins = v.tensor_copy(x2v[:, PAD:PAD + H, a], x2v[:, PAD:PAD + H, b])
                link(ins)
                for d in range(PAD):
                    for a, b in ((d, 2 * PAD - d), (HP - 1 - d, HP - 1 - 2 * PAD + d)):
                        ins = v.tensor_copy(x3v[:, :, a, :], x3v[:, :, b, :])
                        v.tensor_copy(x2v[:, a, :], x2v[:, b, :])
                ins.then_inc(padded, 1)

            @block.scalar
            def _(act):
                act.dma_start(cst[:, :], consts).then_inc(c_in, 16)
                act.wait_ge(bn_ready, 1)
                x2v = x2p[:, :].rearrange("p (r c) -> p r c", c=WP)
                for k in range(NCH):
                    act.wait_ge(conv_done, k + 1)
                    ps = psx[:, k % 2, :, 0:CH]
                    rows = slice(PAD + k * ROWS, PAD + (k + 1) * ROWS)
                    act.activation(x1[:, k * CH:(k + 1) * CH], ps[:, 0, :], ACT.Identity,
                                   bias=tmp[:, 2:3], scale=tmp[:, 0:1]).then_inc(evac_done, 1)
                    act.activation(x2v[:, rows, PAD:PAD + W], ps[:, 1, :].rearrange("p (r c) -> p r c", c=W),
                                   ACT.Identity, bias=tmp[:, 3:4], scale=tmp[:, 0:1]).then_inc(evac_done, 1)
                    for s in range(2):
                        x3v = x3st[:, s, 0:PADDED].rearrange("p (r c) -> p r c", c=WP)
                        act.activation(x3v[:, rows, PAD:PAD + W],
                                       ps[:, 2 + s, :].rearrange("p (r c) -> p r c", c=W), ACT.Identity,
                                       bias=vec("b3b" if s else "b3a")).then_inc(evac_done, 1)

            @block.tensor
            def _(pe):
                pe.wait_ge(c_in, 16)
                pe.wait_ge(bn_ready, 1)
                pe.transpose(psx[:, 1, 0, 0:128], cwt[:, :], mat("ident")).then_inc(cw_turned, 1)
                pe.wait_ge(moments, 1)
                pe.matmul(psx[:, 0, 0, 0:4], mat("pair_mean"), mom[:, :, :].rearrange("p t m -> p (t m)"),
                          start=True, stop=True).then_inc(grouped, 1)
                for k in range(NCH):
                    if k == 1:
                        pe.wait_ge(cw_copied, 1)
                    if k >= 2:
                        pe.wait_ge(evac_done, 4 * (k - 1))
                    for o, name, i in ((0, "w1", 0), (1, "w2", 0), (2, "w3", 0), (3, "w3", PAIRS)):
                        for t in range(PAIRS):
                            if k == 0 and o == 0:
                                pe.wait_ge(xn_ready, t + 1)
                            part = slice(64 * t, 64 * t + 64)
                            ins = pe.matmul(psx[part, k % 2, o, 0:CH], mat(name, i + t)[:, part],
                                            xn[:, t, k * CH:(k + 1) * CH], start=True, stop=True,
                                            tile_position=(0, 64 * t))
                    ins.then_inc(conv_done, 1)


def conv_main(nc, x, cst, front, win, x3_dram, x3_sent, conv_out, tres_in, last_in):
    with ExitStack() as ctx:
        def sb(name, shape, dt=F32):
            return ctx.enter_context(nc.sbuf_tensor(name, shape, dt))

        def psum(name, shape):
            return ctx.enter_context(nc.psum_tensor(name, shape, F32))

        def sem(name):
            return ctx.enter_context(nc.semaphore(name))

        diff = sb("cm_diff", [128, 2, NQ, CH])
        hid = sb("cm_hid", [128, 2, 2, 2, CH])
        lg = sb("cm_lg", [128, 2, STEPS, CH])
        prod = sb("cm_prod", [128, 2, NQ, CH])
        top = sb("cm_top", [128, CH])
        topb = sb("cm_topb", [128, CH])
        tq = sb("cm_tq", [32, 3, CH])
        dsum = sb("cm_dsum", [128, CH])
        QCH = CH // NQ
        rden_q = sb("cm_rden_q", [128, QCH])
        rden_d = sb("cm_rden_d", [128, NQ, QCH])
        rden = sb("cm_rden", [128, CH])
        cout = sb("cm_cout", [128, 2, CH])
        ps_hid = psum("cm_ps_hid", [128, 2, 2, BANK])
        ps_lg = psum("cm_ps_lg", [128, BANK])
        ps_acc = psum("cm_ps_acc", [128, 2, BANK])
        ps_den = psum("cm_ps_den", [128, BANK])

        sub_done = sem("cm_sub_done")
        relu_done = sem("cm_relu_done")
        hid_done = sem("cm_hid_done")
        hrelu_done = sem("cm_hrelu_done")
        logit_done = sem("cm_logit_done")
        logit_out = sem("cm_logit_out")
        run_done = sem("cm_run_done")
        top_done = sem("cm_top_done")
        shift_done = sem("cm_shift_done")
        exp_done = sem("cm_exp_done")
        win_in = [sem(f"cm_win_in{a}") for a in range(2)]
        prod_done = sem("cm_prod_done")
        acc_done = sem("cm_acc_done")
        acc_out = sem("cm_acc_out")
        den_done = sem("cm_den_done")
        den_out = sem("cm_den_out")
        rden_done = sem("cm_rden_done")
        rden_placed = sem("cm_rden_placed")
        wide_done = sem("cm_wide_done")
        wide_out = sem("cm_wide_out")
        out_done = sem("cm_out_done")
        out_sent = sem("cm_out_sent")
        out_free = sem("cm_out_free")
        lanes_done = sem("cm_lanes_done")
        gathered = sem("cm_gathered")
        topb_done = sem("cm_topb_done")
        TOPS = 3
        SHIFT_D, EXP_D, SUM_D = 3, 4, 5
        DEN_AT = SUM_D + 1
        HALVES = 2 * STEPS

        def mat(name, n=128):
            a = CONV_COLS[name][0]
            return cst[:, a:a + n]

        def vec(name):
            a = CONV_COLS["vec"][0] + VEC[name]
            return cst[:, a:a + 1]

        def schedule(eng, body):
            body(0, 0, 0)
            body(1, 1, 1)
            with eng.Fori(0, (NCH - 3) // 2) as it:
                body(it * 2 + 2, 0, None)
                body(it * 2 + 3, 1, None)
            body(NCH - 1, (NCH - 1) % 2, NCH - 1)
            body(NCH, NCH % 2, NCH)
            body(NCH + 1, (NCH + 1) % 2, NCH + 1)

        tres, xa = tokens_of_front(front), second_window(win)

        def stage(i, par, known, j, d):
            back, k = divmod(j - d, STEPS)
            if known is not None and not 0 <= known + back < NCH:
                return None
            return i + back, (par + back) % 2, k

        with nc.Block() as block:
            @block.sync
            def _(sp):
                sp.sem_inc(out_free, 1)
                sp.wait_ge(x3_sent, 64)

                def body(i, par, known):
                    if known is None or known < NCH:
                        if known is None or known >= 2:
                            sp.wait_ge(prod_done, (i - 1) * HALVES)
                        for q in range(NQ):
                            src = bass.AP(tensor=x3_dram.tensor, offset=q + i * (ROWS * WP),
                                          ap=[[SP * STAGE, B * NH], [STAGE, SP], [1, WIN]])
                            sp.dma_start(win[32 * q:32 * q + 32, par, :, :], src).then_inc(win_in[par], 16)
                    if known is None or known >= 2:
                        c = i - 2
                        sp.wait_ge(out_done, c + 1)
                        for r in range(4):
                            dst = bass.AP(tensor=conv_out.tensor, offset=r * PIX + c * CH,
                                          ap=[[C * PIX, B], [SP * PIX, NH], [4 * PIX, 2], [1, CH]])
                            sp.dma_start(dst, cout[32 * r:32 * r + 32, :, :]).then_inc(out_sent, 16)
                        sp.wait_ge(out_sent, (c + 1) * 64)
                        sp.sem_inc(out_free, 1)
                    if known == NCH:
                        sp.wait_ge(sub_done, NCH * STEPS)
                        sp.wait_ge(prod_done, (NCH - 1) * HALVES)
                        for t in range(PAIRS):
                            fetch(t, slice(0, PIX - CH), tres_in[t])
                            sp.dma_start(xa[:, t, :], x[2 * t:2 * t + 2].rearrange("b c h w -> (b c) (h w)")) \
                                .then_inc(tres_in[t], 16)

                def fetch(t, cut, arrived):
                    sp.dma_start(tres[:, t, cut], conv_out[2 * t:2 * t + 2].rearrange("b c n -> (b c) n")[:, cut]) \
                        .then_inc(arrived, 16)
                schedule(sp, body)
                for t in range(PAIRS):
                    fetch(t, slice(PIX - CH, PIX), last_in[t])

            @block.gpsimd
            def _(pool):
                pool.memset(rden_d[:, :, :], 0.0).then_inc(lanes_done, 1)
                pool.wait_ge(lanes_done, 1)
                for a in range(2):
                    pool.memset(lg[96:128, a, 1::2, :], 0.0).then_inc(lanes_done, 1)

            @block.vector
            def _(v):
                def sub(i, par, j, early):
                    dy, x0, n = taps(j)
                    if not early:
                        v.wait_ge(hid_done, i * HALVES + 2 * (j - 1))
                    a = bass.AP(tensor=front, offset=i * CH, ap=[[PIX + PADDED, 128], [0, n], [1, CH]])
                    b = bass.AP(tensor=front, offset=i * (ROWS * WP) + PIX + dy * WP + x0,
                                ap=[[PIX + PADDED, 128], [1, n], [WP, ROWS], [1, W]])
                    v.tensor_tensor(diff[:, j % 2, 0:n, :].rearrange("p n (r c) -> p n r c", c=W),
                                    a.rearrange("p n (r c) -> p n r c", c=W), b, ALU.subtract).then_inc(sub_done, 1)

                def running(c, par, k):
                    n = 32 * taps(k)[2]
                    v.wait_ge(logit_out, c * STEPS + k + 1)
                    if k == 0:
                        v.tensor_copy(top[:, :], lg[:, par, k, :]).then_inc(run_done, 1)
                    else:
                        v.wait_ge(run_done, c * STEPS + k)
                        v.tensor_tensor(top[0:n, :], top[0:n, :], lg[0:n, par, k, :], ALU.max).then_inc(run_done, 1)

                def across(c):
                    v.wait_ge(gathered, c + 1)
                    v.tensor_tensor(tq[:, 0, :], top[0:32, :], tq[:, 0, :], ALU.max).then_inc(top_done, 1)
                    v.tensor_tensor(tq[:, 1, :], tq[:, 1, :], tq[:, 2, :], ALU.max).then_inc(top_done, 1)
                    v.wait_ge(top_done, c * TOPS + 2)
                    v.tensor_tensor(tq[:, 0, :], tq[:, 0, :], tq[:, 1, :], ALU.max).then_inc(top_done, 1)

                def shift(c, par, k):
                    n = 32 * taps(k)[2]
                    if k == 0:
                        v.wait_ge(topb_done, c + 1)
                    v.tensor_tensor(lg[0:n, par, k, :], lg[0:n, par, k, :], topb[0:n, :],
                                    ALU.subtract).then_inc(shift_done, 1)

                def product(c, par, k, known_c):
                    dy, x0, _ = taps(k)
                    if known_c == 0 and k == 0:
                        v.wait_ge(lanes_done, 3)
                    if k == 0:
                        v.wait_ge(win_in[par], window_count(c, par, known_c))
                    v.wait_ge(exp_done, c * STEPS + k + 1)
                    for hs in range(2):
                        if not (known_c == 0 and k == 0):
                            v.wait_ge(acc_done, c * HALVES + 2 * k + hs - 1)
                        wv = win[:, par, 4 * hs:4 * hs + 4, dy * WP:(dy + ROWS) * WP] \
                            .rearrange("p s (r c) -> p s r c", c=WP)[:, :, :, x0:x0 + W]
                        ev = lg[:, par, k, :].unsqueeze(1).broadcast_to([128, 4, CH])
                        v.tensor_tensor(prod[:, hs, :, :].rearrange("p s (r c) -> p s r c", c=W), wv,
                                        ev.rearrange("p s (r c) -> p s r c", c=W), ALU.mult).then_inc(prod_done, 1)

                def window_count(c, par, known_c):
                    return 64 * (c // 2 + 1) if known_c is not None else (c - par) * 32 + 64

                def output(c):
                    v.wait_ge(wide_out, c + 1)
                    v.tensor_tensor(cout[:, :, :], cout[:, :, :], rden[:, :].unsqueeze(1).broadcast_to([128, 2, CH]),
                                    ALU.mult).then_inc(out_done, 1)

                def body(i, par, known):
                    for j in range(STEPS):
                        at = stage(i, par, known, j, -1)
                        if at:
                            sub(*at, early=(known == 0 and at[2] < 2 and j < 2))
                        at = stage(i, par, known, j, STEPS + SHIFT_D)
                        if at:
                            shift(*at)
                        at = stage(i, par, known, j, 2)
                        if at:
                            running(*at)
                        back = stage(i, par, known, j, STEPS + SUM_D)
                        if back:
                            product(*back, known_c=back[0] if known is not None else None)
                        if at and j == 1:
                            across(at[0])
                        if j == DEN_AT + 3 and (known is None or known >= 2):
                            output(i - 2)
                        if j == DEN_AT and (known is None or known >= 2):
                            v.wait_ge(den_out, i - 1)
                            v.reciprocal(rden_q[:, :], rden_q[:, :]).then_inc(rden_done, 1)

                sub(0, 0, 0, True)
                schedule(v, body)

            @block.scalar
            def _(act):
                def front(i, par, j):
                    n = taps(j)[2]
                    act.wait_ge(sub_done, i * STEPS + j + 1)
                    act.activation(diff[:, j % 2, 0:n, :], diff[:, j % 2, 0:n, :], ACT.Relu).then_inc(relu_done, 1)

                def hidden(i, par, j, known):
                    n = taps(j)[2]
                    for a in range(2):
                        m = min(2, n - 2 * a)
                        act.wait_ge(hid_done, i * HALVES + 2 * j + a + 1)
                        if not (known == 0 and j < 2):
                            act.wait_ge(logit_done, i * STEPS + j - 1)
                        act.activation(hid[:, j % 2, a, 0:m, :], ps_hid[:, a, 0:m, 0:CH], ACT.Relu,
                                       bias=vec("t2")).then_inc(hrelu_done, 1)

                def exponent(c, par, k):
                    n = 32 * taps(k)[2]
                    act.wait_ge(shift_done, c * STEPS + k + 1)
                    act.activation(lg[0:n, par, k, :], lg[0:n, par, k, :], ACT.Exp).then_inc(exp_done, 1)

                def logits(c, par, k, known_c):
                    n = 32 * taps(k)[2]
                    act.wait_ge(logit_done, c * STEPS + k + 1)
                    if known_c is None or known_c >= 2:
                        act.wait_ge(acc_done, (c - 2) * HALVES + 2 * k + 2)
                    act.activation(lg[0:n, par, k, :], ps_lg[0:n, 0:CH], ACT.Identity,
                                   bias=vec("cw2b")[0:n]).then_inc(logit_out, 1)

                def gather(c):
                    act.wait_ge(run_done, (c + 1) * STEPS)
                    for q in range(1, NQ):
                        ins = act.copy(tq[:, q - 1, :], top[32 * q:32 * q + 32, :])
                    ins.then_inc(gathered, 1)

                def scatter(c):
                    if not (isinstance(c, int) and c == 0):
                        act.wait_ge(shift_done, c * STEPS)
                    act.wait_ge(top_done, (c + 1) * TOPS)
                    for q in range(NQ):
                        ins = act.copy(topb[32 * q:32 * q + 32, :], tq[:, 0, :])
                    ins.then_inc(topb_done, 1)

                def body(i, par, known):
                    for j in range(STEPS):
                        at = stage(i, par, known, j, -1)
                        if at:
                            front(*at)
                        at = stage(i, par, known, j, 0)
                        if at:
                            hidden(*at, known)
                        at = stage(i, par, known, j, 3)
                        if at and j == 2:
                            scatter(at[0])
                        if j == DEN_AT and (known is None or known >= 2):
                            act.wait_ge(den_done, i - 1)
                            act.copy(rden_q[:, :], ps_lg[:, 0:QCH]).then_inc(den_out, 1)
                        if j == DEN_AT + 1 and (known is None or known >= 2):
                            act.wait_ge(rden_done, i - 1)
                            if known == 2:
                                act.wait_ge(lanes_done, 1)
                            for q in range(NQ):
                                part = slice(32 * q, 32 * q + 32)
                                ins = act.copy(rden_d[part, q, :], rden_q[part, :])
                            ins.then_inc(rden_placed, 1)
                        if j == DEN_AT + 2 and (known is None or known >= 2):
                            act.wait_ge(wide_done, i - 1)
                            act.copy(rden[:, :], ps_lg[:, 0:CH]).then_inc(wide_out, 1)
                        at = stage(i, par, known, j, STEPS + EXP_D)
                        if at:
                            exponent(*at)
                        at = stage(i, par, known, j, 1)
                        if at:
                            logits(*at, known_c=at[0] if known is not None else None)
                        at = stage(i, par, known, j, 2)
                        if at and j == 1:
                            gather(at[0])
                        if j == SUM_D - 1 and (known is None or known >= 2):
                            act.wait_ge(acc_done, (i - 1) * HALVES)
                            act.wait_ge(out_free, i - 1)
                            act.copy(dsum[:, :], ps_den[:, 0:CH])
                            act.copy(cout[:, :, :], ps_acc[:, :, 0:CH]).then_inc(acc_out, 1)

                front(0, 0, 0)
                schedule(act, body)

            @block.tensor
            def _(pe):
                def hidden(i, par, j, known):
                    n = taps(j)[2]
                    pe.wait_ge(relu_done, i * STEPS + j + 1)
                    for a in range(2):
                        m = min(2, n - 2 * a)
                        if not (known == 0 and j == 0):
                            pe.wait_ge(hrelu_done, i * HALVES + 2 * j + a - 1)
                        for b in range(m):
                            ins = pe.matmul(ps_hid[:, a, b, 0:CH], mat("cw1"), diff[:, j % 2, 2 * a + b, :],
                                            start=True, stop=True)
                        ins.then_inc(hid_done, 1)

                def denominators(c):
                    pe.wait_ge(acc_out, c + 1)
                    for q in range(NQ):
                        ins = pe.matmul(ps_lg[32 * q:32 * q + 32, 0:QCH], mat("tap_sum", 32),
                                        dsum[:, q * QCH:(q + 1) * QCH], start=True, stop=True,
                                        tile_position=(0, 32 * q))
                    ins.then_inc(den_done, 1)
                    pe.wait_ge(den_out, c + 1)

                def widened(c):
                    pe.wait_ge(rden_placed, c + 1)
                    pe.matmul(ps_lg[:, 0:CH], mat("tap_sum_all"), rden_d[:, :, :].rearrange("p q n -> p (q n)"),
                              start=True, stop=True).then_inc(wide_done, 1)
                    pe.wait_ge(wide_out, c + 1)

                def logits(c, k):
                    n = taps(k)[2]
                    for q in range(n):
                        if q % 2 == 0:
                            pe.wait_ge(hrelu_done, c * HALVES + 2 * k + q // 2 + 1)
                        ins = pe.matmul(ps_lg[32 * q:32 * q + 32, 0:CH], mat("cw2", 32), hid[:, k % 2, q // 2, q % 2, :],
                                        start=True, stop=True, tile_position=(0, 32 * q))
                    ins.then_inc(logit_done, 1)

                def sums(c, par, k, known_c):
                    if k == 0 and known_c == 0:
                        pe.wait_ge(lanes_done, 3)
                    if k == 0 and known_c != 0:
                        pe.wait_ge(acc_out, c)
                    r = k % NQ
                    pe.wait_ge(exp_done, c * STEPS + k + 1)
                    pe.matmul(ps_den[32 * r:32 * r + 32, 0:CH], mat("tap_sum", 32), lg[:, par, k, :],
                              start=(k < NQ), stop=(k >= STEPS - NQ), tile_position=(0, 32 * r))
                    for hs in range(2):
                        pe.wait_ge(prod_done, c * HALVES + 2 * k + hs + 1)
                        for r in range(4):
                            ins = pe.matmul(ps_acc[32 * r:32 * r + 32, hs, 0:CH], mat("tap_sum", 32),
                                            prod[:, hs, r, :], start=(k == 0), stop=(k == STEPS - 1),
                                            tile_position=(0, 32 * r))
                        ins.then_inc(acc_done, 1)

                def body(i, par, known):
                    for j in range(STEPS):
                        at = stage(i, par, known, j, 0)
                        if at:
                            hidden(*at, known)
                        at = stage(i, par, known, j, 1)
                        if at and not (at[2] == 0 and isinstance(at[0], int) and at[0] == 0):
                            pe.wait_ge(logit_out, at[0] * STEPS + at[2])
                        if known is None or known >= 2:
                            if j == DEN_AT:
                                denominators(i - 2)
                            if j == DEN_AT + 2:
                                widened(i - 2)
                        if at:
                            logits(at[0], at[2])
                        at = stage(i, par, known, j, STEPS + SUM_D)
                        if at:
                            sums(*at, known_c=at[0] if known is not None else None)
                schedule(pe, body)


TT = 128
NT = -(-PIX // TT)
LAST = PIX - (NT - 1) * TT
GROUP = 4
NG = -(-NT // GROUP)
E, HID = 8, 256
HT = E * HID // 128
EP = E // 2
BACK = 13
NORM = 112

TOK_COLS, TOK_N = columns([
    ("ident", 128), ("drop", 128), ("wx", 3 * 128), ("wa", 3 * C), ("den", 128), ("fold", C), ("tvec", 12)])
FFN_COLS, FFN_N = columns([
    ("w1", E * HID), ("w2", HT * C), ("b1", HT), ("b2", EP), ("wg", 2 * E), ("bg", 2 * E), ("rank", 2 * E),
    ("spread", 2 * EP * 128)])
TVEC = {n: i for i, n in enumerate(["keep", "one", "wa", "wb", "wc", "bz", "br", "bf"])}


def tokens_of_front(front):
    return front[:, 0:PAIRS * PIX].rearrange("p (t n) -> p t n", t=PAIRS)


def second_window(win):
    return win[:, 1, :, :].rearrange("p s n -> p (s n)")[:, 0:PAIRS * PIX].rearrange("p (t n) -> p t n", t=PAIRS)


def columns_of(k):
    return slice(k * CH, (k + 1) * CH) if isinstance(k, int) else bass.ds(k * CH, CH)


def tile_tokens(n):
    return TT if n < NT - 1 else LAST


def group_tiles(g):
    return range(GROUP * g, min(NT, GROUP * (g + 1)))


def attention(nc, tok, tres, xa, xhat, xT, xs, vh, vl, wa, attn, tres_in, last_in, t1_dram, in_t):
    with ExitStack() as ctx:
        def sb(name, shape, dt=F32):
            return ctx.enter_context(nc.sbuf_tensor(name, shape, dt))

        def psum(name, shape):
            return ctx.enter_context(nc.psum_tensor(name, shape, F32))

        def sem(name):
            return ctx.enter_context(nc.semaphore(name))

        QT = CH // NORM
        RO = QT * NCH
        PER_SLOT = 3
        DEN_AT, TURN_AT, PROJECT_AT = 5, 10, 11
        NP = 3
        prob = sb("at_prob", [128, NP, 2, CH])
        prob_last = sb("at_prob_last", [128, CH])
        mpart = sb("at_mpart", [NORM, QT, NCH])
        mtop = sb("at_mtop", [NORM, QT])
        mrow = sb("at_mrow", [QT, NORM], F16)
        proj = sb("at_proj", [128, 2, 128])
        vbias = sb("at_vbias", [128, 1])
        rden = sb("at_rden", [128, CH])
        mean = sb("at_mean", [128, PAIRS, 2 * NT])
        var = sb("at_var", [128, PAIRS, 2 * NT])
        rstd = sb("at_rstd", [128, PAIRS, 2 * NT])
        mhalf = sb("at_mhalf", [128, 2 * NT])
        flat = attn[:, :, :].rearrange("p b n -> p (b n)")
        sq = [flat[:, t * NT * 128:(t + 1) * NT * 128].rearrange("p (n c) -> p n c", c=128) for t in range(PAIRS)]
        hi = [attn[:, B - PAIRS + t, :].bitcast(F16)[:, 0:PIX] for t in range(PAIRS)]
        lo = [attn[:, B - PAIRS + t, :].bitcast(F16)[:, PIX:2 * PIX] for t in range(PAIRS)]
        ps_s = psum("at_ps_s", [128, 2, 2, BANK])
        ps_m = psum("at_ps_m", [128, 2, BANK])
        ps_a = psum("at_ps_a", [128, 2, BANK])
        SL = (NT + 1) // 2
        LAG = 2

        folded = sem("at_folded")
        added = sem("at_added")
        stored = [sem(f"at_stored{t}") for t in range(PAIRS)]
        turned = sem("at_turned")
        turned_out = sem("at_turned_out")
        centred = sem("at_centred")
        squared = sem("at_squared")
        var_done = sem("at_var_done")
        mhalf_set = sem("at_mhalf_set")
        rstd_done = sem("at_rstd_done")
        normed = sem("at_normed")
        back = sem("at_back")
        back_out = sem("at_back_out")
        hi_done = sem("at_hi_done")
        ready = sem("at_ready")
        chain = sem("at_chain")
        split = sem("at_split")
        spread = [sem(f"at_spread{t}") for t in range(PAIRS)]
        v_done = sem("at_v_done")
        vh_done = sem("at_vh_done")
        vl_done = sem("at_vl_done")
        rough_done = sem("at_rough_done")
        rough_max = sem("at_rough_max")
        top_done = sem("at_top_done")
        top_turned = sem("at_top_turned")
        top_half = sem("at_top_half")
        top_in = sem("at_top_in")
        divided = sem("at_divided")
        score_done = sem("at_score_done")
        exp_done = sem("at_exp_done")
        sum_done = sem("at_sum_done")
        sums_out = sem("at_sums_out")
        den_done = sem("at_den_done")
        attn_out = sem("at_attn_out")

        def mat(name, i=0, n=128):
            a = TOK_COLS[name][0] + i * n
            return tok[:, a:a + n]

        def vec(name):
            a = TOK_COLS["tvec"][0] + TVEC[name]
            return tok[:, a:a + 1]

        def tiles(s):
            return range(2 * s, min(NT, 2 * s + 2))

        def prob_of(s):
            return prob_last[:, :].unsqueeze(1) if s == SL - 1 else prob[:, s % NP, :, :]

        def steps(eng, body):
            assert NCH % 2 == 1
            for b in range(B):
                body(b, 0, b * NCH, b % 2)
                body(b, 1, b * NCH + 1, (b + 1) % 2)
                with eng.Fori(0, (NCH - 3) // 2) as pair:
                    body(b, pair * 2 + 2, pair * 2 + 2 + b * NCH, b % 2)
                    body(b, pair * 2 + 3, pair * 2 + 3 + b * NCH, (b + 1) % 2)
                body(b, NCH - 1, (b + 1) * NCH - 1, b % 2)
            body(B, 0, B * NCH, B % 2)

        def before(b, q, n):
            return (b - 1, NCH + q - n) if isinstance(q, int) and q < n else (b, q - n)

        def first_bank(k):
            return ps_s[:, k % 4 // 2, k % 2, 0:CH]

        with nc.Block() as block:
            @block.sync
            def _(sp):
                for t in range(PAIRS):
                    sp.wait_ge(added, t + 1)
                    sp.dma_start(t1_dram[t], tres[:, t, :]).then_inc(stored[t], 16)
                def stack(t):
                    sp.wait_ge(stored[t], 16)
                    sp.wait_ge(split, t + 1)
                    for i in range(2):
                        part = slice(64 * i, 64 * i + 64)
                        sp.dma_start(xs[0:64, 2 * t + i, :], hi[t][part, :]).then_inc(spread[t], 16)
                        sp.dma_start(xs[64:128, 2 * t + i, :], lo[t][part, :]).then_inc(spread[t], 16)

                def maxima(b, q):
                    sp.wait_ge(top_half, q + (b * NCH + 1))
                    sp.dma_start(vh[127:128, b, columns_of(q)].rearrange("p (a t) -> p a t", t=NORM),
                                 mrow[:, :]).then_inc(top_in, 16)

                stack(0)
                for b in range(B):
                    maxima(b, 0)
                    if b == 0:
                        stack(1)
                    if b == B - 1:
                        sp.wait_ge(score_done, 2 * NCH * SL)
                        sp.dma_start(tres[:, 0, :], t1_dram[0]).then_inc(in_t[0], 16)
                    with sp.Fori(1, NCH) as q:
                        maxima(b, q)
                sp.wait_ge(top_in, 16 * B * NCH)

            @block.gpsimd
            def _(pool):
                pool.memset(mhalf[:, :], -0.5).then_inc(mhalf_set, 1)
                pool.wait_ge(mhalf_set, 1)
                for t in range(PAIRS):
                    pool.wait_ge(var_done, t + 1)
                    pool.tensor_tensor(rstd[:, t, :], var[:, t, :], mhalf[:, :], ALU.pow).then_inc(rstd_done, 1)

            @block.tensor
            def _(pe):
                def turn(t, g):
                    if t * NG + g >= 2:
                        pe.wait_ge(turned_out, t * NG + g - 1)
                    for n in group_tiles(g):
                        w = tile_tokens(n)
                        ins = pe.transpose(ps_m[0:w, (t * NG + g) % 2, (n % GROUP) * 128:(n % GROUP) * 128 + 128],
                                           tres[:, t, n * TT:n * TT + w], mat("ident"))
                    ins.then_inc(turned, 1)

                def turn_back(t, g):
                    if t * NG + g >= 2:
                        pe.wait_ge(back_out, t * NG + g - 1)
                    for n in group_tiles(g):
                        w = tile_tokens(n)
                        ins = pe.transpose(ps_a[:, (t * NG + g) % 2, (n % GROUP) * TT:(n % GROUP) * TT + w],
                                           xT[0:w, t, n, :], mat("ident")[0:w, 0:w])
                    ins.then_inc(back, 1)

                def project(b, k, bank):
                    pe.matmul(bank, proj[:, b % 2, :], xhat[:, b // 2, columns_of(k)],
                              start=True, stop=True).then_inc(v_done, 1)

                def rough_scores(b, q, i, par, e):
                    a, kb = divmod(e, NCH)
                    if e >= 2:
                        pe.wait_ge(rough_max, i * RO + e - 1)
                    elif e == 0 and not (b == 0 and isinstance(q, int) and q == 0):
                        pe.wait_ge(top_half, i)
                    elif e == 1 and before(b, q, 1)[0] in range(B - 1):
                        pe.wait_ge(vl_done, i + NCH)
                    start = q * CH + a * NORM
                    queries = slice(start, start + NORM) if isinstance(q, int) else bass.ds(start, NORM)
                    pe.matmul(ps_m[0:NORM, (e + par) % 2, 0:CH], vh[:, b, queries], xs[:, b, kb * CH:(kb + 1) * CH],
                              start=True, stop=True).then_inc(rough_done, 1)

                def scores(m, k, n, par, s, a):
                    if a == 0 and s < SL - 1 and not (isinstance(n, int) and n == 0 and s < 2):
                        pe.wait_ge(exp_done, n * SL + s - 1)
                    t = tiles(s)[a]
                    w = tile_tokens(t)
                    for h, half in enumerate((vh, vl)):
                        ins = pe.matmul(ps_s[0:w, (s + par) % 2, a, 0:CH], xs[:, m, t * TT:t * TT + w],
                                        half[:, m, columns_of(k)], start=(h == 0), stop=(h == 1))
                    if a == len(tiles(s)) - 1:
                        ins.then_inc(score_done, 1)

                def sums(m, n, par, s, a):
                    if a == 0:
                        if s == 0 and not (isinstance(n, int) and n == 0):
                            pe.wait_ge(attn_out, n)
                        pe.wait_ge(exp_done, n * SL + s + 1)
                    t = tiles(s)[a]
                    i = m % 2
                    ins = pe.matmul(ps_a[64 * a:64 * a + 64, par, 0:CH], xT[:, m // 2, t, 64 * i:64 * i + 64],
                                    prob_of(s)[:, a, :], start=(t < 2), stop=(t >= NT - 2), tile_position=(0, 64 * a))
                    if a == len(tiles(s)) - 1:
                        ins.then_inc(sum_done, 1)

                pe.matmul(ps_s[:, 0, 0, 0:3 * C], mat("drop"), mat("wa", 0, 3 * C), start=True, stop=True)
                pe.matmul(ps_s[:, 0, 1, 0:1], mat("drop"), vec("wb"), start=True, stop=True).then_inc(folded, 1)
                for t in range(PAIRS):
                    pe.wait_ge(added, t + 1)
                    for g in range(NG):
                        turn(t, g)
                pe.wait_ge(ready, 1)
                for t in range(PAIRS):
                    pe.wait_ge(normed, t + 1)
                    for g in range(NG):
                        turn_back(t, g)
                    if t == 0:
                        pe.wait_ge(back_out, NG)
                        for k in range(NCH):
                            if k >= 4:
                                pe.wait_ge(vl_done, k - 3)
                            project(0, k, first_bank(k))
                pe.wait_ge(spread[0], 64)
                pe.wait_ge(vh_done, NCH)

                def denominators(m, k, n, par):
                    pe.wait_ge(sums_out, n + 1)
                    pe.matmul(ps_a[:, par, 0:CH], mat("den"), attn[:, m, columns_of(k)], start=True,
                              stop=True).then_inc(den_done, 1)

                def body(b, q, i, par):
                    step = (b, q) if isinstance(q, int) else None
                    m, k = before(b, q, 1)
                    late = before(b, q, 2)[0]
                    attend = step != (0, 0)
                    if step == (0, 1):
                        pe.wait_ge(vl_done, NCH)
                        pe.wait_ge(back_out, PAIRS * NG)
                    if step == (PAIRS, 0):
                        pe.wait_ge(spread[1], 64)
                    for s in range(SL):
                        rough = [e for e in range(PER_SLOT * s, PER_SLOT * (s + 1)) if e < RO and b < B]
                        for a in range(2):
                            if attend and s >= LAG and a < len(tiles(s - LAG)):
                                sums(m, i - 1, 1 - par, s - LAG, a)
                            elif attend and s < LAG and step != (0, 1) and a < len(tiles(SL - LAG + s)):
                                sums(late, i - 2, par, SL - LAG + s, a)
                            if a == 0 and rough:
                                rough_scores(b, q, i, par, rough[0])
                        for a in range(2):
                            if attend and a < len(tiles(s)):
                                if s == 0 and a == 0:
                                    pe.wait_ge(top_in, i * 16)
                                scores(m, k, i - 1, 1 - par, s, a)
                            if a + 1 < len(rough):
                                rough_scores(b, q, i, par, rough[a + 1])
                        if s == DEN_AT and step not in ((0, 0), (0, 1)):
                            denominators(*before(b, q, 2), i - 2, par)
                        if s == TURN_AT and b < B:
                            pe.wait_ge(top_done, i + 1)
                            pe.transpose(ps_m[0:QT, 1 - par, 0:NORM], mtop[:, :],
                                         mat("ident")[0:NORM, 0:NORM]).then_inc(top_turned, 1)
                        if s == PROJECT_AT and b < B - 1:
                            pe.wait_ge(rough_max, i * RO + RO - 1)
                            project(b + 1, q, ps_m[:, par, 0:CH])

                steps(pe, body)
                for s in range(SL - LAG, SL):
                    for a in range(len(tiles(s))):
                        sums(B - 1, B * NCH - 1, 1 - B % 2, s, a)
                denominators(B - 1, NCH - 1, B * NCH - 1, 1 - B % 2)

            @block.scalar
            def _(act):
                def query_half(b, k, u, bank):
                    act.wait_ge(v_done, u + 1)
                    act.activation(vh[:, b, columns_of(k)], bank, ACT.Identity,
                                   bias=vbias[:, :]).then_inc(vh_done, 1)

                def body(b, q, i, par):
                    step = (b, q) if isinstance(q, int) else None
                    if step == (0, 0):
                        first_half(1)
                    if step == (0, 1):
                        act.wait_ge(ready, 2)
                    for s in range(SL):
                        if step != (0, 0):
                            n = i - 1
                            act.wait_ge(score_done, n * SL + s + 1)
                            if s == SL - 1 and step != (0, 1):
                                act.wait_ge(sum_done, n * SL)
                            elif NP <= s < SL - 1:
                                act.wait_ge(sum_done, n * SL + s - NP + 1)
                            elif s < NP and step != (0, 1):
                                act.wait_ge(sum_done, n * SL + s - NP)
                            a = len(tiles(s))
                            w = tile_tokens(tiles(s)[-1])
                            act.activation(prob_of(s)[0:w, 0:a, :], ps_s[0:w, (s + 1 - par) % 2, 0:a, 0:CH],
                                           ACT.Exp).then_inc(exp_done, 1)
                        if s == PROJECT_AT and b < B - 1:
                            query_half(b + 1, q, i + NCH, ps_m[:, par, 0:CH])

                def turn_out(t, g):
                    tiles = group_tiles(g)
                    w = tile_tokens(tiles[-1])
                    act.wait_ge(turned, t * NG + g + 1)
                    act.copy(xT[0:w, t, tiles[0]:tiles[-1] + 1, :].rearrange("p n c -> p (n c)"),
                             ps_m[0:w, (t * NG + g) % 2, 0:128 * len(tiles)]).then_inc(turned_out, 1)

                def square(t):
                    act.wait_ge(centred, t + 1)
                    act.activation(sq[t], xT[:, t, :, :], ACT.Square).then_inc(squared, 1)

                def turn_back_out(t, g):
                    tiles = group_tiles(g)
                    n = sum(tile_tokens(a) for a in tiles)
                    act.wait_ge(back, t * NG + g + 1)
                    act.copy(xhat[:, t, tiles[0] * TT:tiles[0] * TT + n],
                             ps_a[:, (t * NG + g) % 2, 0:n]).then_inc(back_out, 1)

                def first_half(t):
                    act.wait_ge(back_out, (t + 1) * NG)
                    act.activation(hi[t], xhat[:, t, :], ACT.Identity, bias=vec("one"),
                                   scale=vec("keep")).then_inc(hi_done, 1)

                for g in range(NG):
                    turn_out(0, g)
                for g in range(NG):
                    turn_out(1, g)
                square(0)
                square(1)
                for g in range(NG):
                    turn_back_out(0, g)
                first_half(0)
                act.wait_ge(ready, 1)
                for k in range(NCH):
                    query_half(0, k, k, first_bank(k))
                for g in range(NG):
                    turn_back_out(1, g)
                steps(act, body)

            @block.vector
            def _(v):
                n = [0]

                def link(ins):
                    n[0] += 1
                    ins.then_inc(chain, 1)
                    v.wait_ge(chain, n[0])

                def query_rest(b, k, u, bank):
                    v.wait_ge(vh_done, u + 1)
                    v.scalar_tensor_tensor(out=vl[:, b, columns_of(k)], in0=bank, scalar=vbias[:, :],
                                           in1=vh[:, b, columns_of(k)], op0=ALU.add,
                                           op1=ALU.subtract).then_inc(vl_done, 1)

                def rows(t):
                    return xT[:, t, :, :].rearrange("p n (i c) -> p (n i) c", i=2)

                def add(t):
                    v.wait_ge(tres_in[t], 32)
                    early, late = slice(0, PIX - CH), slice(PIX - CH, PIX)
                    v.tensor_tensor(tres[:, t, early], tres[:, t, early], xa[:, t, early], ALU.add)
                    v.wait_ge(last_in[t], 16)
                    v.tensor_tensor(tres[:, t, late], tres[:, t, late], xa[:, t, late], ALU.add).then_inc(added, 1)

                def means(t):
                    v.wait_ge(turned_out, NG * (t + 1))
                    link(v.tensor_reduce(mean[:, t, :], rows(t), AX.X, ALU.add))
                    link(v.tensor_scalar(mean[:, t, :], mean[:, t, :], 1.0 / C, None, ALU.mult))

                def centre(t):
                    v.tensor_tensor(rows(t), rows(t), mean[:, t, :].unsqueeze(2).broadcast_to([128, 2 * NT, C]),
                                    ALU.subtract).then_inc(centred, 1)

                def variance(t):
                    v.wait_ge(squared, t + 1)
                    link(v.tensor_reduce(var[:, t, :], sq[t].rearrange("p n (i c) -> p (n i) c", i=2), AX.X, ALU.add))
                    v.tensor_scalar(var[:, t, :], var[:, t, :], 1.0 / C, EPS, ALU.mult, ALU.add).then_inc(var_done, 1)

                def normalize(t):
                    v.wait_ge(rstd_done, t + 1)
                    v.tensor_tensor(rows(t), rows(t), rstd[:, t, :].unsqueeze(2).broadcast_to([128, 2 * NT, C]),
                                    ALU.mult).then_inc(normed, 1)

                def second_half(t):
                    v.wait_ge(hi_done, t + 1)
                    v.scalar_tensor_tensor(out=lo[t], in0=xhat[:, t, :], scalar=vec("keep"), in1=hi[t],
                                           op0=ALU.mult, op1=ALU.subtract).then_inc(split, 1)

                def ones(t):
                    v.wait_ge(back, (t + 1) * NG)
                    for c in (C - 1, 2 * C - 1):
                        v.memset(xT[:, t, 0:NT - 1, c], 1.0)
                        ins = v.memset(xT[0:LAST, t, NT - 1:NT, c], 1.0)
                    return ins

                for t in range(PAIRS):
                    link(v.memset(xT[LAST:128, t, NT - 1, :], 0.0))
                v.memset(prob_last[:, :], 0.0).then_inc(attn_out, 1)
                link(v.memset(proj[:, :, :], 0.0))
                for i in range(2):
                    part = slice(64 * i, 64 * i + 64)
                    for d in range(2):
                        ins = v.tensor_scalar(proj[part, i, 64 * d:64 * d + 64], mat("drop")[part, 0:64],
                                              vec("wc")[part], None, ALU.mult)
                link(ins)
                for i in range(2):
                    part = slice(64 * i, 64 * i + 64)
                    v.tensor_copy(proj[part, i, 63:64], vec("wa")[part])
                v.wait_ge(folded, 1)
                v.tensor_copy(wa[:, :], ps_s[:, 0, 0, 0:3 * C])
                v.tensor_copy(vbias[:, :], ps_s[:, 0, 1, 0:1]).then_inc(ready, 1)
                for t in range(PAIRS):
                    add(t)
                means(0)
                centre(0)
                means(1)
                variance(0)
                centre(1)
                variance(1)
                normalize(0)
                normalize(1)
                second_half(0)
                for k in range(NCH):
                    query_rest(0, k, k, first_bank(k))
                ones(0)
                ones(1).then_inc(ready, 1)

                def block_out(m, k, n, par):
                    v.wait_ge(sum_done, n * SL + SL)
                    v.tensor_copy(attn[:, m, columns_of(k)], ps_a[:, par, 0:CH]).then_inc(sums_out, 1)

                def divide(n, par):
                    v.wait_ge(den_done, n + 1)
                    if not (isinstance(n, int) and n == 0):
                        v.wait_ge(divided, n)
                    v.reciprocal(rden[:, :], ps_a[:, par, 0:CH]).then_inc(attn_out, 1)

                def multiply(m, k, n):
                    v.wait_ge(attn_out, n + 2)
                    v.tensor_tensor(attn[:, m, columns_of(k)], attn[:, m, columns_of(k)], rden[:, :],
                                    ALU.mult).then_inc(divided, 1)

                def body(b, q, i, par):
                    step = (b, q) if isinstance(q, int) else None
                    for e in range(RO):
                        if b < B:
                            v.wait_ge(rough_done, i * RO + e + 1)
                            v.tensor_reduce(mpart[:, e // NCH, e % NCH:e % NCH + 1], ps_m[0:NORM, (e + par) % 2, 0:CH],
                                            AX.X, ALU.max).then_inc(rough_max, 1)
                        if e == PER_SLOT * LAG and step not in ((0, 0), (0, 1)):
                            block_out(*before(b, q, 2), i - 2, par)
                        if e == RO // 2 and step == (0, 1):
                            second_half(1)
                    if b < B:
                        v.wait_ge(rough_max, i * RO + RO)
                        v.tensor_reduce(mtop[:, :], mpart[:, :, :], AX.X, ALU.max).then_inc(top_done, 1)
                        v.wait_ge(top_turned, i + 1)
                        if step != (0, 0):
                            v.wait_ge(top_in, i * 16)
                        v.tensor_copy(mrow[:, :], ps_m[0:QT, 1 - par, 0:NORM]).then_inc(top_half, 1)
                    divides = step not in ((0, 0), (0, 1))
                    if divides:
                        divide(i - 2, par)
                    if b < B - 1:
                        query_rest(b + 1, q, i + NCH, ps_m[:, par, 0:CH])
                    if divides:
                        multiply(*before(b, q, 2), i - 2)
                steps(v, body)
                last = (B - 1, NCH - 1, B * NCH - 1)
                block_out(*last, 1 - B % 2)
                divide(last[2], 1 - B % 2)
                multiply(*last)


def gates_and_experts(nc, tok, ffn_c, wa, xhat, xT, attn, tres, in_t, t1_dram, out):
    with ExitStack() as ctx:
        def sb(name, shape, dt=F32):
            return ctx.enter_context(nc.sbuf_tensor(name, shape, dt))

        def sem(name):
            return ctx.enter_context(nc.semaphore(name))

        R = NT * 2
        NHB = 8
        NB = PAIRS * NCH
        UNITS = B * NCH
        HP2 = HT // EP
        ffn = sb("ffn", [128, FFN_N])
        w1h = sb("w1h", [128, E * HID], F16)
        w1l = sb("w1l", [128, E * HID], F16)
        wt = sb("wt", [128, PAIRS, PIX], F16)
        hb = sb("ge_hb", [128, 2])
        mean = sb("ge_mean", [128, R])
        var = sb("ge_var", [128, R])
        rstd = sb("ge_rstd", [128, R])
        mhalf = sb("ge_mhalf", [128, R])
        lg = sb("ge_lg", [128, R, E])
        eq = sb("ge_eq", [128, R, E])
        one1 = sb("ge_one1", [128, R, E])
        best = sb("ge_best", [128, 4, R])
        hid = sb("ge_hid", [128, NHB, CH])
        wide = sb("ge_wide", [128, CH])
        part = sb("ge_part", [128, EP, CH])
        total = sb("ge_total", [128, 2, CH])
        spread16 = sb("ge_spread16", [128, 2 * EP * 128], F16)
        ps = ctx.enter_context(nc.psum_tensor("ge_ps", [128, 8, BANK], F32))

        g3 = hid[:, 0:6, :].rearrange("p (g j) n -> p g j n", j=3)
        own = [attn[:, 2 * t:2 * t + 2, :].rearrange("p b n -> p (b n)") for t in range(PAIRS)]
        sq = [own[t][:, 0:NT * 128].rearrange("p (n c) -> p n c", c=128) for t in range(PAIRS)]
        own16 = [own[t].bitcast(F16).rearrange("p (b n) -> p b n", b=4) for t in range(PAIRS)]
        hi = [own16[t][:, 2, :] for t in range(PAIRS)]
        lo = [own16[t][:, 3, :] for t in range(PAIRS)]

        ps_o, ps_w, ps_t, ps_n = ps[:, 2:4], ps[:, 4], ps[:, 5], ps[:, 6:8]

        def hidden_banks(b):
            return (0, 1) if b == 0 else (0, 1, 6, 7)

        def hidden_bank(b, j):
            return hidden_banks(b)[j % len(hidden_banks(b))]

        ffn_in = sem("ge_ffn_in")
        gate_done = sem("ge_gate_done")
        tanh_done = sem("ge_tanh_done")
        used = sem("ge_used")
        dve = sem("ge_dve")
        wt_zero = sem("ge_wt_zero")
        cast = sem("ge_cast")
        w1l_done = sem("ge_w1l_done")
        turned = sem("ge_turned")
        turned_out = sem("ge_turned_out")
        centred = sem("ge_centred")
        squared = sem("ge_squared")
        var_done = sem("ge_var_done")
        rstd_done = sem("ge_rstd_done")
        normed = sem("ge_normed")
        back = sem("ge_back")
        back_out = sem("ge_back_out")
        hi_done = sem("ge_hi_done")
        split = sem("ge_split")
        stacked = [sem(f"ge_stacked{t}") for t in range(PAIRS)]
        logits_done = sem("ge_logits_done")
        diff_done = sem("ge_diff_done")
        exp_done = sem("ge_exp_done")
        w_done = sem("ge_w_done")
        w_turned = sem("ge_w_turned")
        w_half = sem("ge_w_half")
        w_out = sem("ge_w_out")
        h_done = sem("ge_h_done")
        gelu_done = sem("ge_gelu_done")
        o_done = sem("ge_o_done")
        wide_done = sem("ge_wide_done")
        wide_out = sem("ge_wide_out")
        part_done = sem("ge_part_done")
        sum_done = sem("ge_sum_done")
        total_done = sem("ge_total_done")
        res_done = sem("ge_res_done")
        sent = sem("ge_sent")

        def mat(name, i=0, n=128):
            cols, tile = (FFN_COLS, ffn) if name in FFN_COLS else (TOK_COLS, tok)
            a = cols[name][0] + i * n
            return tile[:, a:a + n]

        def vec(name):
            a = TOK_COLS["tvec"][0] + TVEC[name]
            return tok[:, a:a + 1]

        def rows(t):
            return xT[:, t, :, :].rearrange("p n (i c) -> p (n i) c", i=2)

        def tokens_of(g):
            tiles = group_tiles(g)
            return tiles[0] * TT, sum(tile_tokens(n) for n in tiles)

        def order(ep):
            return [((2 * ep + a) * 2 + h, a, h) for h in range(2) for a in range(2)]

        def units(eng, body):
            for k in range(NCH):
                body(0, k, k, (0, k - 1) if k else None)
            for b in range(1, B):
                body(b, 0, b * NCH, (b - 1, NCH - 1))
                with eng.Fori(0, NCH // 2) as pair:
                    for i in (1, 2):
                        k = pair * 2 + i
                        body(b, k, b * NCH + k, (b, pair * 2 + i - 1))

        with nc.Block() as block:
            @block.sync
            def _(sp):
                sp.dma_start(ffn[:, :], ffn_c).then_inc(ffn_in, 16)
                sp.dma_start(tres[:, 1, :], t1_dram[1]).then_inc(in_t[1], 16)
                for t in range(PAIRS):
                    sp.wait_ge(split, t + 1)
                    for i in range(2):
                        part_i = slice(64 * i, 64 * i + 64)
                        sp.dma_start(own16[t][0:64, i, :], hi[t][part_i, :]).then_inc(stacked[t], 16)
                        sp.dma_start(own16[t][64:128, i, :], lo[t][part_i, :]).then_inc(stacked[t], 16)

                def body(b, k, u, before):
                    sp.wait_ge(res_done, u + 1)
                    i = b % 2
                    sp.dma_start(bass.AP(tensor=out.tensor, offset=b * C * PIX + k * CH, ap=[[PIX, C], [1, CH]]),
                                 tres[64 * i:64 * i + 64, b // 2, columns_of(k)]).then_inc(sent, 16)
                units(sp, body)
                sp.wait_ge(sent, 16 * UNITS)

            @block.tensor
            def _(pe):
                def gate(t, k, j):
                    n = (t * NCH + k) * 3 + j
                    at = columns_of(k)
                    if n >= 4:
                        pe.wait_ge(tanh_done, n - 3)
                    for i in range(2):
                        pe.matmul(ps[64 * i:64 * i + 64, n % 4, 0:CH], mat("wx", 2 * j + i, C), xhat[:, t, at],
                                  start=True, stop=False, tile_position=(0, 64 * i))
                    for i in range(2):
                        ins = pe.matmul(ps[64 * i:64 * i + 64, n % 4, 0:CH], wa[:, j * C:(j + 1) * C],
                                        attn[:, 2 * t + i, at], start=False, stop=True, tile_position=(0, 64 * i))
                    ins.then_inc(gate_done, 1)

                def turn(t, g):
                    at, n = tokens_of(g)
                    pe.wait_ge(used, t * NCH + min(NCH, -(-(at + n) // CH)))
                    if g >= 2:
                        pe.wait_ge(turned_out, t * NG + g - 1)
                    elif t > 0:
                        pe.wait_ge(w_out, t * NG)
                    for n in group_tiles(g):
                        w = tile_tokens(n)
                        ins = pe.transpose(ps_n[0:w, g % 2, (n % GROUP) * 128:(n % GROUP) * 128 + 128],
                                           tres[:, t, n * TT:n * TT + w], mat("ident"))
                    ins.then_inc(turned, 1)

                def turn_back(t, g):
                    pe.wait_ge(normed, t + 1)
                    if g >= 2:
                        pe.wait_ge(back_out, t * NG + g - 1)
                    for n in group_tiles(g):
                        w = tile_tokens(n)
                        ins = pe.transpose(ps_n[:, g % 2, (n % GROUP) * TT:(n % GROUP) * TT + w],
                                           xT[0:w, t, n, :], mat("ident")[0:w, 0:w])
                    ins.then_inc(back, 1)

                def logits(t):
                    pe.wait_ge(back_out, (t + 1) * NG)
                    for n in range(NT):
                        w = tile_tokens(n)
                        ins = pe.matmul(ps_n[0:w, 1, 16 * n:16 * n + 16], xhat[:, t, n * TT:n * TT + w],
                                        mat("wg", 0, 2 * E), start=True, stop=True)
                    ins.then_inc(logits_done, 1)

                def turn_weights(t, g):
                    pe.wait_ge(w_done, t + 1)
                    if g >= 2:
                        pe.wait_ge(w_out, t * NG + g - 1)
                    for n in group_tiles(g):
                        w = tile_tokens(n)
                        ins = pe.transpose(ps_n[0:16, g % 2, n % GROUP * TT:n % GROUP * TT + w],
                                           lg[0:w, 2 * n:2 * n + 2, :].rearrange("p r e -> p (r e)"),
                                           mat("ident")[0:w, 0:w])
                    ins.then_inc(w_turned, 1)

                for k in range(NCH):
                    for j in range(3):
                        gate(0, k, j)
                    if k >= 2:
                        turn(0, k - 2)
                for i in range(3 * NCH):
                    gate(1, i // 3, i % 3)
                    if i < 2:
                        turn(0, NG - 2 + i)
                    if BACK <= i < BACK + NG:
                        turn_back(0, i - BACK)
                pe.wait_ge(ffn_in, 16)
                logits(0)
                for g in range(NG):
                    turn_weights(0, g)

                def aside(k, j):
                    if k == 0 and j % 2 == 0 and j // 2 < NG:
                        turn(1, j // 2)
                    if k == 3 and j % 2 == 0 and j // 2 < NG:
                        turn_back(1, j // 2)
                    if (k, j) == (4, 0):
                        logits(1)
                    for at, groups in (((5, 10), (0, 1)), ((6, 0), (2, 3)), ((6, 6), (4, 5)), ((6, 10), (6,))):
                        if (k, j) == at:
                            for g in groups:
                                turn_weights(1, g)

                def outer(j, u, before):
                    ep = j // HP2
                    n, a, h = order(ep)[j % HP2]
                    if j % HP2 == 0 and (before or ep >= 2):
                        pe.wait_ge(part_done, u * EP + ep - 1)
                    pe.wait_ge(gelu_done, u * HT + j + 1)
                    ins = pe.matmul(ps_o[64 * a:64 * a + 64, ep % 2, 0:CH], mat("w2", n, C), hid[:, j % NHB, :],
                                    start=(h == 0), stop=(h == 1), tile_position=(0, 64 * a))
                    if j % HP2 == HP2 - 1:
                        ins.then_inc(o_done, 1)

                def body(b, k, u, before):
                    def hidden(j):
                        n = order(j // HP2)[j % HP2][0]
                        behind = len(hidden_banks(b))
                        if b == 1 and isinstance(k, int) and j < 4:
                            behind = 2
                        if before or j >= behind:
                            pe.wait_ge(gelu_done, u * HT + j - behind + 1)
                        for h, w in enumerate((w1h, w1l)):
                            ins = pe.matmul(ps[:, hidden_bank(b, j), 0:CH], w[:, n * 128:(n + 1) * 128],
                                            own16[b // 2][:, b % 2, columns_of(k)], start=(h == 0), stop=(h == 1))
                        ins.then_inc(h_done, 1)

                    def weights(ep):
                        if before or ep >= 1:
                            pe.wait_ge(wide_out, u * EP + ep)
                        s = (b % 2) * EP + ep
                        pe.matmul(ps_w[:, 0:CH], spread16[:, s * 128:(s + 1) * 128], wt[:, b // 2, columns_of(k)],
                                  start=True, stop=True).then_inc(wide_done, 1)

                    if b % 2 == 0 and isinstance(k, int) and k == 0:
                        pe.wait_ge(stacked[b // 2], 64)
                    if b < 2 and isinstance(k, int) and k == 0:
                        pe.wait_ge(w_out, (b + 1) * NG)
                    for j in range(HT):
                        hidden(j)
                        if j % HP2 == HP2 - 1:
                            weights(j // HP2)
                        if j >= 2:
                            outer(j - 2, u, before)
                        elif before:
                            outer(HT - 2 + j, u - 1, True)
                        if j == HP2 + 2 and before:
                            fold(before[0], u - 1)
                        if b == 0:
                            aside(k, j)

                def fold(b, u):
                    i = b % 2
                    pe.wait_ge(sum_done, u * 3 + 3)
                    pe.matmul(ps_t[64 * i:64 * i + 64, 0:CH], mat("fold", 0, C), total[:, 1, :], start=True,
                              stop=True, tile_position=(0, 64 * i)).then_inc(total_done, 1)

                pe.wait_ge(cast, 2)
                pe.wait_ge(w1l_done, 1)
                pe.wait_ge(tanh_done, 3 * NB)
                units(pe, body)
                for j in (HT - 2, HT - 1):
                    outer(j, UNITS - 1, True)
                fold(B - 1, UNITS - 1)

            @block.scalar
            def _(act):
                def tanh(t, k, j):
                    g = t * NCH + k
                    act.wait_ge(gate_done, 3 * g + j + 1)
                    if j == 0 and g >= 2:
                        act.wait_ge(used, g - 1)
                    act.activation(g3[:, g % 2, j, :], ps[:, (3 * g + j) % 4, 0:CH], ACT.Tanh,
                                   bias=vec("bz") if j == 0 else hb[:, j - 1:j],
                                   scale=1.0 if j == 0 else 0.5).then_inc(tanh_done, 1)

                def turn_out(t, g):
                    tiles = group_tiles(g)
                    w = tile_tokens(tiles[-1])
                    act.wait_ge(turned, t * NG + g + 1)
                    act.copy(xT[0:w, t, tiles[0]:tiles[-1] + 1, :].rearrange("p n c -> p (n c)"),
                             ps_n[0:w, g % 2, 0:128 * len(tiles)]).then_inc(turned_out, 1)

                def square(t):
                    act.wait_ge(centred, t + 1)
                    act.activation(sq[t], xT[:, t, :, :], ACT.Square).then_inc(squared, 1)

                def turn_back_out(t, g):
                    at, n = tokens_of(g)
                    act.wait_ge(back, t * NG + g + 1)
                    act.copy(xhat[:, t, at:at + n], ps_n[:, g % 2, 0:n]).then_inc(back_out, 1)

                def first_half(t):
                    act.wait_ge(back_out, (t + 1) * NG)
                    act.copy(hi[t], xhat[:, t, :]).then_inc(hi_done, 1)

                def weight_exp(t):
                    act.wait_ge(diff_done, t + 1)
                    act.activation(best[:, 2, :], best[:, 1, :], ACT.Exp).then_inc(exp_done, 1)

                def weights_half(t, g):
                    at, n = tokens_of(g)
                    act.wait_ge(w_turned, t * NG + g + 1)
                    act.copy(wt[0:16, t, at:at + n], ps_n[0:16, g % 2, 0:n]).then_inc(w_half, 1)

                act.wait_ge(ffn_in, 16)
                act.copy(w1h[:, :], mat("w1", 0, E * HID)).then_inc(cast, 1)
                act.copy(spread16[:, :], mat("spread", 0, 2 * EP * 128)).then_inc(cast, 1)
                act.wait_ge(dve, 1)
                for k in range(NCH):
                    for j in range(3):
                        tanh(0, k, j)
                    if k >= 2:
                        turn_out(0, k - 2)
                for i in range(3 * NCH):
                    tanh(1, i // 3, i % 3)
                    if i < 2:
                        turn_out(0, NG - 2 + i)
                    if i == 5:
                        square(0)
                    if BACK <= i < BACK + NG:
                        turn_back_out(0, i - BACK)
                first_half(0)
                weight_exp(0)
                act.wait_ge(wt_zero, 1)
                for g in range(NG):
                    weights_half(0, g)

                def aside(k, j):
                    if k == 0 and j % 2 == 1 and j // 2 < NG:
                        turn_out(1, j // 2)
                    if (k, j) == (1, 11):
                        square(1)
                    if k == 3 and j % 2 == 1 and j // 2 < NG:
                        turn_back_out(1, j // 2)
                    if (k, j) == (4, 1):
                        first_half(1)
                    if (k, j) == (5, 3):
                        weight_exp(1)
                    for at, groups in (((5, 11), (0, 1)), ((6, 1), (2, 3)), ((6, 7), (4, 5)), ((6, 11), (6,))):
                        if (k, j) == at:
                            for g in groups:
                                weights_half(1, g)

                def body(b, k, u, before):
                    for j in range(HT):
                        n = order(j // HP2)[j % HP2][0]
                        act.wait_ge(h_done, u * HT + j + 1)
                        if before or j >= NHB:
                            act.wait_ge(o_done, u * EP + j // HP2 - 1)
                        act.activation(hid[:, j % NHB, :], ps[:, hidden_bank(b, j), 0:CH], ACT.Gelu,
                                       bias=mat("b1", n, 1)).then_inc(gelu_done, 1)
                        if b == 0:
                            aside(k, j)
                act.wait_ge(used, NB)
                units(act, body)

            @block.vector
            def _(v):
                n_dve = [0]

                def link(ins):
                    n_dve[0] += 1
                    ins.then_inc(dve, 1)
                    v.wait_ge(dve, n_dve[0])

                def residual_of_gates(t, k):
                    g = t * NCH + k
                    at = columns_of(k)
                    z, r, f = (g3[:, g % 2, j, :] for j in range(3))
                    v.wait_ge(in_t[t], 16)
                    v.wait_ge(tanh_done, 3 * (g + 1))
                    v.scalar_tensor_tensor(out=r, in0=r, scalar=1.0, in1=xhat[:, t, at], op0=ALU.add, op1=ALU.mult)
                    link(v.scalar_tensor_tensor(out=f, in0=f, scalar=1.0, in1=z, op0=ALU.add, op1=ALU.mult))
                    link(v.tensor_tensor(r, r, f, ALU.add))
                    v.scalar_tensor_tensor(out=tres[:, t, at], in0=r, scalar=0.5, in1=tres[:, t, at],
                                           op0=ALU.mult, op1=ALU.add).then_inc(used, 1)

                def means(t):
                    v.wait_ge(turned_out, NG * (t + 1))
                    link(v.tensor_reduce(mean[:, :], rows(t), AX.X, ALU.add))
                    link(v.tensor_scalar(mean[:, :], mean[:, :], 1.0 / C, None, ALU.mult))

                def centre(t):
                    v.tensor_tensor(rows(t), rows(t), mean[:, :].unsqueeze(2).broadcast_to([128, R, C]),
                                    ALU.subtract).then_inc(centred, 1)

                def variance(t):
                    v.wait_ge(squared, t + 1)
                    link(v.tensor_reduce(var[:, :], sq[t].rearrange("p n (i c) -> p (n i) c", i=2), AX.X, ALU.add))
                    v.tensor_scalar(var[:, :], var[:, :], 1.0 / C, EPS, ALU.mult, ALU.add).then_inc(var_done, 1)

                def normalize(t):
                    v.wait_ge(rstd_done, t + 1)
                    v.tensor_tensor(rows(t), rows(t), rstd[:, :].unsqueeze(2).broadcast_to([128, R, C]),
                                    ALU.mult).then_inc(normed, 1)

                def second_half(t):
                    v.wait_ge(hi_done, t + 1)
                    v.tensor_tensor(lo[t], xhat[:, t, :], hi[t], ALU.subtract).then_inc(split, 1)

                def biased(t):
                    v.wait_ge(logits_done, t + 1)
                    for a, w in ((0, NT - 1), (NT - 1, NT)):
                        p = TT if a == 0 else LAST
                        bg = mat("bg", 0, 2 * E)[0:p].unsqueeze(1).broadcast_to([p, w - a, 2 * E])
                        ins = v.tensor_tensor(lg[0:p, 2 * a:2 * w, :].rearrange("p (n i) e -> p n (i e)", i=2),
                                              ps_n[0:p, 1, 16 * a:16 * w].rearrange("p (n c) -> p n c", c=16),
                                              bg, ALU.add)
                    link(ins)

                def wide_best(i):
                    return best[:, i, :].unsqueeze(2).broadcast_to([128, R, E])

                def largest(i, out):
                    rank = mat("rank", 0, E).unsqueeze(1).broadcast_to([128, R, E])
                    link(v.tensor_reduce(best[:, i, :], lg[:, :, :], AX.X, ALU.max))
                    link(v.tensor_tensor(eq[:, :, :], lg[:, :, :], wide_best(i), ALU.is_equal))
                    link(v.tensor_tensor(eq[:, :, :], eq[:, :, :], rank, ALU.mult))
                    link(v.tensor_reduce(best[:, 3, :], eq[:, :, :], AX.X, ALU.max))
                    link(v.tensor_tensor(out, eq[:, :, :], wide_best(3), ALU.is_equal))

                def first_expert():
                    largest(0, one1[:, :, :])
                    link(v.scalar_tensor_tensor(out=lg[:, :, :], in0=one1[:, :, :], scalar=-3.0e38, in1=lg[:, :, :],
                                                op0=ALU.mult, op1=ALU.add))

                def second_expert():
                    largest(1, eq[:, :, :])
                    v.tensor_tensor(best[:, 1, :], best[:, 1, :], best[:, 0, :], ALU.subtract).then_inc(diff_done, 1)

                def weights(t):
                    v.wait_ge(exp_done, t + 1)
                    link(v.tensor_scalar(best[:, 3, :], best[:, 2, :], 1.0, None, ALU.add))
                    link(v.reciprocal(best[:, 0, :], best[:, 3, :]))
                    link(v.tensor_tensor(best[:, 1, :], best[:, 2, :], best[:, 0, :], ALU.mult))
                    v.tensor_tensor(one1[:, :, :], one1[:, :, :], wide_best(0), ALU.mult)
                    link(v.tensor_tensor(eq[:, :, :], eq[:, :, :], wide_best(1), ALU.mult))
                    v.tensor_tensor(lg[:, :, :], one1[:, :, :], eq[:, :, :], ALU.add).then_inc(w_done, 1)

                def weights_out(t, g):
                    at, n = tokens_of(g)
                    v.wait_ge(w_half, t * NG + g + 1)
                    v.tensor_tensor(wt[32:48, t, at:at + n], ps_n[0:16, g % 2, 0:n], wt[0:16, t, at:at + n],
                                    ALU.subtract).then_inc(w_out, 1)

                a = TOK_COLS["tvec"][0] + TVEC["br"]
                link(v.tensor_scalar(hb[:, :], tok[:, a:a + 2], 0.5, None, ALU.mult))
                v.memset(lg[:, :, :], 0.0)
                for t in range(PAIRS):
                    v.memset(xT[LAST:128, t, NT - 1, :], 0.0)
                for k in range(NCH):
                    residual_of_gates(0, k)
                    if k == 2:
                        v.wait_ge(cast, 1)
                        v.tensor_tensor(w1l[:, :], mat("w1", 0, E * HID), w1h[:, :], ALU.subtract).then_inc(w1l_done, 1)
                residual_of_gates(1, 0)
                means(0)
                centre(0)
                residual_of_gates(1, 1)
                variance(0)
                residual_of_gates(1, 2)
                normalize(0)
                for k in range(3, NCH):
                    residual_of_gates(1, k)
                biased(0)
                first_expert()
                second_expert()
                weights(0)
                v.wait_ge(wt_zero, 1)
                for g in range(NG):
                    weights_out(0, g)

                def aside(k, ep):
                    if (k, ep) == (0, 3):
                        means(1)
                    if (k, ep) == (1, 0):
                        centre(1)
                    if (k, ep) == (1, 2):
                        variance(1)
                    if (k, ep) == (2, 2):
                        normalize(1)
                    if (k, ep) == (3, 3):
                        biased(1)
                    if (k, ep) == (4, 0):
                        second_half(1)
                    if (k, ep) == (4, 1):
                        first_expert()
                    if (k, ep) == (4, 2):
                        second_expert()
                    if (k, ep) == (5, 0):
                        weights(1)
                    for at, groups in (((5, 2), (0, 1)), ((5, 3), (2, 3)), ((6, 1), (4, 5)), ((6, 2), (6,))):
                        if (k, ep) == at:
                            for g in groups:
                                weights_out(1, g)

                def body(b, k, u, before):
                    for ep in range(EP):
                        v.wait_ge(wide_done, u * EP + ep + 1)
                        if before or ep >= 1:
                            v.wait_ge(part_done, u * EP + ep)
                        v.tensor_copy(wide[:, :], ps_w[:, 0:CH]).then_inc(wide_out, 1)
                        v.wait_ge(o_done, u * EP + ep + 1)
                        v.wait_ge(wide_out, u * EP + ep + 1)
                        if ep == 1 and before:
                            residual(*before, u - 1)
                        if before:
                            v.wait_ge(sum_done, u * 3)
                        v.scalar_tensor_tensor(out=part[:, ep, :], in0=ps_o[:, ep % 2, 0:CH], scalar=mat("b2", ep, 1),
                                               in1=wide[:, :], op0=ALU.add,
                                               op1=ALU.mult).then_inc(part_done, 1)
                        if b == 0:
                            aside(k, ep)

                def residual(b, k, u):
                    i = b % 2
                    at = tres[64 * i:64 * i + 64, b // 2, columns_of(k)]
                    v.wait_ge(total_done, u + 1)
                    v.tensor_tensor(at, at, ps_t[64 * i:64 * i + 64, 0:CH], ALU.add).then_inc(res_done, 1)
                units(v, body)
                residual(B - 1, NCH - 1, UNITS - 1)

            @block.gpsimd
            def _(pool):
                def root(t):
                    pool.wait_ge(var_done, t + 1)
                    pool.tensor_tensor(rstd[:, :], var[:, :], mhalf[:, :], ALU.pow).then_inc(rstd_done, 1)

                pool.memset(wt[:, :, :], 0.0).then_inc(wt_zero, 1)
                pool.memset(mhalf[:, :], -0.5).then_inc(wt_zero, 1)
                pool.wait_ge(wt_zero, 2)
                root(0)
                pool.wait_ge(hi_done, 1)
                pool.tensor_tensor(lo[0], xhat[:, 0, :], hi[0], ALU.subtract).then_inc(split, 1)

                def body(b, k, u, before):
                    pool.wait_ge(part_done, u * EP + 2)
                    pool.tensor_tensor(total[:, 0, :], part[:, 0, :], part[:, 1, :], ALU.add).then_inc(sum_done, 1)
                    pool.wait_ge(part_done, u * EP + 3)
                    pool.wait_ge(sum_done, u * 3 + 1)
                    pool.tensor_tensor(total[:, 0, :], total[:, 0, :], part[:, 2, :], ALU.add).then_inc(sum_done, 1)
                    pool.wait_ge(part_done, u * EP + 4)
                    pool.wait_ge(sum_done, u * 3 + 2)
                    if before:
                        pool.wait_ge(total_done, u)
                    pool.tensor_tensor(total[:, 1, :], total[:, 0, :], part[:, 3, :], ALU.add).then_inc(sum_done, 1)
                    if b == 0 and k == 1:
                        root(1)
                units(pool, body)


def token_constants(w):
    f = np.float32
    tok = np.zeros((128, TOK_N), f)
    ffn = np.zeros((128, FFN_N), f)

    def put(name, a, i=0):
        cols, out = (FFN_COLS, ffn) if name in FFN_COLS else (TOK_COLS, tok)
        at = cols[name][0] + i * a.shape[1]
        out[:a.shape[0], at:at + a.shape[1]] = a

    put("ident", np.eye(128, dtype=f))
    drop = np.eye(C, dtype=f)
    drop[C - 1, :] = -1.0
    drop[C - 1, C - 1] = 0.0
    put("drop", np.tile(drop, (2, 2)))
    for j, n in enumerate(("z", "r", "f")):
        g = w[f"L1_attn_{n}_w"]
        m = np.zeros((2, C, 2, C), f)
        for i in range(2):
            m[i, :, i, :] = g[:, :C].T
        put("wx", m.reshape(128, 128), j)
        put("wa", np.ascontiguousarray(g[:, C:].T), j)
    den = np.zeros((128, 128), f)
    den[C - 1] = den[2 * C - 1] = 1.0
    put("den", den)
    put("fold", np.tile(np.eye(C, dtype=f), (2, 1)))
    put("w1", np.tile(w["L1_ffn_W1"].transpose(1, 0, 2).reshape(C, E * HID), (2, 1)))
    put("w2", w["L1_ffn_W2"].reshape(HT, 128, C).transpose(1, 0, 2).reshape(128, HT * C))
    put("b1", w["L1_ffn_b1"].reshape(HT, 128).T)
    put("b2", w["L1_ffn_b2"].reshape(EP, 2 * C).T)
    m = np.zeros((2, C, 2, E), f)
    for i in range(2):
        m[i, :, i, :] = w["L1_ffn_Wg"]
    put("wg", m.reshape(128, 2 * E))
    put("bg", np.tile(w["L1_ffn_bg"], (128, 2)))
    put("rank", np.tile(np.arange(E, 0, -1, dtype=f), (128, 2)))
    m = np.zeros((128, 2, EP, 2, C), f)
    for i in range(2):
        for e in range(E):
            for half in (0, 32):
                m[half + i * E + e, i, e // 2, e % 2, :] = 1.0
    put("spread", m.reshape(128, 2 * EP * 128))
    v = np.zeros((128, 12), f)
    v[:, TVEC["keep"]] = np.tile(np.arange(C) < C - 1, 2)
    v[:, TVEC["one"]] = np.tile(np.arange(C) == C - 1, 2)
    a = w["L1_attn_att_w"]
    v[:, TVEC["wa"]] = np.tile(a[:C], 2)
    v[:C, TVEC["wb"]] = a[C:2 * C]
    v[:, TVEC["wc"]] = np.tile(a[2 * C:], 2)
    for n in "zrf":
        v[:, TVEC["b" + n]] = np.tile(w[f"L1_attn_{n}_b"], 2)
    put("tvec", v)
    return tok, ffn


def build(nc, x, conv_c, tok_c, ffn_c, out):
    x3_dram = nc.dram_tensor("x3_dram", (B * NH, SP, STAGE), F32).ap()
    conv_out = nc.dram_tensor("conv_out", (B, C, PIX), F32).ap()
    t1_dram = nc.dram_tensor("t1_dram", (PAIRS, 128, PIX), F32).ap()
    with ExitStack() as whole:
        def sb(name, shape):
            return whole.enter_context(nc.sbuf_tensor(name, shape, F32))

        def sems(name, n):
            return [whole.enter_context(nc.semaphore(f"{name}{i}")) for i in range(n)]

        front = sb("front", [128, PIX + PADDED])
        win = sb("win", [128, 2, SP, WIN])
        tok = sb("tok", [128, TOK_N])
        wa = sb("wa", [128, 3 * C])
        x3_sent, = sems("x3_sent", 1)
        tres_in = sems("tres_in", PAIRS)
        in_t = sems("in_t", PAIRS)
        last_in = sems("last_in", PAIRS)
        win_flat = win[:, :, :, :].rearrange("p a s n -> p (a s n)")
        with nc.sbuf_tensor("cst", [128, CONV_N], F32) as cst:
            x3st = win_flat[:, 0:2 * STAGE].rearrange("p (s n) -> p s n", s=2)
            conv_prepare(nc, x, conv_c, tok_c, cst, tok, front[:, 0:PIX], front[:, PIX:PIX + PADDED], x3st, x3_dram,
                         x3_sent)
            conv_main(nc, x, cst, front, win, x3_dram, x3_sent, conv_out, tres_in, last_in)
        tres = tokens_of_front(front)
        xT = win_flat[:, 0:PAIRS * NT * 128].rearrange("p (t n c) -> p t n c", t=PAIRS, c=128)
        xhat = second_window(win)
        with nc.sbuf_tensor("attn", [128, B, PIX], F32) as attn:
            with nc.sbuf_tensor("vh", [128, B, PIX], F16) as vh, nc.sbuf_tensor("vl", [128, B, PIX], F16) as vl:
                xs = tres.rearrange("p t n -> p (t n)").bitcast(F16).rearrange("p (b n) -> p b n", b=B)
                attention(nc, tok, tres, xhat, xhat, xT, xs, vh, vl, wa, attn, tres_in, last_in, t1_dram, in_t)
            gates_and_experts(nc, tok, ffn_c, wa, xhat, xT, attn, tres, in_t, t1_dram, out)


def conv_constants(w):
    f = np.float32
    out = np.zeros((128, CONV_N), f)

    def put(name, a, i=0):
        at = CONV_COLS[name][0] + i * a.shape[1]
        out[:, at:at + a.shape[1]] = a

    for name, src in (("w1", w["L0_conv_w1c"]), ("w2", w["L0_conv_w2c"])):
        for t in range(PAIRS):
            m = np.zeros((2, C, B, CR), f)
            for i in range(2):
                m[i, :, 2 * t + i, :] = src.T
            put(name, m.reshape(128, 128), t)
    w3 = w["L0_conv_w3c"].reshape(NH, 2, 4, C)
    for s in range(2):
        for t in range(PAIRS):
            m = np.zeros((2, C, B, 4, NH), f)
            for i in range(2):
                m[i, :, 2 * t + i, :, :] = w3[:, s].transpose(2, 1, 0)
            put("w3", m.reshape(128, 128), s * PAIRS + t)
    m = np.zeros((B, CR, B, CR), f)
    for b in range(B):
        m[b, :, b, :] = w["L0_conv_cw1"]
    put("cw1", m.reshape(128, 128))
    m = np.zeros((B, CR, B, NH), f)
    for b in range(B):
        m[b, :, b, :] = w["L0_conv_cw2"].T
    put("cw2", m.reshape(128, 32))
    eye = np.eye(128, dtype=f)
    put("ident", eye)
    put("pair_mean", np.kron(np.eye(64, dtype=f), np.full((2, 2), 0.5, f)))
    put("tap_sum", np.tile(np.eye(32, dtype=f), (4, 1)))
    put("tap_sum_all", np.tile(np.eye(32, dtype=f), (4, 4)))
    b3 = w["L0_conv_b3c"].reshape(NH, 2, 4)
    rows = {n: np.tile(w["L0_conv_" + s], B) for n, s in
            (("b1", "b1c"), ("b2", "b2c"), ("g1", "bn1_g"), ("t1", "bn1_b"), ("m1", "bn1_m"), ("v1", "bn1_v"),
             ("g2", "bn2_g"), ("t2", "bn2_b"), ("m2", "bn2_m"), ("v2", "bn2_v"))}
    for s, n in enumerate(("b3a", "b3b")):
        rows[n] = np.broadcast_to(b3[:, s].T, (B, 4, NH)).reshape(128)
    rows["cw2b"] = np.tile(w["L0_conv_cw2_b"], 16)
    rows["mhalf"] = np.full(128, -0.5, f)
    v = np.zeros((128, 16), f)
    for n, a in rows.items():
        v[:, VEC[n]] = a
    put("vec", v)
    return out


def kernel(**inputs):
    import concourse.bacc as bacc
    from concourse.bass_utils import run_bass_kernel_spmd

    w = {n: np.asarray(a) for n, a in inputs.items()}
    tok_c, ffn_c = token_constants(w)
    arrays = {"x": np.ascontiguousarray(w["x"]), "conv_c": conv_constants(w), "tok_c": tok_c, "ffn_c": ffn_c}
    nc = bacc.Bacc("TRN2", target_bir_lowering=False, num_devices=1)
    args = [nc.dram_tensor(n, a.shape, F32, kind="ExternalInput").ap() for n, a in arrays.items()]
    out = nc.dram_tensor("out", (B, C, H, W), F32, kind="ExternalOutput").ap()
    build(nc, *args, out)
    r = run_bass_kernel_spmd(nc, [arrays], core_ids=[0])
    return r.results[0]["out"]
```
